# Optimizing a Trainium2 kernel written in Bass

```python
import numpy as np
import jax
import jax.numpy as jnp

def _softmax(x, axis=-1):
    return jax.nn.softmax(x, axis=axis)

def _gelu(x):
    return jax.nn.gelu(x, approximate=True)

def _silu(x):
    return jax.nn.silu(x)

def _sigmoid(x):
    return jax.nn.sigmoid(x)

def _layernorm(x, axis=-1, eps=1e-05):
    m = jnp.mean(x, axis=axis, keepdims=True)
    v = jnp.var(x, axis=axis, keepdims=True)
    return (x - m) / jnp.sqrt(v + eps)

def _scatter_add(tgt, idx, src, axis=0):
    return tgt.at[idx].add(src)

def _segment_sum(src, seg, n):
    return jax.ops.segment_sum(src, seg, n)
kernel_name = 'mk_audio_tower_d2_tok_audfeat512_r4_019aff'

def setup_inputs(seed: int=0):
    np.random.seed(seed)
    _w = jnp.asarray

    def _rec_inputs():
        import jax
        import jax.numpy as jnp
        _rk = jax.random.key(seed)
        x = -0.0003702 + 0.999946 * jax.random.normal(jax.random.fold_in(_rk, 1), (32, 500, 64), jnp.float32)
        return x
    x = _rec_inputs()

    def _L0_tok_setup():
        import jax, jax.numpy as jnp
        import numpy as np
        CONTEXT_LEN = 3
        SUBSAMPLING = 3
        key = jax.random.key(seed)
        k1, k2, k3 = jax.random.split(key, 3)
        B, T, D = (32, 500, 64)
        OUT = 128
        x = jax.random.normal(k1, (B, T, D), dtype=jnp.float32)
        weight = jax.random.normal(k2, (OUT, D * CONTEXT_LEN), dtype=jnp.float32)
        weight = weight * (1.0 / np.sqrt(D * CONTEXT_LEN * OUT).astype(np.float32))
        bias = jax.random.normal(k3, (1, OUT), dtype=jnp.float32)
        return {'x': x, 'weight': weight, 'bias': bias}
    _L0_tok_all = _L0_tok_setup()
    _L0_tok_in = {k: v for k, v in _L0_tok_all.items() if k in ('weight', 'bias')}
    del _L0_tok_all

    def _L0_attn_setup():
        import jax, jax.numpy as jnp
        import numpy as np
        from jax import lax
        D_IN, D_HIDDEN, D_OUT = (128, 256, 128)
        BATCH, SEQ = (8, 512)
        key = jax.random.key(seed)
        ks = jax.random.split(key, 9)

        def xavier(k, shape):
            std = (2.0 / (shape[0] + shape[1])) ** 0.5
            return std * jax.random.normal(k, shape, dtype=jnp.float32)
        uu = jax.random.uniform(ks[1], (D_HIDDEN,), dtype=jnp.float32, minval=0.001, maxval=1.0)
        nu_log = jnp.log(-0.5 * jnp.log(uu))
        theta_log = jax.random.uniform(ks[2], (D_HIDDEN,), dtype=jnp.float32, minval=0.0, maxval=6.28)
        diag_lambda_abs2 = jnp.exp(-2.0 * jnp.exp(nu_log))
        gamma_log = jnp.log(jnp.sqrt(1.0 - diag_lambda_abs2))
        return {'u': jax.random.normal(ks[0], (BATCH, SEQ, D_IN), dtype=jnp.float32), 'theta_log': theta_log, 'nu_log': nu_log, 'gamma_log': gamma_log, 'B_re': xavier(ks[3], (D_HIDDEN, D_IN)), 'B_im': xavier(ks[4], (D_HIDDEN, D_IN)), 'C_re': xavier(ks[5], (D_OUT, D_HIDDEN)), 'C_im': xavier(ks[6], (D_OUT, D_HIDDEN)), 'D': xavier(ks[7], (D_OUT, D_IN))}
    _L0_attn_all = _L0_attn_setup()
    _L0_attn_in = {k: v for k, v in _L0_attn_all.items() if k in ('theta_log', 'nu_log', 'gamma_log', 'B_re', 'B_im', 'C_re', 'C_im', 'D')}
    del _L0_attn_all

    def _L0_ffn_setup():
        import jax, jax.numpy as jnp
        import numpy as np
        TOP_K = 2
        key = jax.random.key(seed)
        k1, k2, k3, k4 = jax.random.split(key, 4)
        B, S, D, F, E = (4, 128, 128, 512, 16)
        hidden_states = jax.random.normal(k1, (B, S, D), dtype=jnp.float32)
        gate_weight = jax.random.normal(k2, (E, D), dtype=jnp.float32) * 0.02
        w1 = jax.random.normal(k3, (E, F, D), dtype=jnp.float32) * 0.02
        w2 = jax.random.normal(k4, (E, D, F), dtype=jnp.float32) * 0.02
        return {'hidden_states': hidden_states, 'gate_weight': gate_weight, 'w1': w1, 'w2': w2}
    _L0_ffn_all = _L0_ffn_setup()
    _L0_ffn_in = {k: v for k, v in _L0_ffn_all.items() if k in ('gate_weight', 'w1', 'w2')}
    del _L0_ffn_all

    def _L1_attn_setup():
        import jax, jax.numpy as jnp
        import numpy as np
        import math
        N_HEADS = 8
        FACTOR = 5
        key = jax.random.key(seed)
        ks = jax.random.split(key, 6)
        B, L, dm = (4, 2048, 128)
        x = jax.random.normal(ks[0], (B, L, dm), dtype=jnp.float32)
        Wq = jax.random.normal(ks[1], (dm, dm), dtype=jnp.float32) / math.sqrt(dm)
        Wk = jax.random.normal(ks[2], (dm, dm), dtype=jnp.float32) / math.sqrt(dm)
        Wv = jax.random.normal(ks[3], (dm, dm), dtype=jnp.float32) / math.sqrt(dm)
        Wo = jax.random.normal(ks[4], (dm, dm), dtype=jnp.float32) / math.sqrt(dm)
        sample_k = min(max(1, int(FACTOR * math.log(L + 1))), L)
        idx_sample = jax.random.randint(ks[5], (sample_k,), 0, L, dtype=jnp.int64)
        return {'x': x, 'Wq': Wq, 'Wk': Wk, 'Wv': Wv, 'Wo': Wo, 'idx_sample': idx_sample}
    _L1_attn_all = _L1_attn_setup()
    _L1_attn_in = {k: v for k, v in _L1_attn_all.items() if k in ('Wq', 'Wk', 'Wv', 'Wo', 'idx_sample')}
    del _L1_attn_all

    def _L1_ffn_setup():
        import jax, jax.numpy as jnp
        import numpy as np
        B, T, DIM = (2, 64, 128)
        E, H, K = (64, 256, 42)
        key = jax.random.key(seed)
        ks = jax.random.split(key, 7)
        s1 = 1.0 / np.sqrt(DIM).astype(np.float32)
        s2 = 1.0 / np.sqrt(H).astype(np.float32)
        return {'x': jax.random.normal(ks[0], (B, T, DIM), jnp.float32), 'w1': jax.random.uniform(ks[1], (E, DIM, H), jnp.float32, -s1, s1), 'b1': jax.random.uniform(ks[2], (E, H), jnp.float32, -s1, s1), 'w2': jax.random.uniform(ks[3], (E, H, DIM), jnp.float32, -s2, s2), 'b2': jax.random.uniform(ks[4], (E, DIM), jnp.float32, -s2, s2), 'router_w': jax.random.uniform(ks[5], (DIM, E), jnp.float32, -s1, s1), 'router_b': jax.random.uniform(ks[6], (E,), jnp.float32, -s1, s1)}
    _L1_ffn_all = _L1_ffn_setup()
    _L1_ffn_in = {k: v for k, v in _L1_ffn_all.items() if k in ('w1', 'b1', 'w2', 'b2', 'router_w', 'router_b')}
    del _L1_ffn_all
    return {'x': x, 'L0_tok_weight': _L0_tok_in['weight'], 'L0_tok_bias': _L0_tok_in['bias'], 'L0_attn_theta_log': _L0_attn_in['theta_log'], 'L0_attn_nu_log': _L0_attn_in['nu_log'], 'L0_attn_gamma_log': _L0_attn_in['gamma_log'], 'L0_attn_B_re': _L0_attn_in['B_re'], 'L0_attn_B_im': _L0_attn_in['B_im'], 'L0_attn_C_re': _L0_attn_in['C_re'], 'L0_attn_C_im': _L0_attn_in['C_im'], 'L0_attn_D': _L0_attn_in['D'], 'L0_ffn_gate_weight': _L0_ffn_in['gate_weight'], 'L0_ffn_w1': _L0_ffn_in['w1'], 'L0_ffn_w2': _L0_ffn_in['w2'], 'L1_attn_Wq': _L1_attn_in['Wq'], 'L1_attn_Wk': _L1_attn_in['Wk'], 'L1_attn_Wv': _L1_attn_in['Wv'], 'L1_attn_Wo': _L1_attn_in['Wo'], 'L1_attn_idx_sample': _L1_attn_in['idx_sample'], 'L1_ffn_w1': _L1_ffn_in['w1'], 'L1_ffn_b1': _L1_ffn_in['b1'], 'L1_ffn_w2': _L1_ffn_in['w2'], 'L1_ffn_b2': _L1_ffn_in['b2'], 'L1_ffn_router_w': _L1_ffn_in['router_w'], 'L1_ffn_router_b': _L1_ffn_in['router_b']}

def reference(x, L0_tok_weight, L0_tok_bias, L0_attn_theta_log, L0_attn_nu_log, L0_attn_gamma_log, L0_attn_B_re, L0_attn_B_im, L0_attn_C_re, L0_attn_C_im, L0_attn_D, L0_ffn_gate_weight, L0_ffn_w1, L0_ffn_w2, L1_attn_Wq, L1_attn_Wk, L1_attn_Wv, L1_attn_Wo, L1_attn_idx_sample, L1_ffn_w1, L1_ffn_b1, L1_ffn_w2, L1_ffn_b2, L1_ffn_router_w, L1_ffn_router_b):
    import jax
    import jax.numpy as jnp

    def _L0_tok_ref(x, weight, bias):
        import jax, jax.numpy as jnp
        import numpy as np
        CONTEXT_LEN = 3
        SUBSAMPLING = 3
        B, T, D = x.shape
        l = CONTEXT_LEN
        N = T - l + 1
        spliced = jnp.concatenate([x[:, i:i + N, :] for i in range(l)], axis=-1)
        spliced = spliced[:, ::SUBSAMPLING, :]
        return jnp.einsum('bnk,ok->bno', spliced, weight) + bias[0]

    def _L0_attn_ref(u, theta_log, nu_log, gamma_log, B_re, B_im, C_re, C_im, D):
        import jax, jax.numpy as jnp
        import numpy as np
        from jax import lax
        D_IN, D_HIDDEN, D_OUT = (128, 256, 128)
        BATCH, SEQ = (8, 512)
        lam = jnp.exp(-jnp.exp(nu_log) + 1j * jnp.exp(theta_log)).astype(jnp.complex64)
        B_norm = gamma_log[:, None].astype(jnp.complex64) * (B_re + 1j * B_im)
        C = (C_re + 1j * C_im).astype(jnp.complex64)
        Bu = jnp.einsum('btd,hd->bth', u.astype(jnp.complex64), B_norm)
        h0 = jnp.zeros((u.shape[0], lam.shape[0]), dtype=jnp.complex64)

        def step(h, bu_t):
            h = h * lam + bu_t
            return (h, h)
        _, hs = lax.scan(step, h0, jnp.swapaxes(Bu, 0, 1))
        y = jnp.real(jnp.einsum('tbh,oh->bto', hs, C)) + jnp.einsum('btd,od->bto', u, D)
        return y

    def _L0_ffn_ref(hidden_states, gate_weight, w1, w2):
        import jax, jax.numpy as jnp
        import numpy as np
        TOP_K = 2
        B, S, D = hidden_states.shape
        E = gate_weight.shape[0]
        x = hidden_states.reshape(-1, D)
        gate_logits = x @ gate_weight.T
        top_vals, top_idx = jax.lax.top_k(gate_logits, TOP_K)
        routing_w = jax.nn.softmax(top_vals, axis=-1)
        mask = jnp.any(top_idx[:, :, None] == jnp.arange(E)[None, None, :], axis=1)
        h = jax.nn.silu(jnp.einsum('td,efd->tef', x, w1))
        counts = jnp.sum(mask, axis=0)
        h_sum = jnp.einsum('tef,te->ef', h, mask.astype(h.dtype))
        h_mean = h_sum / jnp.maximum(counts, 1)[:, None].astype(h.dtype)
        y_mean = jnp.einsum('ef,edf->ed', h_mean, w2)
        y_mean = jnp.where((counts > 0)[:, None], y_mean, 0.0)
        out = jnp.einsum('tk,tkd->td', routing_w, y_mean[top_idx])
        return out.reshape(B, S, D)

    def _L1_attn_ref(x, Wq, Wk, Wv, Wo, idx_sample):
        import jax, jax.numpy as jnp
        import numpy as np
        import math
        N_HEADS = 8
        FACTOR = 5
        B, L, dm = x.shape
        H = N_HEADS
        D = dm // H
        scale = 1.0 / math.sqrt(D)
        u = min(max(1, int(FACTOR * math.log(L + 1))), L)
        Q = (x @ Wq).reshape(B, L, H, D).transpose(0, 2, 1, 3)
        K = (x @ Wk).reshape(B, L, H, D).transpose(0, 2, 1, 3)
        V = (x @ Wv).reshape(B, L, H, D).transpose(0, 2, 1, 3)
        K_sample = K[:, :, idx_sample, :]
        QK_sample = jnp.einsum('bhld,bhsd->bhls', Q, K_sample) * scale
        M = QK_sample.max(axis=-1) - QK_sample.mean(axis=-1)
        _, top_idx = jax.lax.top_k(M, u)
        Q_reduce = jnp.take_along_axis(Q, top_idx[..., None], axis=2)
        scores = jnp.einsum('bhud,bhld->bhul', Q_reduce, K) * scale
        attn = jax.nn.softmax(scores, axis=-1)
        V_top = jnp.einsum('bhul,bhld->bhud', attn, V)
        out = jnp.broadcast_to(V.mean(axis=2, keepdims=True), (B, H, L, D))
        b_idx = jnp.arange(B)[:, None, None]
        h_idx = jnp.arange(H)[None, :, None]
        out = out.at[b_idx, h_idx, top_idx].set(V_top)
        out = out.transpose(0, 2, 1, 3).reshape(B, L, H * D)
        return out @ Wo

    def _L1_ffn_ref(x, w1, b1, w2, b2, router_w, router_b):
        import jax, jax.numpy as jnp
        import numpy as np
        B, T, DIM = (2, 64, 128)
        E, H, K = (64, 256, 42)
        Bb, Tt, C = x.shape
        N = Bb * Tt
        logits = x @ router_w + router_b
        probs = jax.nn.softmax(logits, axis=-1)
        top_w, top_idx = jax.lax.top_k(probs, K)
        top_w = jax.nn.softmax(top_w, axis=-1)
        xt = x.reshape(N, C)
        top_w = top_w.reshape(N, K)
        top_idx = top_idx.reshape(N, K)
        comb = jnp.zeros((N, E), x.dtype).at[jnp.arange(N)[:, None], top_idx].set(top_w)
        h = jax.nn.gelu(jnp.einsum('td,edh->teh', xt, w1) + b1, approximate=False)
        y = jnp.einsum('teh,ehd->ted', h, w2) + b2
        out = jnp.einsum('ted,te->td', y, comb)
        return out.reshape(Bb, Tt, C)
    h = _L0_tok_ref(x, L0_tok_weight, L0_tok_bias)
    h = h + _L0_attn_ref(_layernorm(h, axis=-1), L0_attn_theta_log, L0_attn_nu_log, L0_attn_gamma_log, L0_attn_B_re, L0_attn_B_im, L0_attn_C_re, L0_attn_C_im, L0_attn_D)
    h = h + _L0_ffn_ref(_layernorm(h, axis=-1), L0_ffn_gate_weight, L0_ffn_w1, L0_ffn_w2)
    h = h + _L1_attn_ref(_layernorm(h, axis=-1), L1_attn_Wq, L1_attn_Wk, L1_attn_Wv, L1_attn_Wo, L1_attn_idx_sample)
    h = h + _L1_ffn_ref(_layernorm(h, axis=-1), L1_ffn_w1, L1_ffn_b1, L1_ffn_w2, L1_ffn_b2, L1_ffn_router_w, L1_ffn_router_b)
    return h

_drawn_inputs = setup_inputs


def setup_inputs(seed=0):
    import zlib

    import numpy as np

    out = dict(_drawn_inputs(seed))
    spreads = {}
    factors = {'L0_ffn_gate_weight': 3.259,
     'L0_ffn_w1': 3.362,
     'L0_ffn_w2': 3.096,
     'L1_attn_Wq': 8.0,
     'L1_attn_Wk': 8.0,
     'L1_ffn_w1': 4.425,
     'L1_ffn_b1': 8.0,
     'L1_ffn_w2': 3.885,
     'L1_ffn_b2': 24.733,
     'L1_ffn_router_w': 5.914,
     'L1_ffn_router_b': 8.0}
    for name, (base, spread) in spreads.items():
        noise = np.random.default_rng([zlib.crc32(name.encode()), seed]).standard_normal(out[name].shape)
        drawn = base * np.exp(spread * noise) if base else spread * noise
        out[name] = jnp.asarray(drawn.astype(out[name].dtype))
    for name, factor in factors.items():
        out[name] = (out[name] * factor).astype(out[name].dtype)
    return out
```

```python
from contextlib import ExitStack

import concourse.bass as bass
from concourse import mybir

ALU = mybir.AluOpType
ACT = mybir.ActivationFunctionType
X = mybir.AxisListType.X
F32 = mybir.dt.float32
F16 = mybir.dt.float16
BF16 = mybir.dt.bfloat16
I32 = mybir.dt.int32

B, L, D = 32, 166, 128
T = B * L
HALF = L // 2
NT = 2 * B
CH = 2 * L
NC = T // CH
BLK = 2 * CH
NB = T // BLK
KT = 96
HID = 256
E0, FF0 = 16, 512
FC = FF0 // 128
E1, FF1, TOP1 = 64, 256, 42
HC = FF1 // 128
NH, DH = 8, 16
NS = 38
NU = 25
HG = 4
GE, NG = 16, 4
SENT = -2.0e38
MARK = -3.0e38
CUT = -2.5e38
EPS = 1e-5
SCL = 256.0
ROUND = 12582912.0
LOG2E = 1.4426950408889634
LN2_HI, LN2_LO = 0.693359375, -2.12194440e-4
INV2PI = 0.15915494309189535
PI2_A, PI2_B = 6.28125, 0.0019350051879882812
PI2_C = 6.283185307179586 - 6.28125 - 0.0019350051879882812


def chunk(c):
    return bass.ts(c, CH)


class Kernel:
    pass


def constants_and_tokens(nc, k, x, w_tok, bias):
    with ExitStack() as ctx:
        xs = ctx.enter_context(nc.sbuf_tensor("xs", [KT, 2, T], F32))
        wt = ctx.enter_context(nc.sbuf_tensor("wt", [KT, 2, D], F32))
        bs = ctx.enter_context(nc.sbuf_tensor("bs", [128, 1], F32))
        parts = 4
        per = NC // parts
        w_in = k.semaphore("tok_w_in")
        x_in = [k.semaphore(f"tok_x_in{p}") for p in range(parts)]
        prod = k.semaphore("tok_product_ready")
        h_ready = k.semaphore("tok_bank_read")
        blank = k.semaphore("const_blank")
        made = k.semaphore("const_made")
        block = ctx.enter_context(nc.Block())

        @block.sync
        def _(sp):
            sp.dma_start(wt[:], w_tok).then_inc(w_in, 16)
            sp.dma_start(bs[:], bias).then_inc(w_in, 16)
            for p in range(parts):
                cols = slice(p * per * CH, (p + 1) * per * CH)
                sp.dma_start(xs[:, :, cols], x[:, :, cols]).then_inc(x_in[p], 16)

        @block.gpsimd
        def _(pool):
            g = nc.gpsimd
            g.memset(k.ident[:], 0.0).then_inc(blank, 1)
            g.memset(k.sel[:], 0.0).then_inc(blank, 1)
            g.memset(k.hm[:], 1.0).then_inc(blank, 1)
            g.memset(k.mean_w[:], 1.0 / D).then_inc(made, 1)
            g.memset(k.ones[:], 1.0).then_inc(made, 1)
            g.memset(k.rstd[:], 0.0).then_inc(made, 1)
            g.memset(k.eps[:], EPS).then_inc(made, 1)
            pool.wait_ge(blank, 3)
            g.affine_select(out=k.ident[:], in_=k.ident[:], compare_op=ALU.not_equal, fill=1.0, base=0,
                            pattern=[[-1, 128]], channel_multiplier=1).then_inc(made, 1)
            g.affine_select(out=k.sel[:], in_=k.sel[:], compare_op=ALU.not_equal, fill=1.0 / SCL, base=0,
                            pattern=[[-1, E1], [0, 128]], channel_multiplier=1).then_inc(blank, 1)
            g.affine_select(out=k.hm[:], in_=k.hm[:], compare_op=ALU.is_ge, fill=0.0, base=0,
                            pattern=[[-DH, NH]], channel_multiplier=1).then_inc(blank, 1)
            pool.wait_ge(blank, 5)
            g.affine_select(out=k.sel[:], in_=k.sel[:], compare_op=ALU.not_equal, fill=1.0 / SCL, base=-E1,
                            pattern=[[-1, E1], [0, 128]], channel_multiplier=1).then_inc(made, 1)
            g.affine_select(out=k.hm[:], in_=k.hm[:], compare_op=ALU.is_ge, fill=0.0, base=DH - 1,
                            pattern=[[DH, NH]], channel_multiplier=-1).then_inc(made, 1)

        @block.tensor
        def _(pe):
            pe.wait_ge(w_in, 32)
            for p in range(parts):
                pe.wait_ge(x_in[p], 16)
                for cc in range(per):
                    c = p * per + cc
                    if c >= 4:
                        pe.wait_ge(h_ready, c - 3)
                    for q in range(2):
                        last = nc.tensor.matmul(k.bank[:, c % 4, 0:CH], wt[:, q, :], xs[:, q, c * CH:(c + 1) * CH],
                                                start=(q == 0), stop=(q == 1))
                    last.then_inc(prod, 1)

        @block.vector
        def _(dve):
            dve.wait_ge(w_in, 32)
            for c in range(NC):
                dve.wait_ge(prod, c + 1)
                nc.vector.tensor_scalar(k.h[:, c * CH:(c + 1) * CH], k.bank[:, c % 4, 0:CH], bs[:], None,
                                        ALU.add).then_inc(h_ready, 1)


def norm_statistics(nc, k, name):
    with ExitStack() as ctx:
        sq = ctx.enter_context(nc.sbuf_tensor(f"{name}_sq", [128, 2, CH], F32))
        st = ctx.enter_context(nc.sbuf_tensor(f"{name}_st", [HALF, 4, NT], F32))
        mean = k.semaphore(f"{name}_mean")
        centred = k.semaphore(f"{name}_centred")
        squared = k.semaphore(f"{name}_squared")
        var = k.semaphore(f"{name}_variance")
        root = k.semaphore(f"{name}_root")
        step = k.semaphore(f"{name}_step")
        block = ctx.enter_context(nc.Block())
        v = k.bank[0:HALF, 2, 0:NT]

        @block.tensor
        def _(pe):
            pe.sem_inc(var, 2)
            with pe.Fori(0, NC // 2) as i:
                for j in range(2):
                    pe.wait_ge(centred, 2 * i + j + 1)
                    nc.tensor.matmul(k.bank[:, j, 0:CH], k.mean_w[:], k.h[:, chunk(2 * i + j)],
                                     start=True, stop=True).then_inc(mean, 1)
                for j in range(2):
                    pe.wait_ge(squared, 2 * i + j + 1)
                    for q in range(4):
                        last = nc.tensor.matmul(k.bank[0:HALF, 2, bass.ds((2 * i + j) * 4 + q, 1)],
                                                sq[:, j, q * HALF:(q + 1) * HALF], k.mean_w[:, 0:1],
                                                start=True, stop=True)
                    last.then_inc(var, 1)

        @block.vector
        def _(dve):
            dve.sem_inc(centred, 2)
            with dve.Fori(0, NC // 2) as i:
                for j in range(2):
                    dve.wait_ge(mean, 2 * i + j + 1)
                    nc.vector.tensor_tensor(k.hc[:, chunk(2 * i + j)], k.h[:, chunk(2 * i + j)], k.bank[:, j, 0:CH],
                                            ALU.subtract).then_inc(centred, 1)
            dve.wait_ge(var, NC + 2)
            nc.vector.tensor_scalar(st[:, 0], v, EPS, None, ALU.add).then_inc(step, 1)
            dve.wait_ge(root, 1)
            nc.vector.reciprocal(st[:, 2], st[:, 1]).then_inc(step, 1)
            dve.wait_ge(step, 2)
            nc.vector.tensor_tensor(st[:, 3], st[:, 2], st[:, 2], ALU.mult).then_inc(step, 1)
            dve.wait_ge(step, 3)
            nc.vector.tensor_tensor(st[:, 1], st[:, 3], st[:, 0], ALU.mult).then_inc(step, 1)
            dve.wait_ge(step, 4)
            nc.vector.tensor_scalar(st[:, 3], st[:, 1], -0.5, 1.5, ALU.mult, ALU.add).then_inc(step, 1)
            dve.wait_ge(step, 5)
            nc.vector.tensor_tensor(k.rstd[0:HALF, 0:NT], st[:, 2], st[:, 3], ALU.mult).then_inc(step, 1)

        @block.scalar
        def _(act):
            with act.Fori(0, NC // 2) as i:
                for j in range(2):
                    act.wait_ge(centred, 2 * i + j + 3)
                    act.wait_ge(var, 2 * i + j + 1)
                    nc.scalar.activation(sq[:, j, :], k.hc[:, chunk(2 * i + j)], ACT.Square).then_inc(squared, 1)
            act.wait_ge(step, 1)
            nc.scalar.activation(st[:, 1], st[:, 0], ACT.Sqrt).then_inc(root, 1)


def recurrence(nc, k):
    a = k.a
    with ExitStack() as ctx:
        def sb(name, shape, dt=F32):
            return ctx.enter_context(nc.sbuf_tensor(f"lru_{name}", shape, dt))

        def sem(name):
            return k.semaphore(f"lru_{name}")

        par = sb("par", [128, 3, 2])
        w_b = sb("w_b", [128, 2, HID])
        w_c = sb("w_c", [128, 3, 2, 128])
        w_cr = sb("w_cr", [128, 2, 2, 128])
        w_d = sb("w_d", [128, 128])
        ex = sb("ex", [128, 7, 4])
        bits = sb("bits", [128, 4], I32)
        mag = sb("mag", [128, 4])
        ph = sb("ph", [128, 5, 2])
        time = sb("time", [128, L])
        ang = sb("ang", [128, 4, 2, L])
        rot = sb("rot", [128, 4, 2, CH])
        decay = sb("decay", [128, 2, CH])
        diag = sb("diag", [HALF, 2, 4, HALF])
        ut = sb("ut", [128, 2, CH])
        va = sb("va", [128, 2, CH])
        vb = sb("vb", [128, 2, CH])
        gs = sb("gs", [128, 2, CH])
        xc = sb("xc", [128, 2, 2, CH])
        xsn = sb("xs", [128, 2, 2, CH])
        ysb = sb("ysb", [128, 2, CH])
        wst = sb("wst", [128, 2, 2048])

        small_in = sem("small_in")
        blank = sem("time_made")
        t = sem("table_step")
        conv = sem("exponent_bits")
        sine = sem("sine")
        tables = sem("tables_ready")
        negated = sem("c_negated")
        diag_ready = sem("diag_ready")
        spread = sem("rstd_spread")
        u_ready = sem("u_ready")
        bu = sem("bu_ready")
        turned = sem("bu_turned")
        joined = sem("turned_joined")
        scanned = sem("scanned")
        back = sem("turned_back")
        y_ready = sem("y_ready")
        y_copied = sem("y_copied")
        y_added = sem("y_added")
        w_in = [sem(f"w0_in{p}") for p in range(2)]
        w_hi = sem("w0_high")
        block = ctx.enter_context(nc.Block())
        w0 = k.weights[:, 0].rearrange("p a b -> p (a b)")
        w0_hi, w0_lo = w0[:, 0:E0 * FF0], w0[:, E0 * FF0:]
        k.w0_down = k.weights[:, 1].bitcast(F32).rearrange("p a b -> p (a b)")
        pieces = E0 * FF0 // 2048

        @block.sync
        def _(sp):
            for q, name in enumerate(("theta", "nu", "gamma")):
                sp.dma_start(par[:, q, :], a[name]).then_inc(small_in, 16)
            sp.dma_start(w_b[:, 0, :], a["b_re"]).then_inc(small_in, 16)
            sp.dma_start(w_b[:, 1, :], a["b_im"]).then_inc(small_in, 16)
            sp.dma_start(w_cr[:, 0], a["c_re"]).then_inc(small_in, 16)
            sp.dma_start(w_cr[:, 1], a["c_im"]).then_inc(small_in, 16)
            sp.dma_start(w_d[:], a["d"]).then_inc(small_in, 16)
            sp.dma_start(k.w0_down, a["w2"].rearrange("p e f d -> p (e f d)")).then_inc(k.w2_in, 16)
            for p in range(pieces):
                if p >= 2:
                    sp.wait_ge(k.w0_split, p - 1)
                sp.dma_start(wst[:, p % 2, :], a["w1"][:, p * 2048:(p + 1) * 2048]).then_inc(w_in[p % 2], 16)

        @block.gpsimd
        def _(pool):
            g = nc.gpsimd
            g.iota(time[:], [[1, L]], base=1, channel_multiplier=0,
                   allow_small_or_imprecise_dtypes=True).then_inc(blank, 1)
            with pool.Fori(0, NC // 2) as i:
                for j in range(2):
                    pool.wait_ge(spread, 2 * i + j + 1)
                    g.tensor_tensor(diag[:, j], k.ident[0:HALF, 0:HALF].unsqueeze(1).broadcast_to([HALF, 4, HALF]),
                                    k.rstd[0:HALF, bass.ts(2 * i + j, 4)].unsqueeze(2).broadcast_to([HALF, 4, HALF]),
                                    ALU.mult).then_inc(diag_ready, 1)
                for j in range(2):
                    pool.wait_ge(y_copied, 2 * i + j + 3)
                    g.tensor_tensor(k.h[:, chunk(2 * i + j)], k.h[:, chunk(2 * i + j)], ysb[:, j, :],
                                    ALU.add).then_inc(y_added, 1)
            for p in range(pieces):
                cols = slice(p * 2048, (p + 1) * 2048)
                pool.wait_ge(w_in[p % 2], 16 * (p // 2 + 1))
                g.tensor_copy(w0_hi[:, cols], wst[:, p % 2, :]).then_inc(w_hi, 1)
                pool.wait_ge(w_hi, p + 1)
                g.tensor_tensor(w0_lo[:, cols], wst[:, p % 2, :], w0_hi[:, cols], ALU.subtract).then_inc(k.w0_split, 1)

        @block.scalar
        def _(act):
            act.wait_ge(t, TABLE_ANGLE)
            nc.scalar.activation(ang[:, 1], ang[:, 0], ACT.Sin).then_inc(sine, 1)
            nc.scalar.activation(ang[:, 2], ang[:, 0], ACT.Sin, scale=0.5).then_inc(sine, 1)
            act.sem_inc(y_copied, 2)
            act.sem_inc(y_added, 2)
            with act.Fori(0, NC // 2) as i:
                for j in range(2):
                    act.wait_ge(y_ready, 2 * i + j + 1)
                    act.wait_ge(y_added, 2 * i + j + 1)
                    nc.scalar.activation(ysb[:, j, :], k.bank[:, 6 + j, 0:CH], ACT.Copy).then_inc(y_copied, 1)

        @block.vector
        def _(dve):
            n = [0]
            v = nc.vector

            def step(ins):
                n[0] += 1
                ins.then_inc(t, 1)
                dve.wait_ge(t, n[0])

            done = [0]

            def exponential(out, x, cols):
                w = [ex[:, m, 0:cols] for m in range(7)]
                step(v.tensor_scalar(w[6], x, -87.0, 87.0, ALU.max, ALU.min))
                step(v.tensor_scalar(w[0], w[6], LOG2E, ROUND, ALU.mult, ALU.add))
                step(v.tensor_scalar(w[1], w[0], ROUND, None, ALU.subtract))
                step(v.scalar_tensor_tensor(w[2], w[1], -LN2_HI, w[6], ALU.mult, ALU.add))
                step(v.scalar_tensor_tensor(w[3], w[1], -LN2_LO, w[2], ALU.mult, ALU.add))
                step(v.tensor_scalar(w[4], w[3], 1.0 / 5040, None, ALU.mult))
                src, dst = w[4], w[5]
                for c in (1.0 / 720, 1.0 / 120, 1.0 / 24, 1.0 / 6, 0.5, 1.0):
                    step(v.scalar_tensor_tensor(dst, src, c, w[3], ALU.add, ALU.mult))
                    src, dst = dst, src
                step(v.tensor_scalar(w[0], w[1], 127.0, 8388608.0, ALU.add, ALU.mult))
                step(v.tensor_copy(bits[:, 0:cols], w[0]))
                step(v.scalar_tensor_tensor(out, src, 1.0, bits[:, 0:cols].bitcast(F32), ALU.add, ALU.mult))

            def wrapped(x, work, turns):
                step(v.tensor_scalar(work, turns, INV2PI, ROUND, ALU.mult, ALU.add))
                step(v.tensor_scalar(work, work, ROUND, None, ALU.subtract))
                for part in (PI2_A, PI2_B, PI2_C):
                    step(v.scalar_tensor_tensor(x, work, -part, x, ALU.mult, ALU.add))

            dve.wait_ge(small_in, 128)
            for p in range(2):
                v.tensor_scalar(w_c[:, 1, p], w_cr[:, 1, p], -1.0, None, ALU.mult)
                v.tensor_scalar(w_c[:, 2, p], w_cr[:, 0, p], -1.0, None, ALU.mult)
                step(v.tensor_copy(w_c[:, 0, p], w_cr[:, 0, p]))
            both = par[:, 0:2, :].rearrange("p a b -> p (a b)")
            exponential(mag[:], both, 4)
            step(v.tensor_scalar(ph[:, 0], mag[:, 2:4], -1.0, None, ALU.mult))
            exponential(mag[:, 2:4], ph[:, 0], 2)
            step(v.tensor_copy(ph[:, 1], mag[:, 0:2]))
            wrapped(ph[:, 1], ph[:, 2], ph[:, 1])
            step(v.tensor_scalar(ph[:, 2], ph[:, 1], ROUND / 1024, None, ALU.add))
            step(v.tensor_scalar(ph[:, 3], ph[:, 2], ROUND / 1024, None, ALU.subtract))
            step(v.tensor_tensor(ph[:, 4], ph[:, 1], ph[:, 3], ALU.subtract))
            dve.wait_ge(blank, 1)
            for p in range(2):
                step(v.tensor_scalar(ang[:, 0, p], time[:], ph[:, 3, p:p + 1], None, ALU.mult))
                step(v.tensor_scalar(ang[:, 1, p], time[:], ph[:, 4, p:p + 1], None, ALU.mult))
                step(v.tensor_tensor(ang[:, 2, p], ang[:, 0, p], ang[:, 1, p], ALU.add))
                wrapped(ang[:, 0, p], ang[:, 3, p], ang[:, 2, p])
                step(v.tensor_tensor(ang[:, 0, p], ang[:, 0, p], ang[:, 1, p], ALU.add))
                step(v.tensor_scalar(ang[:, 0, p], ang[:, 0, p], 3.1415925, -3.1415925, ALU.min, ALU.max))
            assert n[0] == TABLE_ANGLE, n[0]
            dve.wait_ge(sine, 2)
            step(v.tensor_tensor(ang[:, 3], ang[:, 2], ang[:, 2], ALU.mult))
            step(v.tensor_scalar(ang[:, 2], ang[:, 3], -2.0, 1.0, ALU.mult, ALU.add))
            for p in range(2):
                for q in range(2):
                    cols = slice(q * L, (q + 1) * L)
                    v.tensor_copy(rot[:, 0, p, cols], ang[:, 2, p])
                    v.tensor_copy(rot[:, 1, p, cols], ang[:, 1, p])
                    v.tensor_scalar(rot[:, 2, p, cols], ang[:, 2, p], par[:, 2, p:p + 1], None, ALU.mult)
                    v.tensor_scalar(rot[:, 3, p, cols], ang[:, 1, p], par[:, 2, p:p + 1], None, ALU.mult)
                    step(v.tensor_scalar(decay[:, p, cols], time[:], 0.0, mag[:, 2 + p:3 + p], ALU.mult, ALU.add))
                    step(v.memset(decay[:, p, q * L:q * L + 1], 0.0))
            dve.sem_inc(spread, 2)
            dve.sem_inc(tables, 1)

            def tab(m, p):
                return rot[:, m, p].unsqueeze(1).broadcast_to([128, 2, CH])

            with dve.Fori(0, NC // 2) as i:
                for j in range(2):
                    dve.wait_ge(spread, 2 * i + j + 3)
                    v.tensor_tensor(ut[:, j, :], k.hc[:, chunk(2 * i + j)], k.bank[:, j, 0:CH],
                                    ALU.mult).then_inc(u_ready, 1)
                for j in range(2):
                    for p in range(2):
                        m = (2 * i + j) * 2 + p
                        pair = k.bank[:, 2 + 2 * p:4 + 2 * p, 0:CH]
                        dve.wait_ge(bu, m + 1)
                        v.tensor_tensor(va[:], pair, tab(2, p), ALU.mult).then_inc(turned, 1)
                        v.tensor_tensor(vb[:], pair, tab(3, p), ALU.mult).then_inc(turned, 1)
                        dve.wait_ge(turned, 2 * m + 2)
                        v.tensor_tensor(va[:, 0], va[:, 0], vb[:, 1], ALU.add).then_inc(joined, 1)
                        v.tensor_tensor(va[:, 1], va[:, 1], vb[:, 0], ALU.subtract).then_inc(joined, 1)
                        dve.wait_ge(joined, 2 * m + 2)
                        for q in range(2):
                            v.tensor_tensor_scan(gs[:, q], decay[:, p], va[:, q], 0.0, ALU.mult,
                                                 ALU.add).then_inc(scanned, 1)
                        dve.wait_ge(scanned, 2 * m + 2)
                        if p == 0:
                            dve.wait_ge(y_ready, 2 * i + j)
                        v.tensor_tensor(xc[:, p], gs[:], tab(0, p), ALU.mult).then_inc(back, 1)
                        v.tensor_tensor(xsn[:, p], gs[:], tab(1, p), ALU.mult).then_inc(back, 1)

        @block.tensor
        def _(pe):
            pe.wait_ge(small_in, 128)
            pe.wait_ge(tables, 1)
            with pe.Fori(0, NC // 2) as i:
                for j in range(2):
                    pe.wait_ge(diag_ready, 2 * i + j + 1)
                    nc.tensor.matmul(k.bank[:, j, 0:CH], k.ones[0:HALF, :], diag[:, j].rearrange("p a b -> p (a b)"),
                                     start=True, stop=True).then_inc(spread, 1)
                for j in range(2):
                    pe.wait_ge(u_ready, 2 * i + j + 1)
                    for p in range(2):
                        m = (2 * i + j) * 2 + p
                        for q in range(2):
                            last = nc.tensor.matmul(k.bank[:, 2 + 2 * p + q, 0:CH], w_b[:, q, p * 128:(p + 1) * 128],
                                                    ut[:, j, :], start=True, stop=True)
                        last.then_inc(bu, 1)
                    pe.wait_ge(y_copied, 2 * i + j + 1)
                    pe.wait_ge(back, 4 * (2 * i + j + 1))
                    parts = [(w_d[:], ut[:, j, :])]
                    for p in range(2):
                        parts += [(w_c[:, 0, p], xc[:, p, 0]), (w_c[:, 2, p], xsn[:, p, 1]),
                                  (w_c[:, 1, p], xsn[:, p, 0]), (w_c[:, 1, p], xc[:, p, 1])]
                    for q, (w, x) in enumerate(parts):
                        last = nc.tensor.matmul(k.bank[:, 6 + j, 0:CH], w, x, start=(q == 0), stop=(q == len(parts) - 1))
                    last.then_inc(y_ready, 1)


TABLE_ANGLE = 62


class Normed:

    def __init__(self, nc, k, ctx, name):
        self.nc, self.k = nc, k
        self.diag = ctx.enter_context(nc.sbuf_tensor(f"{name}_diag", [HALF, 2, 4, HALF], F32))
        self.ut = ctx.enter_context(nc.sbuf_tensor(f"{name}_ut", [128, 2, CH], F32))
        self.diag_ready = k.semaphore(f"{name}_diag_ready")
        self.spread = k.semaphore(f"{name}_rstd_spread")
        self.u_ready = k.semaphore(f"{name}_u_ready")

    def pool_diagonal(self, pool, c, j):
        k = self.k
        pool.wait_ge(self.spread, c + 1)
        self.nc.gpsimd.tensor_tensor(
            self.diag[:, j], k.ident[0:HALF, 0:HALF].unsqueeze(1).broadcast_to([HALF, 4, HALF]),
            k.rstd[0:HALF, bass.ts(c, 4)].unsqueeze(2).broadcast_to([HALF, 4, HALF]), ALU.mult).then_inc(self.diag_ready, 1)

    def pe_spread(self, pe, c, j):
        pe.wait_ge(self.diag_ready, c + 1)
        self.nc.tensor.matmul(self.k.bank[:, j, 0:CH], self.k.ones[0:HALF, :],
                              self.diag[:, j].rearrange("p a b -> p (a b)"), start=True, stop=True).then_inc(self.spread, 1)

    def dve_start(self, dve):
        dve.sem_inc(self.spread, 2)

    def dve_apply(self, dve, c, j):
        dve.wait_ge(self.spread, c + 3)
        self.nc.vector.tensor_tensor(self.ut[:, j, :], self.k.hc[:, chunk(c)], self.k.bank[:, j, 0:CH],
                                     ALU.mult).then_inc(self.u_ready, 1)


def first_mixture(nc, k):
    a = k.a
    with ExitStack() as ctx:
        def sb(name, shape, dt=F32):
            return ctx.enter_context(nc.sbuf_tensor(f"m0_{name}", shape, dt))

        def sem(name):
            return k.semaphore(f"m0_{name}")

        norm = Normed(nc, k, ctx, "m0")
        ut = norm.ut
        gate = sb("gate", [128, E0])
        u_hi = sb("u_hi", [128, T], BF16)
        u_lo = sb("u_lo", [128, T], BF16)
        rows = sb("rows", [HALF, NT, E0 + 8])
        top = sb("top", [HALF, NT, 8])
        left = sb("left", [HALF, NT, E0 + 8])
        gap = sb("gap", [HALF, NT, E0])
        e = sb("e", [HALF, NT, E0])
        tot = sb("tot", [HALF, 2, NT])
        cat = sb("cat", [HALF, NT, 48])
        rt = k.hc[0:48, :]
        mask = sb("mask", [128, T], F16)
        xm_hi = sb("xm_hi", [128, 2, BLK], BF16)
        xm_lo = sb("xm_lo", [128, 2, BLK], BF16)
        junk = sb("junk", [128, 2, BLK], BF16)
        part = sb("part", [128, E0 * FC * NB])
        hsum = sb("hsum", [128, E0 * FC])
        msum = sb("msum", [HALF, E0])
        cnt = sb("cnt", [128, 2, E0])
        ymt = sb("ymt", [128, E0])
        ym = sb("ym", [E0, 128])

        gate_in = sem("gate_in")
        u_high = sem("u_high")
        u_low = sem("u_low")
        logits = sem("logits")
        copied = sem("logits_copied")
        s = sem("routing_step")
        expd = sem("exp_ready")
        blank = sem("mask_blank")
        turned = sem("rows_turned")
        rt_ready = sem("rt_ready")
        mask_ready = sem("mask_ready")
        spread = sem("mask_spread")
        masked = sem("u_masked")
        up = sem("up_ready")
        summed = sem("silu_summed")
        fin = sem("mean_step")
        fin_pe = sem("mean_product")
        out = sem("out_ready")
        added = sem("out_added")
        block = ctx.enter_context(nc.Block())
        w0 = k.weights[:, 0].rearrange("p a b -> p (a b)")
        w0_hi, w0_lo = w0[:, 0:E0 * FF0], w0[:, E0 * FF0:]
        w2 = k.w0_down.rearrange("p (e f d) -> p e f d", e=E0, f=FC)
        n_route = 12

        @block.sync
        def _(sp):
            sp.dma_start(gate[:], a["gate"]).then_inc(gate_in, 16)

        @block.gpsimd
        def _(pool):
            nc.gpsimd.memset(cat[:], 0.0).then_inc(blank, 1)
            nc.gpsimd.memset(mask[:], 0.0).then_inc(blank, 1)
            with pool.Fori(0, NC // 2) as i:
                for j in range(2):
                    norm.pool_diagonal(pool, 2 * i + j, j)

        @block.scalar
        def _(act):
            with act.Fori(0, NC // 2) as i:
                for j in range(2):
                    act.wait_ge(norm.u_ready, 2 * i + j + 1)
                    nc.scalar.activation(u_hi[:, chunk(2 * i + j)], ut[:, j, :], ACT.Copy).then_inc(u_high, 1)
            act.wait_ge(s, 2)
            nc.scalar.activation(e[:], gap[:], ACT.Exp).then_inc(expd, 1)
            act.wait_ge(blank, 2)
            with act.Fori(0, NC // 4) as i:
                for j in range(4):
                    act.wait_ge(turned, 4 * i + j + 1)
                    nc.scalar.activation(rt[:, chunk(4 * i + j)], k.bank[0:48, j, 0:CH], ACT.Copy).then_inc(rt_ready, 1)
            act.wait_ge(rt_ready, NC)
            nc.scalar.activation(mask[0:E0, :], rt[32:48, :], ACT.Copy).then_inc(mask_ready, 1)
            act.sem_inc(summed, 2)
            with act.Fori(0, E0) as x:
                for i in range(NB):
                    for f in range(FC):
                        act.wait_ge(up, (x * NB + i) * FC + f + 1)
                        pair = slice(2 + 2 * (f % 2), 4 + 2 * (f % 2))
                        nc.scalar.activation(junk[:, f % 2].rearrange("p (a b) -> p a b", a=2),
                                             k.bank[:, pair, 0:CH], ACT.Silu,
                                             accum_out=part[:, bass.ds(x * (NB * FC) + (f * NB + i), 1)]).then_inc(summed, 1)

        @block.vector
        def _(dve):
            v = nc.vector
            norm.dve_start(dve)
            v.memset(rows[:], SENT).then_inc(copied, 1)
            dve.wait_ge(copied, 1)
            with dve.Fori(0, NC // 2) as i:
                dve.wait_ge(u_low, 2 * i)
                for j in range(2):
                    norm.dve_apply(dve, 2 * i + j, j)
                for j in range(2):
                    dve.wait_ge(u_high, 2 * i + j + 1)
                    v.tensor_tensor(u_lo[:, chunk(2 * i + j)], ut[:, j, :], u_hi[:, chunk(2 * i + j)],
                                    ALU.subtract).then_inc(u_low, 1)
                    dve.wait_ge(logits, 2 * i + j + 1)
                    v.tensor_copy(rows[:, bass.ts(2 * i + j, 4), 0:E0],
                                  k.bank[0:HALF, 4 + j, 0:4 * E0].rearrange("p (n e) -> p n e", n=4)).then_inc(copied, 1)
            dve.wait_ge(copied, NC + 1)
            for n in range(NT):
                last = v.max(top[:, n, :], rows[:, n, :])
            last.then_inc(s, 1)
            dve.wait_ge(s, 1)
            v.tensor_tensor(gap[:], rows[:, :, 0:E0], top[:, :, 0:1].broadcast_to([HALF, NT, E0]), ALU.subtract).then_inc(s, 1)
            dve.wait_ge(s, 2)
            v.memset(top[:, :, 2:8], SENT).then_inc(s, 1)
            dve.wait_ge(s, 3)
            for n in range(NT):
                last = v.match_replace(left[:, n, :], top[:, n, :], rows[:, n, :], MARK)
            last.then_inc(s, 1)
            dve.wait_ge(s, 4)
            dve.wait_ge(blank, 1)
            v.tensor_scalar(cat[:, :, 32:48], left[:, :, 0:E0], CUT, SCL, ALU.is_le, ALU.mult).then_inc(s, 1)
            dve.wait_ge(s, 5)
            dve.wait_ge(expd, 1)
            v.scalar_tensor_tensor(gap[:], cat[:, :, 32:48], 1.0 / SCL, e[:], ALU.mult, ALU.mult).then_inc(s, 1)
            v.tensor_reduce(msum[:], cat[:, :, 32:48].rearrange("p n e -> p e n"), X, ALU.add).then_inc(s, 1)
            dve.wait_ge(s, 6)
            v.tensor_reduce(tot[:, 0], gap[:], X, ALU.add).then_inc(s, 1)
            dve.wait_ge(s, 8)
            v.reciprocal(tot[:, 1], tot[:, 0]).then_inc(s, 1)
            dve.wait_ge(s, 9)
            v.tensor_tensor(cat[:, :, 0:E0], gap[:], tot[:, 1].unsqueeze(2).broadcast_to([HALF, NT, E0]),
                            ALU.mult).then_inc(s, 1)
            dve.wait_ge(u_low, NC)
            with dve.Fori(0, E0) as x:
                for i in range(NB):
                    dve.wait_ge(spread, x * NB + i + 1)
                    m = k.bank[:, 6 * (i % 2):6 * (i % 2) + 2, 0:CH]
                    for dst, src in ((xm_hi, u_hi), (xm_lo, u_lo)):
                        v.tensor_tensor(dst[:, i % 2].rearrange("p (a b) -> p a b", a=2),
                                        src[:, i * BLK:(i + 1) * BLK].rearrange("p (a b) -> p a b", a=2), m,
                                        ALU.mult).then_inc(masked, 1)
            dve.wait_ge(summed, E0 * NB * FC + 2)
            v.tensor_reduce(hsum[:], part[:].rearrange("p (a b) -> p a b", b=NB), X, ALU.add).then_inc(fin, 1)
            dve.wait_ge(fin_pe, 1)
            v.tensor_scalar(cnt[:, 0], k.bank[:, 0, 0:E0], 1.0 / SCL, 1.0, ALU.mult, ALU.max).then_inc(fin, 1)
            dve.wait_ge(fin, 2)
            v.reciprocal(cnt[:, 1], cnt[:, 0]).then_inc(fin, 1)
            dve.wait_ge(fin, 3)
            dve.wait_ge(fin_pe, 2)
            v.tensor_tensor(ymt[:], k.bank[:, 1, 0:E0], cnt[:, 1], ALU.mult).then_inc(fin, 1)
            dve.wait_ge(fin_pe, 3)
            v.tensor_copy(ym[:], k.bank[0:E0, 2, 0:128]).then_inc(fin, 1)
            dve.sem_inc(added, 4)
            with dve.Fori(0, NC // 4) as i:
                for j in range(4):
                    dve.wait_ge(out, 4 * i + j + 1)
                    v.tensor_tensor(k.h[:, chunk(4 * i + j)], k.h[:, chunk(4 * i + j)], k.bank[:, 4 + j, 0:CH],
                                    ALU.add).then_inc(added, 1)

        @block.tensor
        def _(pe):
            t = nc.tensor
            pe.wait_ge(gate_in, 16)
            with pe.Fori(0, NC // 2) as i:
                for j in range(2):
                    norm.pe_spread(pe, 2 * i + j, j)
                for j in range(2):
                    pe.wait_ge(norm.u_ready, 2 * i + j + 1)
                    pe.wait_ge(copied, 2 * i + j)
                    for q in range(4):
                        last = t.matmul(k.bank[0:HALF, 4 + j, q * E0:(q + 1) * E0], ut[:, j, q * HALF:(q + 1) * HALF],
                                        gate[:], start=True, stop=True)
                    last.then_inc(logits, 1)
            pe.wait_ge(s, 10)
            for c in range(NC):
                if c >= 4:
                    pe.wait_ge(rt_ready, c - 3)
                for q in range(4):
                    last = t.transpose(k.bank[0:48, c % 4, q * HALF:(q + 1) * HALF], cat[:, 4 * c + q, :],
                                       k.ident[0:HALF, 0:HALF])
                last.then_inc(turned, 1)
            pe.wait_ge(mask_ready, 1)
            pe.wait_ge(k.w0_split, E0 * FF0 // 2048)

            def pe_mask(x, i):
                for q in range(2):
                    last = t.matmul(k.bank[:, 6 * (i % 2) + q, 0:CH], k.sel[:, bass.ds(x, 1), :].rearrange("p a b -> p (a b)"),
                                    mask[:, i * BLK + q * CH:i * BLK + (q + 1) * CH], start=True, stop=True)
                last.then_inc(spread, 1)

            pe_mask(0, 0)
            with pe.Fori(0, E0) as x:
                for i in range(NB):
                    pe_mask(x + (i + 1) // NB, (i + 1) % NB)
                    pe.wait_ge(masked, 2 * (x * NB + i) + 2)
                    for f in range(FC):
                        hi = w0_hi[:, bass.ds(x * FF0 + f * 128, 128)]
                        lo = w0_lo[:, bass.ds(x * FF0 + f * 128, 128)]
                        pe.wait_ge(summed, (x * NB + i) * FC + f + 1)
                        for m, (w, u) in enumerate(((hi, xm_hi), (hi, xm_lo), (lo, xm_hi))):
                            for q in range(2):
                                last = t.matmul(k.bank[:, 2 + 2 * (f % 2) + q, 0:CH], w, u[:, i % 2, q * CH:(q + 1) * CH],
                                                start=(m == 0), stop=(m == 2))
                        last.then_inc(up, 1)
            pe.wait_ge(masked, 2 * E0 * NB)
            pe.wait_ge(s, 7)
            t.matmul(k.bank[:, 0, 0:E0], k.ones[0:HALF, :], msum[:], start=True, stop=True).then_inc(fin_pe, 1)
            pe.wait_ge(fin, 1)
            pe.wait_ge(k.w2_in, 16)
            for x in range(E0):
                for f in range(FC):
                    last = t.matmul(k.bank[:, 1, x:x + 1], w2[:, x, f, :], hsum[:, x * FC + f:x * FC + f + 1],
                                    start=(f == 0), stop=(f == FC - 1))
            last.then_inc(fin_pe, 1)
            pe.wait_ge(fin, 4)
            t.transpose(k.bank[0:E0, 2, 0:128], ymt[:], k.ident[:]).then_inc(fin_pe, 1)
            pe.wait_ge(fin, 5)
            with pe.Fori(0, NC // 4) as i:
                for j in range(4):
                    pe.wait_ge(added, 4 * i + j + 1)
                    t.matmul(k.bank[:, 4 + j, 0:CH], ym[:], rt[0:E0, chunk(4 * i + j)], start=True, stop=True).then_inc(out, 1)


def sparse_attention(nc, k):
    a = k.a
    with ExitStack() as ctx:
        def sb(name, shape, dt=F32):
            return ctx.enter_context(nc.sbuf_tensor(f"at_{name}", shape, dt))

        def sem(name):
            return k.semaphore(f"at_{name}")

        NR = NH * NU
        GR = HG * NU
        q_all = k.weights[0:HALF, 1].bitcast(F32).rearrange("p a b -> p (a b)").rearrange("p (n d) -> p n d", n=NT)
        kt_all = k.hc
        v_all = sb("v_all", [HALF, NT, 128])
        wst = sb("wst", [128, 2, 1024])
        w_o = sb("w_o", [128, 128])
        hmu = sb("hmu", [128, NH])
        rank_t = sb("rank_t", [HALF, 2, 2 * 128])
        rank = sb("rank", [128, 2, L], BF16)
        expand = sb("expand", [128, 16, 2, GR], BF16)

        small_in = sem("small_in")
        made = sem("made")
        step = sem("choose_step")
        step_pe = sem("choose_product")
        w_in = [sem(f"w_in{p}") for p in range(2)]
        w_hi = sem("w_high")

        with ExitStack() as first:
            def sb1(name, shape, dt=F32):
                return first.enter_context(nc.sbuf_tensor(f"at_{name}", shape, dt))

            norm = Normed(nc, k, first, "at")
            ut = norm.ut
            w_qk = sb1("w_qk", [128, 3, 128])
            qt = sb1("qt", [128, 2, CH])
            kx = sb1("kx", [HALF, 2, 4, 128])
            idx = sb1("idx", [HALF, NS], I32)
            pos = sb1("pos", [HALF, 3, NS])
            line = sb1("line", [HALF, 2])
            pick = sb1("pick", [HALF, 2, NS + 1])
            ksm = sb1("ksm", [128, 2, NH, NS + 1])
            peak = sb1("peak", [HALF, 2, NH])
            m_all = sb1("m_all", [HALF, 2, 2 * 128])
            cand = sb1("cand", [128, 2, L + 8])
            best = sb1("best", [128, 2, 8])
            chosen = sb1("chosen", [128, 2, L])
            count = sb1("count", [128, 2, L])
            qt_ready = sem("qt_ready")
            q_copied = sem("q_copied")
            kt_ready = sem("kt_ready")
            kt_copied = sem("kt_copied")
            tok_ready = sem("token_major_ready")
            kx_copied = sem("k_copied")
            ks_ready = sem("samples_ready")
            ks_masked = sem("samples_masked")
            sc_ready = sem("sampled_scores_ready")
            peaked = sem("peak_taken")
            measured = sem("measure_taken")
            block = first.enter_context(nc.Block())

            @block.sync
            def _(sp):
                for q, name in enumerate(("wq", "wv", "wk")):
                    sp.dma_start(w_qk[:, q], a[name]).then_inc(small_in, 16)
                sp.dma_start(w_o[:], a["wo"]).then_inc(small_in, 16)
                sp.dma_start(idx[:], a["idx"].partition_broadcast(HALF)).then_inc(small_in, 16)

            @block.gpsimd
            def _(pool):
                g = nc.gpsimd
                g.iota(line[:], [[HALF, 2]], base=0, channel_multiplier=1,
                       allow_small_or_imprecise_dtypes=True).then_inc(made, 1)
                g.memset(expand[:], 0.0).then_inc(made, 1)
                with pool.Fori(0, NC // 2) as i:
                    for j in range(2):
                        norm.pool_diagonal(pool, 2 * i + j, j)
                pool.wait_ge(made, 2)
                g.affine_select(out=expand[:].rearrange("p b g (h u) -> p (b g h) u", h=HG),
                                in_=expand[:].rearrange("p b g (h u) -> p (b g h) u", h=HG),
                                compare_op=ALU.not_equal, fill=1.0, base=0,
                                pattern=[[-1, 128], [0, NU]], channel_multiplier=1).then_inc(made, 1)

            @block.scalar
            def _(act):
                act.sem_inc(q_copied, 2)
                with act.Fori(0, NC // 2) as i:
                    for j in range(2):
                        c = 2 * i + j
                        act.wait_ge(qt_ready, c + 1)
                        act.wait_ge(sc_ready, 4 * c - 4 * j)
                        nc.scalar.activation(qt[:, j], k.bank[:, 2, 0:CH], ACT.Copy).then_inc(q_copied, 1)
                        act.wait_ge(kt_ready, c + 1)
                        nc.scalar.activation(kt_all[:, chunk(c)], k.bank[:, 3, 0:CH], ACT.Copy).then_inc(kt_copied, 1)
                        for q in range(4):
                            act.wait_ge(tok_ready, 4 * c + q + 1)
                            nc.scalar.activation(q_all[:, bass.ds(4 * c + q, 1), :].rearrange("p a b -> p (a b)"),
                                                 k.bank[0:HALF, 4 + q % 2, 0:128], ACT.Copy)
                            nc.scalar.activation(v_all[:, bass.ds(4 * c + q, 1), :].rearrange("p a b -> p (a b)"),
                                                 k.bank[0:HALF, 4 + q % 2, 128:256], ACT.Copy)
                            nc.scalar.activation(kx[:, j, q], k.bank[0:HALF, 4 + q % 2, 256:384], ACT.Copy).then_inc(kx_copied, 1)

            @block.vector
            def _(dve):
                v = nc.vector
                n = [0]

                def link(ins):
                    n[0] += 1
                    ins.then_inc(step, 1)
                    dve.wait_ge(step, n[0])

                norm.dve_start(dve)
                dve.wait_ge(small_in, 80)
                dve.wait_ge(made, 1)
                link(v.tensor_copy(pos[:, 0], idx[:]))
                link(v.tensor_scalar(pos[:, 1], pos[:, 0], 0.0, float(L), ALU.is_lt, ALU.mult))
                link(v.tensor_tensor(pos[:, 2], pos[:, 0], pos[:, 1], ALU.add))
                link(v.tensor_scalar(pos[:, 0], pos[:, 2], 0.0, float(L - 1), ALU.max, ALU.min))
                for q in range(2):
                    link(v.tensor_scalar(pick[:, q, 0:NS], pos[:, 0], line[:, q:q + 1], None, ALU.is_equal))
                link(v.tensor_reduce(pos[:, 1, 0:2], pick[:, :, 0:NS], X, ALU.add))
                link(v.tensor_scalar(pick[:, :, NS:NS + 1], pos[:, 1, 0:2].unsqueeze(2), 1.0 / NS, None, ALU.mult))
                link(v.tensor_scalar(hmu[:], k.hm[:], DH ** -0.5, None, ALU.mult))
                link(v.memset(cand[:], SENT))
                with dve.Fori(0, NC // 2) as i:
                    dve.wait_ge(kx_copied, 8 * i)
                    for j in range(2):
                        c = 2 * i + j
                        norm.dve_apply(dve, c, j)
                    for j in range(2):
                        c = 2 * i + j
                        for b in range(2):
                            dve.wait_ge(ks_ready, 2 * c + b + 1)
                            v.tensor_tensor(ksm[:, b], k.bank[:, 6, b * 64:b * 64 + NS + 1].unsqueeze(1).broadcast_to([128, NH, NS + 1]),
                                            k.hm[:].unsqueeze(2).broadcast_to([128, NH, NS + 1]), ALU.mult).then_inc(ks_masked, 1)
                        for q in range(4):
                            m = 4 * c + q
                            sc = k.bank[0:HALF, 7, 0:NH * (NS + 1)].rearrange("p (h s) -> p h s", h=NH)
                            dve.wait_ge(sc_ready, m + 1)
                            v.tensor_reduce(peak[:, q % 2], sc[:, :, 0:NS], X, ALU.max).then_inc(peaked, 1)
                            dve.wait_ge(peaked, m + 1)
                            v.tensor_tensor(m_all[:, q % 2, bass.ds((2 * c + q // 2) * NH, NH)], peak[:, q % 2],
                                            sc[:, :, NS:NS + 1].rearrange("p a b -> p (a b)"), ALU.subtract).then_inc(measured, 1)
                dve.wait_ge(step_pe, 1)
                for gq in range(4):
                    last = v.tensor_copy(cand[:, gq // 2, (gq % 2) * HALF:(gq % 2) * HALF + HALF],
                                         k.bank[:, 0, gq * HALF:(gq + 1) * HALF])
                link(last)
                for r in range(NU // 8):
                    for g in range(2):
                        last = v.max(best[:, g], cand[:, g])
                    link(last)
                    for g in range(2):
                        last = v.match_replace(cand[:, g], best[:, g], cand[:, g], MARK)
                    link(last)
                for g in range(2):
                    last = v.max(best[:, g], cand[:, g])
                link(last)
                link(v.memset(best[:, :, NU % 8:8], SENT))
                for g in range(2):
                    last = v.match_replace(cand[:, g], best[:, g], cand[:, g], MARK)
                link(last)
                link(v.tensor_scalar(chosen[:], cand[:, :, 0:L], CUT, None, ALU.is_le))
                for g in range(2):
                    last = v.tensor_tensor_scan(count[:, g], k.ones[:, 0:1].broadcast_to([128, L]), chosen[:, g], 0.0, ALU.mult, ALU.add)
                link(last)
                link(v.tensor_tensor(count[:], count[:], chosen[:], ALU.mult))
                v.tensor_copy(rank[:], count[:]).then_inc(step, 1)
                dve.wait_ge(step_pe, 2)
                for gq in range(4):
                    g, half = gq // 2, gq % 2
                    v.tensor_copy(rank_t[:, half, g * 128:(g + 1) * 128], k.bank[0:HALF, 1, gq * 128:(gq + 1) * 128])
                k.at_steps = n[0]

            @block.tensor
            def _(pe):
                t = nc.tensor
                pe.wait_ge(small_in, 80)
                pe.wait_ge(step, 10)
                with pe.Fori(0, NC // 2) as i:
                    for j in range(2):
                        norm.pe_spread(pe, 2 * i + j, j)
                    for j in range(2):
                        c = 2 * i + j
                        pe.wait_ge(norm.u_ready, c + 1)
                        pe.wait_ge(q_copied, c + 2)
                        t.matmul(k.bank[:, 2, 0:CH], w_qk[:, 0], ut[:, j], start=True, stop=True).then_inc(qt_ready, 1)
                        pe.wait_ge(kt_copied, c)
                        t.matmul(k.bank[:, 3, 0:CH], w_qk[:, 2], ut[:, j], start=True, stop=True).then_inc(kt_ready, 1)
                        for q in range(4):
                            pe.wait_ge(kx_copied, 4 * c + (q - 1 if q >= 2 else 0))
                            t.matmul(k.bank[0:HALF, 4 + q % 2, 0:384], ut[:, j, q * HALF:(q + 1) * HALF],
                                     w_qk[:].rearrange("p a b -> p (a b)"), start=True, stop=True).then_inc(tok_ready, 1)
                        for b in range(2):
                            pe.wait_ge(kx_copied, 4 * c + 2 * b + 2)
                            pe.wait_ge(ks_masked, 2 * c + b)
                            for half in range(2):
                                last = t.matmul(k.bank[:, 6, b * 64:b * 64 + NS + 1], kx[:, j, 2 * b + half], pick[:, half],
                                                start=(half == 0), stop=(half == 1))
                            last.then_inc(ks_ready, 1)
                        for q in range(4):
                            m = 4 * c + q
                            pe.wait_ge(ks_masked, 2 * c + q // 2 + 1)
                            pe.wait_ge(q_copied, c + 3)
                            pe.wait_ge(measured, m)
                            t.matmul(k.bank[0:HALF, 7, 0:NH * (NS + 1)], qt[:, j, q * HALF:(q + 1) * HALF],
                                     ksm[:, q // 2].rearrange("p a b -> p (a b)"), start=True, stop=True).then_inc(sc_ready, 1)
                pe.wait_ge(measured, NT)
                for gq in range(4):
                    last = t.transpose(k.bank[:, 0, gq * HALF:(gq + 1) * HALF],
                                       m_all[:, gq % 2, (gq // 2) * 128:(gq // 2 + 1) * 128], k.ident[0:HALF, 0:HALF])
                last.then_inc(step_pe, 1)
                pe.wait_ge(step, 10 + 1 + 2 * (NU // 8) + 6)
                for gq in range(4):
                    g, half = gq // 2, gq % 2
                    last = t.transpose(k.bank[0:HALF, 1, gq * 128:(gq + 1) * 128], count[:, g, half * HALF:(half + 1) * HALF],
                                       k.ident[:])
                last.then_inc(step_pe, 1)

        attend(nc, k, q_all, kt_all, v_all, wst, w_o, hmu, rank, rank_t, expand, w_in, w_hi)


def attend(nc, k, q_all, kt_all, v_all, wst, w_o, hmu, rank, rank_t, expand, w_in, w_hi):
    a = k.a
    with ExitStack() as ctx:
        def sb(name, shape, dt=F32):
            return ctx.enter_context(nc.sbuf_tensor(f"att_{name}", shape, dt))

        def sem(name):
            return k.semaphore(f"att_{name}")

        NR, GR = NH * NU, HG * NU
        uline = sb("uline", [HALF, NU])
        urow = sb("urow", [128, 5])
        hmt = sb("hmt", [GR, 2, NH, DH])
        ones_row = sb("ones_row", [1, L])
        inv = sb("inv", [HALF, 1])
        oht = sb("oht", [GR, 2, 2, L])
        oh = sb("oh", [HALF, 2, 2, NR])
        qs = sb("qs", [HALF, 2, 2, 128])
        qm = sb("qm", [128, 2, NR])
        nmax = sb("nmax", [GR, 2, 2])
        prob = sb("prob", [GR, 2, 2, L])
        tot = sb("tot", [GR, 2, 2, 2])
        pt = sb("pt", [HALF, 2, 4, GR])
        pv = sb("pv", [GR, 2, 2, 128])
        vm = sb("vm", [1, 2, 128])
        ot = sb("ot", [128, 2, L])
        made = sem("made")
        prep = sem("prep")
        rows = sem("rank_rows")
        onehot = sem("onehot")
        staged = sem("q_staged")
        gathered = sem("q_gathered")
        qmask = sem("q_masked")
        scored = sem("scored")
        maxed = sem("maxed")
        expd = sem("exped")
        recip = sem("recip")
        normed = sem("normed")
        turned = sem("prob_turned")
        pt_ready = sem("pt_ready")
        pv_ready = sem("pv_ready")
        pv_masked = sem("pv_masked")
        vm_ready = sem("vm_ready")
        vm_copied = sem("vm_copied")
        scat = sem("scattered")
        ot_ready = sem("ot_ready")
        proj = sem("projected")
        added = sem("added")
        block = ctx.enter_context(nc.Block())
        sizes = GE * HC * 128

        @block.sync
        def _(sp):
            load_group(sp, k, 0, wst, w_in, k.group_split, 0)

        @block.gpsimd
        def _(pool):
            g = nc.gpsimd
            g.iota(uline[:], [[1, NU]], base=1, channel_multiplier=0, allow_small_or_imprecise_dtypes=True).then_inc(made, 1)
            g.iota(urow[:, 0:1], [[0, 1]], base=0, channel_multiplier=1, allow_small_or_imprecise_dtypes=True).then_inc(made, 1)
            g.memset(hmt[:], 1.0).then_inc(made, 1)
            g.memset(ones_row[:], 1.0).then_inc(made, 1)
            g.memset(inv[:], 1.0 / L).then_inc(made, 1)
            pool.wait_ge(made, 5)
            for q in range(2):
                g.affine_select(out=hmt[:, q], in_=hmt[:, q], compare_op=ALU.is_ge, fill=0.0, base=NU * HG * q,
                                pattern=[[-NU, NH], [0, DH]], channel_multiplier=1).then_inc(made, 1)
            pool.wait_ge(made, 7)
            for q in range(2):
                g.affine_select(out=hmt[:, q], in_=hmt[:, q], compare_op=ALU.is_ge, fill=0.0, base=NU - 1 - NU * HG * q,
                                pattern=[[NU, NH], [0, DH]], channel_multiplier=-1).then_inc(made, 1)
            split_group(nc, pool, k, 0, wst, w_in, w_hi, 0, 0)

        @block.scalar
        def _(act):
            s = nc.scalar
            with act.Fori(0, B // 2) as i:
                for j in range(2):
                    b = 2 * i + j
                    act.wait_ge(gathered, 2 * i)
                    s.activation(qs[:, j], q_all[:, bass.ts(b, 2), :], ACT.Copy).then_inc(staged, 1)
                for j in range(2):
                    b = 2 * i + j
                    for g in range(2):
                        act.wait_ge(maxed, 2 * b + 2)
                        act.wait_ge(turned, 2 * i)
                        s.activation(prob[:, j, g], k.bank[0:GR, 2, g * L:(g + 1) * L], ACT.Exp, bias=nmax[:, j, g:g + 1],
                                     accum_out=tot[:, j, 0, g:g + 1]).then_inc(expd, 1)
                for j in range(2):
                    b = 2 * i + j
                    act.wait_ge(turned, b + 1)
                    act.wait_ge(pv_ready, 2 * i)
                    s.activation(pt[:, j].rearrange("p a b -> p (a b)"), k.bank[0:HALF, 3, 0:4 * GR], ACT.Copy).then_inc(pt_ready, 1)
                    act.wait_ge(vm_ready, b + 1)
                    act.wait_ge(scat, 2 * i)
                    s.activation(vm[:, j], k.bank[0:1, 6, 0:128], ACT.Copy).then_inc(vm_copied, 1)
                    act.wait_ge(scat, b + 1)
                    act.wait_ge(proj, 2 * i)
                    s.activation(ot[:, j], k.bank[:, 5, 0:L], ACT.Copy).then_inc(ot_ready, 1)

        @block.vector
        def _(dve):
            v = nc.vector
            dve.wait_ge(made, 9)
            for m, edge in enumerate((NU, 2 * NU, 3 * NU)):
                v.tensor_scalar(urow[:, m + 1:m + 2], urow[:, 0:1], float(edge), -float(NU), ALU.is_ge, ALU.mult).then_inc(prep, 1)
            dve.wait_ge(prep, 3)
            v.tensor_reduce(urow[:, 4:5], urow[:, 0:4], X, ALU.add).then_inc(prep, 1)
            dve.wait_ge(prep, 4)
            v.tensor_scalar(urow[:, 0:1], urow[:, 4:5], 1.0, None, ALU.add).then_inc(prep, 1)
            dve.wait_ge(prep, 5)
            with dve.Fori(0, B // 2) as i:
                for j in range(2):
                    b = 2 * i + j
                    dve.wait_ge(rows, b + 1)
                    v.tensor_scalar(oht[:, j], k.bank[0:GR, 0, 0:2 * L].rearrange("p (g l) -> p g l", g=2), urow[0:GR, 0:1], None,
                                    ALU.is_equal).then_inc(onehot, 1)
                    for half in range(2):
                        v.tensor_tensor(oh[:, j, half].rearrange("p (h u) -> p h u", h=NH),
                                        rank_t[:, half, bass.ts(b, NH)].unsqueeze(2).broadcast_to([HALF, NH, NU]),
                                        uline[:].unsqueeze(1).broadcast_to([HALF, NH, NU]), ALU.is_equal).then_inc(onehot, 1)
                for j in range(2):
                    b = 2 * i + j
                    dve.wait_ge(gathered, b + 1)
                    v.tensor_tensor(qm[:, j].rearrange("p (h u) -> p h u", h=NH), k.bank[:, 1, 0:NR].rearrange("p (h u) -> p h u", h=NH),
                                    hmu[:].unsqueeze(2).broadcast_to([128, NH, NU]), ALU.mult).then_inc(qmask, 1)
                    dve.wait_ge(scored, b + 1)
                    for g in range(2):
                        dve.wait_ge(expd, 4 * i)
                        v.tensor_reduce(nmax[:, j, g:g + 1], k.bank[0:GR, 2, g * L:(g + 1) * L], X, ALU.max,
                                        negate=True).then_inc(maxed, 1)
                for j in range(2):
                    b = 2 * i + j
                    dve.wait_ge(expd, 2 * b + 2)
                    v.reciprocal(tot[:, j, 1], tot[:, j, 0]).then_inc(recip, 1)
                    dve.wait_ge(recip, b + 1)
                    for g in range(2):
                        v.tensor_scalar(prob[:, j, g], prob[:, j, g], tot[:, j, 1, g:g + 1], -1.0 / L, ALU.mult,
                                        ALU.add).then_inc(normed, 1)
                for j in range(2):
                    b = 2 * i + j
                    dve.wait_ge(pv_ready, b + 1)
                    v.tensor_tensor(pv[:, j], k.bank[0:GR, 4, 0:256].rearrange("p (g d) -> p g d", g=2),
                                    hmt[:].rearrange("p g h d -> p g (h d)"), ALU.mult).then_inc(pv_masked, 1)
                    dve.wait_ge(proj, b + 1)
                    v.tensor_tensor(k.h[:, bass.ts(b, L)], k.h[:, bass.ts(b, L)], k.bank[:, 7, 0:L], ALU.add).then_inc(added, 1)

        @block.tensor
        def _(pe):
            t = nc.tensor
            pe.wait_ge(made, 9)
            for gb in range(2):
                with pe.Fori(0, B // 4) as ii:
                    i = ii + gb * (B // 4)
                    for j in range(2):
                        b = 2 * i + j
                        pe.wait_ge(onehot, 3 * b)
                        for g in range(2):
                            last = t.matmul(k.bank[0:GR, 0, g * L:(g + 1) * L],
                                            expand[:, bass.ds(2 * ii + j, 1), g].rearrange("p a b -> p (a b)"),
                                            rank[:, gb], start=True, stop=True)
                        last.then_inc(rows, 1)
                    for j in range(2):
                        b = 2 * i + j
                        pe.wait_ge(onehot, 3 * b + 3)
                        pe.wait_ge(staged, b + 1)
                        pe.wait_ge(qmask, b)
                        for half in range(2):
                            last = t.matmul(k.bank[:, 1, 0:NR], qs[:, j, half], oh[:, j, half], start=(half == 0), stop=(half == 1))
                        last.then_inc(gathered, 1)
                        pe.wait_ge(qmask, b + 1)
                        pe.wait_ge(expd, 2 * b)
                        for g in range(2):
                            last = t.matmul(k.bank[0:GR, 2, g * L:(g + 1) * L], qm[:, j, g * GR:(g + 1) * GR],
                                            kt_all[:, bass.ts(b, L)], start=True, stop=True)
                        last.then_inc(scored, 1)
                    for j in range(2):
                        b = 2 * i + j
                        pe.wait_ge(vm_copied, b)
                        for half in range(2):
                            last = t.matmul(k.bank[0:1, 6, 0:128], inv[:], v_all[:, bass.ds(2 * b + half, 1), :].rearrange("p a b -> p (a b)"),
                                            start=(half == 0), stop=(half == 1))
                        last.then_inc(vm_ready, 1)
                        pe.wait_ge(normed, 2 * b + 2)
                        pe.wait_ge(pt_ready, b)
                        for half in range(2):
                            for g in range(2):
                                q = half * 2 + g
                                last = t.transpose(k.bank[0:HALF, 3, q * GR:(q + 1) * GR], prob[:, j, g, half * HALF:(half + 1) * HALF],
                                                   k.ident[0:GR, 0:GR])
                        last.then_inc(turned, 1)
                        pe.wait_ge(pt_ready, b + 1)
                        pe.wait_ge(pv_masked, b)
                        for g in range(2):
                            for half in range(2):
                                last = t.matmul(k.bank[0:GR, 4, g * 128:(g + 1) * 128], pt[:, j, half * 2 + g],
                                                v_all[:, bass.ds(2 * b + half, 1), :].rearrange("p a b -> p (a b)"),
                                                start=(half == 0), stop=(half == 1))
                        last.then_inc(pv_ready, 1)
                        pe.wait_ge(pv_masked, b + 1)
                        pe.wait_ge(vm_copied, b + 1)
                        pe.wait_ge(ot_ready, b)
                        t.matmul(k.bank[:, 5, 0:L], vm[:, j], ones_row[:], start=True, stop=False)
                        for g in range(2):
                            last = t.matmul(k.bank[:, 5, 0:L], pv[:, j, g], oht[:, j, g], start=False, stop=(g == 1))
                        last.then_inc(scat, 1)
                        pe.wait_ge(ot_ready, b + 1)
                        pe.wait_ge(added, b)
                        t.matmul(k.bank[:, 7, 0:L], w_o[:], ot[:, j], start=True, stop=True).then_inc(proj, 1)


PIECES = 4
PIECE = GE * HC * 128 // PIECES


def load_group(sp, k, g, wst, w_in, split, before):
    for m in range(2 * PIECES):
        src = k.a["e_w1"] if m < PIECES else k.a["e_w2"]
        if m + before >= 2:
            sp.wait_ge(split, before + m - 1)
        sp.dma_start(wst[:, m % 2, :], src[:, bass.ds(g * GE * HC * 128 + (m % PIECES) * PIECE, PIECE)]).then_inc(w_in[m % 2], 16)


def split_group(nc, pool, k, slot, wst, w_in, w_hi, before, high_before):
    for m in range(2 * PIECES):
        cols = slice((m % PIECES) * PIECE, (m % PIECES + 1) * PIECE)
        hi = k.weights[:, slot, 2 * (m // PIECES), cols]
        lo = k.weights[:, slot, 2 * (m // PIECES) + 1, cols]
        pool.wait_ge(w_in[m % 2], 8 * before + 16 * (m // 2 + 1))
        nc.gpsimd.tensor_copy(hi, wst[:, m % 2, :]).then_inc(w_hi, 1)
        pool.wait_ge(w_hi, high_before + m + 1)
        nc.gpsimd.tensor_tensor(lo, wst[:, m % 2, :], hi, ALU.subtract).then_inc(k.group_split, 1)


def second_mixture(nc, k):
    a = k.a
    with ExitStack() as ctx:
        def sb(name, shape, dt=F32):
            return ctx.enter_context(nc.sbuf_tensor(f"m1_{name}", shape, dt))

        def sem(name):
            return k.semaphore(f"m1_{name}")

        drop = E1 - TOP1
        norm = Normed(nc, k, ctx, "m1")
        ut = norm.ut
        router = sb("router", [128, E1])
        rb = sb("rb", [HALF, E1])
        b1 = sb("b1", [128, E1, HC])
        b2 = sb("b2", [E1, 128])
        u_hi = sb("u_hi", [128, T], BF16)
        u_lo = sb("u_lo", [128, T], BF16)
        lg = sb("lg", [HALF, NT, E1])
        ex = k.hc[0:HALF, 0:NT * E1].rearrange("p (n e) -> p n e", n=NT)
        red = sb("red", [HALF, 5, NT])
        row = sb("row", [HALF, 2, E1 + 8])
        best = sb("best", [HALF, 2, 8])
        fin = sb("fin", [HALF, 2, E1 + 8])
        cat = sb("cat", [HALF, 2, 4, 2, E1])
        ct = sb("ct", [E1, 2, CH])
        comb = sb("comb", [128, T], F16)
        wst = sb("wst", [128, 2, PIECE])
        g = k.hc[:, 0:2 * BLK].rearrange("p (c n) -> p c n", c=2)
        hs = k.hc[:, 2 * BLK:4 * BLK].rearrange("p (c n) -> p c n", c=2)
        halves = k.hc[:, 4 * BLK:8 * BLK].bitcast(BF16).rearrange("p (m x c n) -> p m x c n", m=2, x=2, c=2)
        h_hi, h_lo = halves[:, 0], halves[:, 1]

        small_in = sem("small_in")
        u_high = sem("u_high")
        u_low = sem("u_low")
        logits = sem("logits")
        copied = sem("logits_copied")
        s = sem("routing_step")
        expd = sem("exp_ready")
        topk = sem("top_step")
        passed = sem("top_step_passed")
        kept = sem("kept")
        cat_ready = sem("cat_ready")
        turned = sem("comb_turned")
        c_high = sem("comb_high")
        c_low = sem("comb_low")
        bias = sem("bias_ready")
        bias_added = sem("bias_added")
        up = sem("up_ready")
        spread = sem("comb_spread")
        g_ready = sem("gelu_ready")
        scaled = sem("scaled")
        hi_ready = sem("hidden_high")
        low = sem("hidden_low")
        used = sem("hidden_used")
        y_ready = sem("y_ready")
        y_added = sem("y_added")
        w_in = [sem(f"w_in{p}") for p in range(2)]
        w_hi = sem("w_high")
        block = ctx.enter_context(nc.Block())

        def number(grp, tb, e):
            return (grp * NB + tb) * GE + e

        def two(ap):
            return ap.rearrange("p (a b) -> p a b", a=2)

        @block.sync
        def _(sp):
            for dst, src in ((router[:], a["router"]), (rb[:], a["router_b"].partition_broadcast(HALF)), (b1[:], a["e_b1"]),
                             (b2[:], a["e_b2"])):
                sp.dma_start(dst, src).then_inc(small_in, 16)
            for grp in range(1, NG):
                load_group(sp, k, grp, wst, w_in, k.group_split, 2 * PIECES * grp)

        @block.gpsimd
        def _(pool):
            with pool.Fori(0, NC // 2) as i:
                for j in range(2):
                    norm.pool_diagonal(pool, 2 * i + j, j)
            for grp in range(1, NG):
                if grp >= 2:
                    pool.wait_ge(y_ready, (grp - 1) * NB)
                split_group(nc, pool, k, grp % 2, wst, w_in, w_hi, 2 * PIECES * (grp - 1), 2 * PIECES * (grp - 1))

        @block.scalar
        def _(act):
            sc = nc.scalar
            with act.Fori(0, NC // 2) as i:
                for j in range(2):
                    act.wait_ge(norm.u_ready, 2 * i + j + 1)
                    sc.activation(u_hi[:, chunk(2 * i + j)], ut[:, j, :], ACT.Copy).then_inc(u_high, 1)
            act.wait_ge(s, 2)
            sc.activation(ex, lg[:], ACT.Exp).then_inc(expd, 1)
            act.wait_ge(s, 6)
            sc.activation(ex, ex, ACT.Exp).then_inc(expd, 1)
            with act.Fori(0, NC // 2) as i:
                for j in range(2):
                    c = 2 * i + j
                    act.wait_ge(turned, c + 1)
                    act.wait_ge(bias, 2 * i)
                    sc.activation(ct[:, j], k.bank[0:E1, j, 0:CH], ACT.Copy).then_inc(c_high, 1)
                    sc.activation(comb[:, chunk(c)], k.bank[:, j, 0:CH], ACT.Copy, scale=SCL).then_inc(c_high, 1)
            act.sem_inc(used, 2)
            act.wait_ge(c_low, NC)
            for grp in range(NG):
                with act.Fori(0, NB) as tb:
                    with act.Fori(0, GE // 2) as ee:
                        for x in range(2):
                            e = 2 * ee + x
                            it = number(grp, tb, e)
                            for c in range(HC):
                                act.wait_ge(up, 2 * it + c + 1)
                                act.wait_ge(scaled, 2 * it + c + 1)
                                sc.activation(two(g[:, c]), k.bank[:, 2 * c:2 * c + 2, 0:CH], ACT.Gelu,
                                              bias=b1[:, bass.ds(grp * GE + e, 1), c]).then_inc(g_ready, 1)
                            for c in range(HC):
                                act.wait_ge(scaled, 2 * it + c + 3)
                                act.wait_ge(used, it + 1)
                                sc.activation(h_hi[:, x, c], hs[:, c], ACT.Copy).then_inc(hi_ready, 1)

        @block.vector
        def _(dve):
            v = nc.vector
            norm.dve_start(dve)
            dve.wait_ge(small_in, 64)
            with dve.Fori(0, NC // 2) as i:
                dve.wait_ge(u_low, 2 * i)
                for j in range(2):
                    norm.dve_apply(dve, 2 * i + j, j)
                for j in range(2):
                    dve.wait_ge(u_high, 2 * i + j + 1)
                    v.tensor_tensor(u_lo[:, chunk(2 * i + j)], ut[:, j, :], u_hi[:, chunk(2 * i + j)],
                                    ALU.subtract).then_inc(u_low, 1)
                    dve.wait_ge(logits, 2 * i + j + 1)
                    v.tensor_tensor(lg[:, bass.ts(2 * i + j, 4), :],
                                    k.bank[0:HALF, 4 + j, 0:4 * E1].rearrange("p (n e) -> p n e", n=4),
                                    rb[:].unsqueeze(1).broadcast_to([HALF, 4, E1]), ALU.add).then_inc(copied, 1)
            dve.wait_ge(copied, NC)

            def wide(ap):
                return ap.unsqueeze(2).broadcast_to([HALF, NT, E1])

            v.tensor_reduce(red[:, 0], lg[:], X, ALU.max).then_inc(s, 1)
            dve.wait_ge(s, 1)
            v.tensor_tensor(lg[:], lg[:], wide(red[:, 0]), ALU.subtract).then_inc(s, 1)
            dve.wait_ge(expd, 1)
            v.tensor_reduce(red[:, 1], ex, X, ALU.add).then_inc(s, 1)
            dve.wait_ge(s, 3)
            v.reciprocal(red[:, 2], red[:, 1]).then_inc(s, 1)
            dve.wait_ge(s, 4)
            v.tensor_tensor(lg[:], ex, wide(red[:, 2]), ALU.mult).then_inc(s, 1)
            dve.wait_ge(s, 5)
            v.tensor_tensor(ex, lg[:], wide(red[:, 2]), ALU.subtract).then_inc(s, 1)
            v.memset(row[:], SENT).then_inc(s, 1)
            dve.wait_ge(s, 7)
            dve.wait_ge(expd, 2)
            n_top = [0]

            def link(last, per, i):
                n_top[0] += 1
                last.then_inc(topk, 1)
                dve.wait_ge(topk, i * per + n_top[0])
                dve.sem_inc(passed, 1)

            per = 2 + 2 * (drop // 8) + 2
            with dve.Fori(0, NT // 2) as i:
                dve.wait_ge(kept, 2 * i)
                for j in range(2):
                    last = v.tensor_scalar(row[:, j, 0:E1], lg[:, bass.ds(2 * i + j, 1), :].rearrange("p a b -> p (a b)"), -1.0, None, ALU.mult)
                link(last, per, i)
                for _r in range(drop // 8):
                    for j in range(2):
                        last = v.max(best[:, j], row[:, j])
                    link(last, per, i)
                    for j in range(2):
                        last = v.match_replace(row[:, j], best[:, j], row[:, j], MARK)
                    link(last, per, i)
                for j in range(2):
                    last = v.max(best[:, j], row[:, j])
                link(last, per, i)
                link(v.memset(best[:, :, drop % 8:8], SENT), per, i)
                for j in range(2):
                    last = v.match_replace(fin[:, j], best[:, j], row[:, j], MARK)
                link(last, per, i)
                for j in range(2):
                    here = ex[:, bass.ds(2 * i + j, 1), :].rearrange("p a b -> p (a b)")
                    v.scalar_tensor_tensor(here, fin[:, j, 0:E1], CUT, here, ALU.is_gt, ALU.mult).then_inc(kept, 1)
            assert n_top[0] == per
            dve.wait_ge(kept, NT)
            v.tensor_reduce(red[:, 3], ex, X, ALU.add).then_inc(s, 1)
            dve.wait_ge(s, 8)
            v.reciprocal(red[:, 4], red[:, 3]).then_inc(s, 1)
            dve.wait_ge(s, 9)
            with dve.Fori(0, NC // 2) as i:
                for j in range(2):
                    c = 2 * i + j
                    dve.wait_ge(turned, 2 * i)
                    v.tensor_tensor(cat[:, j], ex[:, bass.ts(c, 4), :].unsqueeze(2).broadcast_to([HALF, 4, 2, E1]),
                                    red[:, 4, bass.ts(c, 4)].unsqueeze(2).unsqueeze(3).broadcast_to([HALF, 4, 2, E1]),
                                    ALU.mult).then_inc(cat_ready, 1)
                for j in range(2):
                    c = 2 * i + j
                    dve.wait_ge(c_high, 2 * c + 2)
                    lo = comb[E1:128, chunk(c)]
                    v.scalar_tensor_tensor(lo, k.bank[E1:128, j, 0:CH], SCL, lo, ALU.mult, ALU.subtract).then_inc(c_low, 1)
                    dve.wait_ge(bias, c + 1)
                    v.tensor_tensor(k.h[:, chunk(c)], k.h[:, chunk(c)], k.bank[:, 2 + j, 0:CH], ALU.add).then_inc(bias_added, 1)
            dve.sem_inc(scaled, 2)
            dve.sem_inc(low, 2)

            def expert(grp, tb, e, x):
                it = number(grp, tb, e)
                for c in range(HC):
                    dve.wait_ge(g_ready, 2 * it + c + 1)
                    dve.wait_ge(spread, it + 1)
                    dve.wait_ge(low, 2 * it + c + 1)
                    v.tensor_tensor(two(hs[:, c]), two(g[:, c]), k.bank[:, 4:6, 0:CH], ALU.mult).then_inc(scaled, 1)
                for c in range(HC):
                    dve.wait_ge(hi_ready, 2 * it + c + 1)
                    v.tensor_tensor(h_lo[:, x, c], hs[:, c], h_hi[:, x, c], ALU.subtract).then_inc(low, 1)

            def add(nth, tb):
                dve.wait_ge(y_ready, nth + 1)
                v.tensor_tensor(two(k.h[:, bass.ds(tb * BLK, BLK)]), two(k.h[:, bass.ds(tb * BLK, BLK)]), k.bank[:, 6:8, 0:CH],
                                ALU.add).then_inc(y_added, 1)

            def rest(grp, tb):
                expert(grp, tb, 1, 1)
                with dve.Fori(1, GE // 2) as ee:
                    for x in range(2):
                        expert(grp, tb, 2 * ee + x, x)

            for grp in range(NG):
                expert(grp, 0, 0, 0)
                if grp:
                    add(grp * NB - 1, NB - 1)
                rest(grp, 0)
                with dve.Fori(1, NB) as tb:
                    expert(grp, tb, 0, 0)
                    add(grp * NB + tb - 1, tb - 1)
                    rest(grp, tb)
            add(NG * NB - 1, NB - 1)

        @block.tensor
        def _(pe):
            t = nc.tensor
            pe.wait_ge(small_in, 64)
            with pe.Fori(0, NC // 2) as i:
                for j in range(2):
                    norm.pe_spread(pe, 2 * i + j, j)
                for j in range(2):
                    pe.wait_ge(norm.u_ready, 2 * i + j + 1)
                    pe.wait_ge(copied, 2 * i)
                    for q in range(4):
                        last = t.matmul(k.bank[0:HALF, 4 + j, q * E1:(q + 1) * E1], ut[:, j, q * HALF:(q + 1) * HALF],
                                        router[:], start=True, stop=True)
                    last.then_inc(logits, 1)
            with pe.Fori(0, NC // 2) as i:
                for j in range(2):
                    c = 2 * i + j
                    pe.wait_ge(cat_ready, c + 1)
                    pe.wait_ge(c_low, 2 * i)
                    for q in range(4):
                        last = t.transpose(k.bank[:, j, q * HALF:(q + 1) * HALF], cat[:, j, q].rearrange("p a b -> p (a b)"),
                                           k.ident[0:HALF, 0:HALF])
                    last.then_inc(turned, 1)
                for j in range(2):
                    c = 2 * i + j
                    pe.wait_ge(c_high, 2 * c + 1)
                    pe.wait_ge(bias_added, 2 * i)
                    t.matmul(k.bank[:, 2 + j, 0:CH], b2[:], ct[:, j], start=True, stop=True).then_inc(bias, 1)
            pe.wait_ge(bias_added, NC)
            pe.wait_ge(c_low, NC)

            def front(grp, tb, e, first=False):
                it = number(grp, tb, e)
                for c in range(HC):
                    if not first:
                        pe.wait_ge(g_ready, 2 * it + c - 1)
                    at = bass.ds((e * HC + c) * 128, 128)
                    w = [k.weights[:, grp % 2, m, at] for m in range(2)]
                    for m, (ww, uu) in enumerate(((w[0], u_hi), (w[0], u_lo), (w[1], u_hi))):
                        for q in range(2):
                            last = t.matmul(k.bank[:, 2 * c + q, 0:CH], ww, uu[:, bass.ds(tb * BLK + q * CH, CH)],
                                            start=(m == 0), stop=(m == 2))
                    last.then_inc(up, 1)
                if not first:
                    pe.wait_ge(scaled, 2 * it + 2)
                for q in range(2):
                    last = t.matmul(k.bank[:, 4 + q, 0:CH], k.sel[:, bass.ds(grp * GE + e, 1), :].rearrange("p a b -> p (a b)"),
                                    comb[:, bass.ds(tb * BLK + q * CH, CH)], start=True, stop=True)
                last.then_inc(spread, 1)

            def back(grp, tb, e, x, start=False, stop=False):
                it = number(grp, tb, e)
                for c in range(HC):
                    at = bass.ds((e * HC + c) * 128, 128)
                    w = [k.weights[:, grp % 2, 2 + m, at] for m in range(2)]
                    pe.wait_ge(hi_ready, 2 * it + c + 1)
                    for m, (ww, hh) in enumerate(((w[0], h_hi), (w[1], h_hi), (w[0], h_lo))):
                        if m == 2:
                            pe.wait_ge(low, 2 * it + c + 3)
                        for q in range(2):
                            last = t.matmul(k.bank[:, 6 + q, 0:CH], ww, hh[:, x, c, q * CH:(q + 1) * CH],
                                            start=(start and c == 0 and m == 0), stop=(stop and c == HC - 1 and m == 2))
                    if c == 0:
                        continue
                    last.then_inc(used, 1)
                    if stop:
                        pe.wait_ge(used, it + 3)
                        pe.sem_inc(y_ready, 1)

            def block_of_tokens(grp, tb, after, first=False):
                front(grp, tb, 1)
                if not first:
                    pe.wait_ge(y_added, grp * NB + tb)
                back(grp, tb, 0, 0, start=True)
                with pe.Fori(0, GE // 2 - 1) as ee:
                    for x in (1, 2):
                        front(grp, tb, 2 * ee + x + 1)
                        back(grp, tb, 2 * ee + x, x % 2)
                if after:
                    front(*after, 0)
                back(grp, tb, GE - 1, 1, stop=True)

            pe.wait_ge(k.group_split, 2 * PIECES)
            for grp in range(NG):
                if grp == 0:
                    front(0, 0, 0, first=True)
                    block_of_tokens(grp, 0, (grp, 1), first=True)
                with pe.Fori(0 if grp else 1, NB - 1) as tb:
                    block_of_tokens(grp, tb, (grp, tb + 1))
                if grp + 1 < NG:
                    pe.wait_ge(k.group_split, 2 * PIECES * (grp + 2))
                    block_of_tokens(grp, NB - 1, (grp + 1, 0))
                else:
                    block_of_tokens(grp, NB - 1, None)


def store(nc, k, out):
    with ExitStack() as ctx:
        stored = k.semaphore("result_stored")
        block = ctx.enter_context(nc.Block())

        @block.sync
        def _(sp):
            for p in range(4):
                cols = slice(p * T // 4, (p + 1) * T // 4)
                sp.dma_start(out[:, cols], k.h[:, cols]).then_inc(stored, 16)
            sp.wait_ge(stored, 64)


def audio_tower(nc, a, out):
    k = Kernel()
    k.a = a
    with ExitStack() as ctx:
        def sb(name, shape, dt=F32):
            return ctx.enter_context(nc.sbuf_tensor(name, shape, dt))

        k.semaphore = lambda name: ctx.enter_context(nc.semaphore(name))
        k.bank = ctx.enter_context(nc.psum_tensor("bank", [128, 8, 512], F32))
        k.h = sb("h", [128, T])
        k.hc = sb("hc", [128, T])
        k.rstd = sb("rstd", [128, NT])
        k.ident = sb("ident", [128, 128])
        k.mean_w = sb("mean_w", [128, 128])
        k.ones = sb("ones", [128, 128])
        k.eps = sb("eps", [128, 1])
        k.hm = sb("hm", [128, NH])
        k.sel = sb("sel", [128, E1, 128], F16)
        k.weights = sb("weights", [128, 2, 4, GE * HC * 128], BF16)
        k.w0_split = k.semaphore("w0_split")
        k.w2_in = k.semaphore("w0_down_in")
        k.group_split = k.semaphore("expert_group_split")
        stages = [
            lambda: constants_and_tokens(nc, k, a["x"], a["w_tok"], a["bias"]),
            lambda: (norm_statistics(nc, k, "n1"), recurrence(nc, k)),
            lambda: (norm_statistics(nc, k, "n2"), first_mixture(nc, k)),
            lambda: (norm_statistics(nc, k, "n3"), sparse_attention(nc, k)),
            lambda: (norm_statistics(nc, k, "n4"), second_mixture(nc, k)),
        ]
        for stage in stages:
            stage()
        store(nc, k, out)


def kernel(**i):
    import numpy as np
    import concourse.bacc as bacc
    from concourse.bass_utils import run_bass_kernel_spmd

    def two(v):
        return v.reshape(2, 128).T

    lay = {
        "x": i["x"][:, :3 * L].reshape(B * L, 2, KT).transpose(2, 1, 0),
        "w_tok": i["L0_tok_weight"].T.reshape(2, KT, D).transpose(1, 0, 2),
        "bias": i["L0_tok_bias"].reshape(D, 1),
        "theta": two(i["L0_attn_theta_log"]),
        "nu": two(i["L0_attn_nu_log"]),
        "gamma": two(i["L0_attn_gamma_log"]),
        "b_re": i["L0_attn_B_re"].T,
        "b_im": i["L0_attn_B_im"].T,
        "c_re": i["L0_attn_C_re"].T.reshape(2, 128, D).transpose(1, 0, 2),
        "c_im": i["L0_attn_C_im"].T.reshape(2, 128, D).transpose(1, 0, 2),
        "d": i["L0_attn_D"].T,
        "gate": i["L0_ffn_gate_weight"].T,
        "w1": i["L0_ffn_w1"].transpose(2, 0, 1).reshape(D, E0 * FF0),
        "w2": i["L0_ffn_w2"].reshape(E0, D, FC, 128).transpose(3, 0, 2, 1),
        "wq": i["L1_attn_Wq"], "wk": i["L1_attn_Wk"], "wv": i["L1_attn_Wv"], "wo": i["L1_attn_Wo"],
        "idx": i["L1_attn_idx_sample"].reshape(1, NS),
        "e_w1": i["L1_ffn_w1"][::-1].transpose(1, 0, 2).reshape(D, E1 * FF1),
        "e_b1": i["L1_ffn_b1"][::-1].reshape(E1, HC, 128).transpose(2, 0, 1),
        "e_w2": i["L1_ffn_w2"][::-1].reshape(E1, HC, 128, D).transpose(2, 0, 1, 3).reshape(128, E1 * HC * D),
        "e_b2": i["L1_ffn_b2"][::-1],
        "router": i["L1_ffn_router_w"][:, ::-1],
        "router_b": i["L1_ffn_router_b"][::-1].reshape(1, E1),
    }
    nc = bacc.Bacc("TRN2", target_bir_lowering=False, num_devices=1)
    arrays, args = {}, {}
    for name, v in lay.items():
        arrays[f"{name}_dram"] = v = np.ascontiguousarray(v)
        args[name] = nc.dram_tensor(f"{name}_dram", v.shape, mybir.dt.from_np(v.dtype), kind="ExternalInput").ap()
    out = nc.dram_tensor("out_dram", (D, T), F32, kind="ExternalOutput").ap()
    audio_tower(nc, args, out)
    r = run_bass_kernel_spmd(nc, [arrays], core_ids=[0])
    return r.results[0]["out_dram"].reshape(D, B, L).transpose(1, 2, 0)
```

```python
from contextlib import ExitStack

import concourse.bass as bass
from concourse import mybir

ALU = mybir.AluOpType
ACT = mybir.ActivationFunctionType
X = mybir.AxisListType.X
F32 = mybir.dt.float32
F16 = mybir.dt.float16
BF16 = mybir.dt.bfloat16
I32 = mybir.dt.int32

B, L, D = 32, 166, 128
T = B * L
HALF = L // 2
NT = 2 * B
CH = 2 * L
NC = T // CH
BLK = 2 * CH
NB = T // BLK
KT = 96
HID = 256
E0, FF0 = 16, 512
FC = FF0 // 128
E1, FF1, TOP1 = 64, 256, 42
HC = FF1 // 128
NH, DH = 8, 16
NS = 38
NU = 25
HG = 4
GE, NG = 16, 4
SENT = -2.0e38
MARK = -3.0e38
CUT = -2.5e38
EPS = 1e-5
SCL = 256.0
ROUND = 12582912.0
LOG2E = 1.4426950408889634
LN2_HI, LN2_LO = 0.693359375, -2.12194440e-4
INV2PI = 0.15915494309189535
PI2_A, PI2_B = 6.28125, 0.0019350051879882812
PI2_C = 6.283185307179586 - 6.28125 - 0.0019350051879882812


def chunk(c):
    return bass.ts(c, CH)


class Kernel:
    pass


def constants_and_tokens(nc, k, x, w_tok, bias):
    with ExitStack() as ctx:
        xs = ctx.enter_context(nc.sbuf_tensor("xs", [KT, 2, T], F32))
        wt = ctx.enter_context(nc.sbuf_tensor("wt", [KT, 2, D], F32))
        bs = ctx.enter_context(nc.sbuf_tensor("bs", [128, 1], F32))
        parts = 4
        per = NC // parts
        w_in = k.semaphore("tok_w_in")
        x_in = [k.semaphore(f"tok_x_in{p}") for p in range(parts)]
        prod = k.semaphore("tok_product_ready")
        h_ready = k.semaphore("tok_bank_read")
        blank = k.semaphore("const_blank")
        made = k.semaphore("const_made")
        block = ctx.enter_context(nc.Block())

        @block.sync
        def _(sp):
            sp.dma_start(wt[:], w_tok).then_inc(w_in, 16)
            sp.dma_start(bs[:], bias).then_inc(w_in, 16)
            for p in range(parts):
                cols = slice(p * per * CH, (p + 1) * per * CH)
                sp.dma_start(xs[:, :, cols], x[:, :, cols]).then_inc(x_in[p], 16)

        @block.gpsimd
        def _(pool):
            g = nc.gpsimd
            g.memset(k.ident[:], 0.0).then_inc(blank, 1)
            g.memset(k.sel[:], 0.0).then_inc(blank, 1)
            g.memset(k.hm[:], 1.0).then_inc(blank, 1)
            g.memset(k.mean_w[:], 1.0 / D).then_inc(made, 1)
            g.memset(k.ones[:], 1.0).then_inc(made, 1)
            g.memset(k.rstd[:], 0.0).then_inc(made, 1)
            g.memset(k.eps[:], EPS).then_inc(made, 1)
            pool.wait_ge(blank, 3)
            g.affine_select(out=k.ident[:], in_=k.ident[:], compare_op=ALU.not_equal, fill=1.0, base=0,
                            pattern=[[-1, 128]], channel_multiplier=1).then_inc(made, 1)
            g.affine_select(out=k.sel[:], in_=k.sel[:], compare_op=ALU.not_equal, fill=1.0 / SCL, base=0,
                            pattern=[[-1, E1], [0, 128]], channel_multiplier=1).then_inc(blank, 1)
            g.affine_select(out=k.hm[:], in_=k.hm[:], compare_op=ALU.is_ge, fill=0.0, base=0,
                            pattern=[[-DH, NH]], channel_multiplier=1).then_inc(blank, 1)
            pool.wait_ge(blank, 5)
            g.affine_select(out=k.sel[:], in_=k.sel[:], compare_op=ALU.not_equal, fill=1.0 / SCL, base=-E1,
                            pattern=[[-1, E1], [0, 128]], channel_multiplier=1).then_inc(made, 1)
            g.affine_select(out=k.hm[:], in_=k.hm[:], compare_op=ALU.is_ge, fill=0.0, base=DH - 1,
                            pattern=[[DH, NH]], channel_multiplier=-1).then_inc(made, 1)

        @block.tensor
        def _(pe):
            pe.wait_ge(w_in, 32)
            for p in range(parts):
                pe.wait_ge(x_in[p], 16)
                for cc in range(per):
                    c = p * per + cc
                    if c >= 4:
                        pe.wait_ge(h_ready, c - 3)
                    for q in range(2):
                        last = nc.tensor.matmul(k.bank[:, c % 4, 0:CH], wt[:, q, :], xs[:, q, c * CH:(c + 1) * CH],
                                                start=(q == 0), stop=(q == 1))
                    last.then_inc(prod, 1)

        @block.vector
        def _(dve):
            dve.wait_ge(w_in, 32)
            for c in range(NC):
                dve.wait_ge(prod, c + 1)
                nc.vector.tensor_scalar(k.h[:, c * CH:(c + 1) * CH], k.bank[:, c % 4, 0:CH], bs[:], None,
                                        ALU.add).then_inc(h_ready, 1)


DEEP = 4


def norm_statistics(nc, k, name):
    with ExitStack() as ctx:
        sq = ctx.enter_context(nc.sbuf_tensor(f"{name}_sq", [128, DEEP, CH], F32))
        st = ctx.enter_context(nc.sbuf_tensor(f"{name}_st", [HALF, 4, NT], F32))
        mean = k.semaphore(f"{name}_mean")
        centred = k.semaphore(f"{name}_centred")
        squared = k.semaphore(f"{name}_squared")
        var = k.semaphore(f"{name}_variance")
        root = k.semaphore(f"{name}_root")
        step = k.semaphore(f"{name}_step")
        block = ctx.enter_context(nc.Block())
        v = k.bank[0:HALF, DEEP, 0:NT]

        @block.tensor
        def _(pe):
            pe.sem_inc(var, DEEP)
            with pe.Fori(0, NC // DEEP) as i:
                for j in range(DEEP):
                    pe.wait_ge(centred, DEEP * i + j + 1)
                    nc.tensor.matmul(k.bank[:, j, 0:CH], k.mean_w[:], k.h[:, chunk(DEEP * i + j)],
                                     start=True, stop=True).then_inc(mean, 1)
                for j in range(DEEP):
                    pe.wait_ge(squared, DEEP * i + j + 1)
                    for q in range(4):
                        last = nc.tensor.matmul(k.bank[0:HALF, DEEP, bass.ds((DEEP * i + j) * 4 + q, 1)],
                                                sq[:, j, q * HALF:(q + 1) * HALF], k.mean_w[:, 0:1],
                                                start=True, stop=True)
                    last.then_inc(var, 1)

        @block.vector
        def _(dve):
            dve.sem_inc(centred, DEEP)
            with dve.Fori(0, NC // DEEP) as i:
                for j in range(DEEP):
                    dve.wait_ge(mean, DEEP * i + j + 1)
                    nc.vector.tensor_tensor(k.hc[:, chunk(DEEP * i + j)], k.h[:, chunk(DEEP * i + j)], k.bank[:, j, 0:CH],
                                            ALU.subtract).then_inc(centred, 1)
            dve.wait_ge(var, NC + DEEP)
            nc.vector.tensor_scalar(st[:, 0], v, EPS, None, ALU.add).then_inc(step, 1)
            dve.wait_ge(root, 1)
            nc.vector.reciprocal(st[:, 2], st[:, 1]).then_inc(step, 1)
            dve.wait_ge(step, 2)
            nc.vector.tensor_tensor(st[:, 3], st[:, 2], st[:, 2], ALU.mult).then_inc(step, 1)
            dve.wait_ge(step, 3)
            nc.vector.tensor_tensor(st[:, 1], st[:, 3], st[:, 0], ALU.mult).then_inc(step, 1)
            dve.wait_ge(step, 4)
            nc.vector.tensor_scalar(st[:, 3], st[:, 1], -0.5, 1.5, ALU.mult, ALU.add).then_inc(step, 1)
            dve.wait_ge(step, 5)
            nc.vector.tensor_tensor(k.rstd[0:HALF, 0:NT], st[:, 2], st[:, 3], ALU.mult).then_inc(step, 1)

        @block.scalar
        def _(act):
            with act.Fori(0, NC // DEEP) as i:
                for j in range(DEEP):
                    act.wait_ge(centred, DEEP * i + j + DEEP + 1)
                    act.wait_ge(var, DEEP * i + j + 1)
                    nc.scalar.activation(sq[:, j, :], k.hc[:, chunk(DEEP * i + j)], ACT.Square).then_inc(squared, 1)
            act.wait_ge(step, 1)
            nc.scalar.activation(st[:, 1], st[:, 0], ACT.Sqrt).then_inc(root, 1)


def recurrence(nc, k):
    a = k.a
    with ExitStack() as ctx:
        def sb(name, shape, dt=F32):
            return ctx.enter_context(nc.sbuf_tensor(f"lru_{name}", shape, dt))

        def sem(name):
            return k.semaphore(f"lru_{name}")

        par = sb("par", [128, 3, 2])
        w_b = sb("w_b", [128, 2, HID])
        w_c = sb("w_c", [128, 3, 2, 128])
        w_cr = sb("w_cr", [128, 2, 2, 128])
        w_d = sb("w_d", [128, 128])
        ex = sb("ex", [128, 7, 4])
        bits = sb("bits", [128, 4], I32)
        mag = sb("mag", [128, 4])
        ph = sb("ph", [128, 5, 2])
        time = sb("time", [128, L])
        ang = sb("ang", [128, 4, 2, L])
        rot = sb("rot", [128, 4, 2, CH])
        decay = sb("decay", [128, 2, CH])
        diag = sb("diag", [HALF, 2, 4, HALF])
        ut = sb("ut", [128, 2, CH])
        va = sb("va", [128, 2, CH])
        vb = sb("vb", [128, 2, CH])
        gs = sb("gs", [128, 2, CH])
        xc = sb("xc", [128, 2, 2, CH])
        xsn = sb("xs", [128, 2, 2, CH])
        ysb = sb("ysb", [128, 2, CH])
        wst = sb("wst", [128, 2, 2048])

        small_in = sem("small_in")
        blank = sem("time_made")
        t = sem("table_step")
        conv = sem("exponent_bits")
        sine = sem("sine")
        tables = sem("tables_ready")
        negated = sem("c_negated")
        diag_ready = sem("diag_ready")
        spread = sem("rstd_spread")
        u_ready = sem("u_ready")
        bu = sem("bu_ready")
        turned = sem("bu_turned")
        joined = sem("turned_joined")
        scanned = sem("scanned")
        back = sem("turned_back")
        y_half = sem("y_half")
        y_ready = sem("y_ready")
        y_copied = sem("y_copied")
        y_added = sem("y_added")
        w_in = [sem(f"w0_in{p}") for p in range(2)]
        w_hi = sem("w0_high")
        block = ctx.enter_context(nc.Block())

        def exists(c):
            return not isinstance(c, int) or 0 <= c < NC

        def chunks(eng, work):
            for c in range(2):
                work(c, c)
            with eng.Fori(1, NC // 2 - 1) as i:
                for j in range(2):
                    work(2 * i + j, j)
            for c in range(NC - 2, NC):
                work(c, c % 2)

        w0 = k.weights[:, 0].rearrange("p a b -> p (a b)")
        w0_hi, w0_lo = w0[:, 0:E0 * FF0], w0[:, E0 * FF0:]
        k.w0_down = k.weights[:, 1].bitcast(F32).rearrange("p a b -> p (a b)")
        pieces = E0 * FF0 // 2048

        @block.sync
        def _(sp):
            for q, name in enumerate(("theta", "nu", "gamma")):
                sp.dma_start(par[:, q, :], a[name]).then_inc(small_in, 16)
            sp.dma_start(w_b[:, 0, :], a["b_re"]).then_inc(small_in, 16)
            sp.dma_start(w_b[:, 1, :], a["b_im"]).then_inc(small_in, 16)
            sp.dma_start(w_cr[:, 0], a["c_re"]).then_inc(small_in, 16)
            sp.dma_start(w_cr[:, 1], a["c_im"]).then_inc(small_in, 16)
            sp.dma_start(w_d[:], a["d"]).then_inc(small_in, 16)
            for p in range(pieces):
                if p >= 2:
                    sp.wait_ge(k.w0_split, p - 1)
                sp.dma_start(wst[:, p % 2, :], a["w1"][:, p * 2048:(p + 1) * 2048]).then_inc(w_in[p % 2], 16)
            sp.dma_start(k.w0_down, a["w2"].rearrange("p e f d -> p (e f d)")).then_inc(k.w2_in, 16)

        @block.gpsimd
        def _(pool):
            g = nc.gpsimd
            g.iota(time[:], [[1, L]], base=1, channel_multiplier=0,
                   allow_small_or_imprecise_dtypes=True).then_inc(blank, 1)
            for p in range(pieces):
                cols = slice(p * 2048, (p + 1) * 2048)
                pool.wait_ge(w_in[p % 2], 16 * (p // 2 + 1))
                g.tensor_copy(w0_hi[:, cols], wst[:, p % 2, :]).then_inc(w_hi, 1)
                pool.wait_ge(w_hi, p + 1)
                g.tensor_tensor(w0_lo[:, cols], wst[:, p % 2, :], w0_hi[:, cols], ALU.subtract).then_inc(k.w0_split, 1)

            def diagonal(c, j):
                pool.wait_ge(spread, c + 1)
                g.tensor_tensor(diag[:, j], k.ident[0:HALF, 0:HALF].unsqueeze(1).broadcast_to([HALF, 4, HALF]),
                                k.rstd[0:HALF, bass.ts(c, 4)].unsqueeze(2).broadcast_to([HALF, 4, HALF]),
                                ALU.mult).then_inc(diag_ready, 1)

            def work(c, j):
                if exists(c + 2):
                    diagonal(c + 2, j)
                pool.wait_ge(y_copied, c + 3)
                g.tensor_tensor(k.h[:, chunk(c)], k.h[:, chunk(c)], ysb[:, j, :], ALU.add).then_inc(y_added, 1)

            for j in range(2):
                diagonal(j, j)
            chunks(pool, work)

        @block.scalar
        def _(act):
            act.wait_ge(t, TABLE_ANGLE)
            nc.scalar.activation(ang[:, 1], ang[:, 0], ACT.Sin).then_inc(sine, 1)
            nc.scalar.activation(ang[:, 2], ang[:, 0], ACT.Sin, scale=0.5).then_inc(sine, 1)
            act.sem_inc(y_copied, 2)
            act.sem_inc(y_added, 2)
            with act.Fori(0, NC // 2) as i:
                for j in range(2):
                    act.wait_ge(y_ready, 2 * i + j + 1)
                    act.wait_ge(y_added, 2 * i + j + 1)
                    nc.scalar.activation(ysb[:, j, :], k.bank[:, 6 + j, 0:CH], ACT.Copy).then_inc(y_copied, 1)

        @block.vector
        def _(dve):
            n = [0]
            v = nc.vector

            def step(ins):
                n[0] += 1
                ins.then_inc(t, 1)
                dve.wait_ge(t, n[0])

            done = [0]

            def exponential(out, x, cols):
                w = [ex[:, m, 0:cols] for m in range(7)]
                step(v.tensor_scalar(w[6], x, -87.0, 87.0, ALU.max, ALU.min))
                step(v.tensor_scalar(w[0], w[6], LOG2E, ROUND, ALU.mult, ALU.add))
                step(v.tensor_scalar(w[1], w[0], ROUND, None, ALU.subtract))
                step(v.scalar_tensor_tensor(w[2], w[1], -LN2_HI, w[6], ALU.mult, ALU.add))
                step(v.scalar_tensor_tensor(w[3], w[1], -LN2_LO, w[2], ALU.mult, ALU.add))
                step(v.tensor_scalar(w[4], w[3], 1.0 / 5040, None, ALU.mult))
                src, dst = w[4], w[5]
                for c in (1.0 / 720, 1.0 / 120, 1.0 / 24, 1.0 / 6, 0.5, 1.0):
                    step(v.scalar_tensor_tensor(dst, src, c, w[3], ALU.add, ALU.mult))
                    src, dst = dst, src
                step(v.tensor_scalar(w[0], w[1], 127.0, 8388608.0, ALU.add, ALU.mult))
                step(v.tensor_copy(bits[:, 0:cols], w[0]))
                step(v.scalar_tensor_tensor(out, src, 1.0, bits[:, 0:cols].bitcast(F32), ALU.add, ALU.mult))

            def wrapped(x, work, turns):
                step(v.tensor_scalar(work, turns, INV2PI, ROUND, ALU.mult, ALU.add))
                step(v.tensor_scalar(work, work, ROUND, None, ALU.subtract))
                for part in (PI2_A, PI2_B, PI2_C):
                    step(v.scalar_tensor_tensor(x, work, -part, x, ALU.mult, ALU.add))

            dve.wait_ge(small_in, 128)
            for p in range(2):
                v.tensor_scalar(w_c[:, 1, p], w_cr[:, 1, p], -1.0, None, ALU.mult)
                v.tensor_scalar(w_c[:, 2, p], w_cr[:, 0, p], -1.0, None, ALU.mult)
                step(v.tensor_copy(w_c[:, 0, p], w_cr[:, 0, p]))
            both = par[:, 0:2, :].rearrange("p a b -> p (a b)")
            exponential(mag[:], both, 4)
            step(v.tensor_scalar(ph[:, 0], mag[:, 2:4], -1.0, None, ALU.mult))
            exponential(mag[:, 2:4], ph[:, 0], 2)
            step(v.tensor_copy(ph[:, 1], mag[:, 0:2]))
            wrapped(ph[:, 1], ph[:, 2], ph[:, 1])
            step(v.tensor_scalar(ph[:, 2], ph[:, 1], ROUND / 1024, None, ALU.add))
            step(v.tensor_scalar(ph[:, 3], ph[:, 2], ROUND / 1024, None, ALU.subtract))
            step(v.tensor_tensor(ph[:, 4], ph[:, 1], ph[:, 3], ALU.subtract))
            dve.wait_ge(blank, 1)
            for p in range(2):
                step(v.tensor_scalar(ang[:, 0, p], time[:], ph[:, 3, p:p + 1], None, ALU.mult))
                step(v.tensor_scalar(ang[:, 1, p], time[:], ph[:, 4, p:p + 1], None, ALU.mult))
                step(v.tensor_tensor(ang[:, 2, p], ang[:, 0, p], ang[:, 1, p], ALU.add))
                wrapped(ang[:, 0, p], ang[:, 3, p], ang[:, 2, p])
                step(v.tensor_tensor(ang[:, 0, p], ang[:, 0, p], ang[:, 1, p], ALU.add))
                step(v.tensor_scalar(ang[:, 0, p], ang[:, 0, p], 3.1415925, -3.1415925, ALU.min, ALU.max))
            assert n[0] == TABLE_ANGLE, n[0]
            dve.wait_ge(sine, 2)
            step(v.tensor_tensor(ang[:, 3], ang[:, 2], ang[:, 2], ALU.mult))
            step(v.tensor_scalar(ang[:, 2], ang[:, 3], -2.0, 1.0, ALU.mult, ALU.add))
            for p in range(2):
                for q in range(2):
                    cols = slice(q * L, (q + 1) * L)
                    v.tensor_copy(rot[:, 0, p, cols], ang[:, 2, p])
                    v.tensor_copy(rot[:, 1, p, cols], ang[:, 1, p])
                    v.tensor_scalar(rot[:, 2, p, cols], ang[:, 2, p], par[:, 2, p:p + 1], None, ALU.mult)
                    v.tensor_scalar(rot[:, 3, p, cols], ang[:, 1, p], par[:, 2, p:p + 1], None, ALU.mult)
                    step(v.tensor_scalar(decay[:, p, cols], time[:], 0.0, mag[:, 2 + p:3 + p], ALU.mult, ALU.add))
                    step(v.memset(decay[:, p, q * L:q * L + 1], 0.0))
            dve.sem_inc(spread, 2)
            dve.sem_inc(tables, 1)

            def tab(m, p):
                return rot[:, m, p].unsqueeze(1).broadcast_to([128, 2, CH])

            def normed(c, j):
                if exists(c - 2):
                    dve.wait_ge(y_ready, c - 1)
                dve.wait_ge(spread, c + 3)
                v.tensor_tensor(ut[:, j, :], k.hc[:, chunk(c)], k.bank[:, j, 0:CH], ALU.mult).then_inc(u_ready, 1)

            def state(c, p):
                m = 2 * c + p
                pair = k.bank[:, 2 + 2 * p:4 + 2 * p, 0:CH]
                dve.wait_ge(bu, m + 1)
                if p or exists(c - 1):
                    dve.wait_ge(scanned, 2 * m)
                v.tensor_tensor(va[:], pair, tab(2, p), ALU.mult).then_inc(turned, 1)
                v.tensor_tensor(vb[:], pair, tab(3, p), ALU.mult).then_inc(turned, 1)
                dve.wait_ge(turned, 2 * m + 2)
                v.tensor_tensor(va[:, 0], va[:, 0], vb[:, 1], ALU.add).then_inc(joined, 1)
                v.tensor_tensor(va[:, 1], va[:, 1], vb[:, 0], ALU.subtract).then_inc(joined, 1)
                dve.wait_ge(joined, 2 * m + 2)
                if p or exists(c - 1):
                    dve.wait_ge(back, 2 * m)
                for q in range(2):
                    v.tensor_tensor_scan(gs[:, q], decay[:, p], va[:, q], 0.0, ALU.mult, ALU.add).then_inc(scanned, 1)
                dve.wait_ge(scanned, 2 * m + 2)
                if exists(c - 1):
                    dve.wait_ge(y_half if p == 0 else y_ready, c)
                v.tensor_tensor(xc[:, p], gs[:], tab(0, p), ALU.mult).then_inc(back, 1)
                v.tensor_tensor(xsn[:, p], gs[:], tab(1, p), ALU.mult).then_inc(back, 1)

            def work(c, j):
                state(c, 0)
                if exists(c + 1):
                    normed(c + 1, 1 - j)
                state(c, 1)

            normed(0, 0)
            chunks(dve, work)

        @block.tensor
        def _(pe):
            pe.wait_ge(small_in, 128)
            pe.wait_ge(tables, 1)

            def spread_rstd(c, j):
                pe.wait_ge(diag_ready, c + 1)
                nc.tensor.matmul(k.bank[:, j, 0:CH], k.ones[0:HALF, :], diag[:, j].rearrange("p a b -> p (a b)"),
                                 start=True, stop=True).then_inc(spread, 1)

            def inputs(c, j, p):
                pe.wait_ge(u_ready, c + 1)
                if exists(c - 1):
                    pe.wait_ge(turned, 4 * c + 2 * p - 2)
                for q in range(2):
                    last = nc.tensor.matmul(k.bank[:, 2 + 2 * p + q, 0:CH], w_b[:, q, p * 128:(p + 1) * 128],
                                            ut[:, j, :], start=True, stop=True)
                last.then_inc(bu, 1)

            def outputs(c, j, p):
                if p == 0:
                    pe.wait_ge(y_copied, c + 1)
                pe.wait_ge(back, 4 * c + 2 * p + 2)
                parts = [] if p else [(w_d[:], ut[:, j, :])]
                parts += [(w_c[:, 0, p], xc[:, p, 0]), (w_c[:, 2, p], xsn[:, p, 1]),
                          (w_c[:, 1, p], xsn[:, p, 0]), (w_c[:, 1, p], xc[:, p, 1])]
                for q, (w, x) in enumerate(parts):
                    last = nc.tensor.matmul(k.bank[:, 6 + j, 0:CH], w, x, start=(p == 0 and q == 0),
                                            stop=(p == 1 and q == len(parts) - 1))
                last.then_inc(y_ready if p else y_half, 1)

            def work(c, j):
                outputs(c, j, 0)
                if exists(c + 1):
                    for p in range(2):
                        inputs(c + 1, 1 - j, p)
                if exists(c + 2):
                    spread_rstd(c + 2, j)
                outputs(c, j, 1)

            for j in range(2):
                spread_rstd(j, j)
            for p in range(2):
                inputs(0, 0, p)
            chunks(pe, work)


TABLE_ANGLE = 62


class Normed:

    def __init__(self, nc, k, ctx, name):
        self.nc, self.k = nc, k
        self.diag = ctx.enter_context(nc.sbuf_tensor(f"{name}_diag", [HALF, 2, 4, HALF], F32))
        self.ut = ctx.enter_context(nc.sbuf_tensor(f"{name}_ut", [128, 2, CH], F32))
        self.diag_ready = k.semaphore(f"{name}_diag_ready")
        self.spread = k.semaphore(f"{name}_rstd_spread")
        self.u_ready = k.semaphore(f"{name}_u_ready")

    def pool_diagonal(self, pool, c, j):
        k = self.k
        pool.wait_ge(self.spread, c + 1)
        self.nc.gpsimd.tensor_tensor(
            self.diag[:, j], k.ident[0:HALF, 0:HALF].unsqueeze(1).broadcast_to([HALF, 4, HALF]),
            k.rstd[0:HALF, bass.ts(c, 4)].unsqueeze(2).broadcast_to([HALF, 4, HALF]), ALU.mult).then_inc(self.diag_ready, 1)

    def pe_spread(self, pe, c, j):
        pe.wait_ge(self.diag_ready, c + 1)
        self.nc.tensor.matmul(self.k.bank[:, j, 0:CH], self.k.ones[0:HALF, :],
                              self.diag[:, j].rearrange("p a b -> p (a b)"), start=True, stop=True).then_inc(self.spread, 1)

    def dve_start(self, dve):
        dve.sem_inc(self.spread, 2)

    def dve_apply(self, dve, c, j):
        dve.wait_ge(self.spread, c + 3)
        self.nc.vector.tensor_tensor(self.ut[:, j, :], self.k.hc[:, chunk(c)], self.k.bank[:, j, 0:CH],
                                     ALU.mult).then_inc(self.u_ready, 1)


def first_mixture(nc, k):
    a = k.a
    with ExitStack() as ctx:
        def sb(name, shape, dt=F32):
            return ctx.enter_context(nc.sbuf_tensor(f"m0_{name}", shape, dt))

        def sem(name):
            return k.semaphore(f"m0_{name}")

        norm = Normed(nc, k, ctx, "m0")
        ut = norm.ut
        gate = sb("gate", [128, E0])
        u_hi = sb("u_hi", [128, T], BF16)
        u_lo = sb("u_lo", [128, T], BF16)
        rows = sb("rows", [HALF, NT, E0 + 8])
        top = sb("top", [HALF, NT, 8])
        left = sb("left", [HALF, NT, E0 + 8])
        gap = sb("gap", [HALF, NT, E0])
        e = sb("e", [HALF, NT, E0])
        tot = sb("tot", [HALF, 2, NT])
        cat = sb("cat", [HALF, NT, 48])
        rt = k.hc[0:48, :]
        mask = sb("mask", [128, T], F16)
        xm_hi = sb("xm_hi", [128, 2, BLK], BF16)
        xm_lo = sb("xm_lo", [128, 2, BLK], BF16)
        junk = sb("junk", [128, 2, BLK], BF16)
        part = sb("part", [128, E0 * FC * NB])
        hsum = sb("hsum", [128, E0 * FC])
        msum = sb("msum", [HALF, E0])
        cnt = sb("cnt", [128, 2, E0])
        ymt = sb("ymt", [128, E0])
        ym = sb("ym", [E0, 128])

        gate_in = sem("gate_in")
        u_high = sem("u_high")
        u_low = sem("u_low")
        logits = sem("logits")
        copied = sem("logits_copied")
        s = sem("routing_step")
        expd = sem("exp_ready")
        blank = sem("mask_blank")
        turned = sem("rows_turned")
        rt_ready = sem("rt_ready")
        mask_ready = sem("mask_ready")
        spread = sem("mask_spread")
        masked = sem("u_masked")
        up = sem("up_ready")
        summed = sem("silu_summed")
        fin = sem("mean_step")
        fin_pe = sem("mean_product")
        out = sem("out_ready")
        added = sem("out_added")
        block = ctx.enter_context(nc.Block())
        w0 = k.weights[:, 0].rearrange("p a b -> p (a b)")
        w0_hi, w0_lo = w0[:, 0:E0 * FF0], w0[:, E0 * FF0:]
        w2 = k.w0_down.rearrange("p (e f d) -> p e f d", e=E0, f=FC)
        n_route = 12

        @block.sync
        def _(sp):
            sp.dma_start(gate[:], a["gate"]).then_inc(gate_in, 16)

        @block.gpsimd
        def _(pool):
            nc.gpsimd.memset(cat[:], 0.0).then_inc(blank, 1)
            nc.gpsimd.memset(mask[:], 0.0).then_inc(blank, 1)
            with pool.Fori(0, NC // 2) as i:
                for j in range(2):
                    norm.pool_diagonal(pool, 2 * i + j, j)

        @block.scalar
        def _(act):
            with act.Fori(0, NC // 2) as i:
                for j in range(2):
                    act.wait_ge(norm.u_ready, 2 * i + j + 1)
                    nc.scalar.activation(u_hi[:, chunk(2 * i + j)], ut[:, j, :], ACT.Copy).then_inc(u_high, 1)
            act.wait_ge(s, 2)
            nc.scalar.activation(e[:], gap[:], ACT.Exp).then_inc(expd, 1)
            act.wait_ge(blank, 2)
            with act.Fori(0, NC // 4) as i:
                for j in range(4):
                    act.wait_ge(turned, 4 * i + j + 1)
                    nc.scalar.activation(rt[:, chunk(4 * i + j)], k.bank[0:48, j, 0:CH], ACT.Copy).then_inc(rt_ready, 1)
            act.wait_ge(rt_ready, NC)
            nc.scalar.activation(mask[0:E0, :], rt[32:48, :], ACT.Copy).then_inc(mask_ready, 1)
            act.sem_inc(summed, 2)
            with act.Fori(0, E0) as x:
                for i in range(NB):
                    for f in range(FC):
                        act.wait_ge(up, (x * NB + i) * FC + f + 1)
                        pair = slice(2 + 2 * (f % 2), 4 + 2 * (f % 2))
                        nc.scalar.activation(junk[:, f % 2].rearrange("p (a b) -> p a b", a=2),
                                             k.bank[:, pair, 0:CH], ACT.Silu,
                                             accum_out=part[:, bass.ds(x * (NB * FC) + (f * NB + i), 1)]).then_inc(summed, 1)

        @block.vector
        def _(dve):
            v = nc.vector
            norm.dve_start(dve)
            v.memset(rows[:], SENT).then_inc(copied, 1)
            dve.wait_ge(copied, 1)
            with dve.Fori(0, NC // 2) as i:
                dve.wait_ge(u_low, 2 * i)
                for j in range(2):
                    norm.dve_apply(dve, 2 * i + j, j)
                for j in range(2):
                    dve.wait_ge(u_high, 2 * i + j + 1)
                    v.tensor_tensor(u_lo[:, chunk(2 * i + j)], ut[:, j, :], u_hi[:, chunk(2 * i + j)],
                                    ALU.subtract).then_inc(u_low, 1)
                    dve.wait_ge(logits, 2 * i + j + 1)
                    v.tensor_copy(rows[:, bass.ts(2 * i + j, 4), 0:E0],
                                  k.bank[0:HALF, 4 + j, 0:4 * E0].rearrange("p (n e) -> p n e", n=4)).then_inc(copied, 1)
            dve.wait_ge(copied, NC + 1)
            for n in range(NT):
                last = v.max(top[:, n, :], rows[:, n, :])
            last.then_inc(s, 1)
            dve.wait_ge(s, 1)
            v.tensor_tensor(gap[:], rows[:, :, 0:E0], top[:, :, 0:1].broadcast_to([HALF, NT, E0]), ALU.subtract).then_inc(s, 1)
            dve.wait_ge(s, 2)
            v.memset(top[:, :, 2:8], SENT).then_inc(s, 1)
            dve.wait_ge(s, 3)
            for n in range(NT):
                last = v.match_replace(left[:, n, :], top[:, n, :], rows[:, n, :], MARK)
            last.then_inc(s, 1)
            dve.wait_ge(s, 4)
            dve.wait_ge(blank, 1)
            v.tensor_scalar(cat[:, :, 32:48], left[:, :, 0:E0], CUT, SCL, ALU.is_le, ALU.mult).then_inc(s, 1)
            dve.wait_ge(s, 5)
            dve.wait_ge(expd, 1)
            v.scalar_tensor_tensor(gap[:], cat[:, :, 32:48], 1.0 / SCL, e[:], ALU.mult, ALU.mult).then_inc(s, 1)
            v.tensor_reduce(msum[:], cat[:, :, 32:48].rearrange("p n e -> p e n"), X, ALU.add).then_inc(s, 1)
            dve.wait_ge(s, 6)
            v.tensor_reduce(tot[:, 0], gap[:], X, ALU.add).then_inc(s, 1)
            dve.wait_ge(s, 8)
            v.reciprocal(tot[:, 1], tot[:, 0]).then_inc(s, 1)
            dve.wait_ge(s, 9)
            v.tensor_tensor(cat[:, :, 0:E0], gap[:], tot[:, 1].unsqueeze(2).broadcast_to([HALF, NT, E0]),
                            ALU.mult).then_inc(s, 1)
            dve.wait_ge(u_low, NC)
            with dve.Fori(0, E0) as x:
                for i in range(NB):
                    dve.wait_ge(spread, x * NB + i + 1)
                    m = k.bank[:, 6 * (i % 2):6 * (i % 2) + 2, 0:CH]
                    for dst, src in ((xm_hi, u_hi), (xm_lo, u_lo)):
                        v.tensor_tensor(dst[:, i % 2].rearrange("p (a b) -> p a b", a=2),
                                        src[:, i * BLK:(i + 1) * BLK].rearrange("p (a b) -> p a b", a=2), m,
                                        ALU.mult).then_inc(masked, 1)
            dve.wait_ge(summed, E0 * NB * FC + 2)
            v.tensor_reduce(hsum[:], part[:].rearrange("p (a b) -> p a b", b=NB), X, ALU.add).then_inc(fin, 1)
            dve.wait_ge(fin_pe, 1)
            v.tensor_scalar(cnt[:, 0], k.bank[:, 0, 0:E0], 1.0 / SCL, 1.0, ALU.mult, ALU.max).then_inc(fin, 1)
            dve.wait_ge(fin, 2)
            v.reciprocal(cnt[:, 1], cnt[:, 0]).then_inc(fin, 1)
            dve.wait_ge(fin, 3)
            dve.wait_ge(fin_pe, 2)
            v.tensor_tensor(ymt[:], k.bank[:, 1, 0:E0], cnt[:, 1], ALU.mult).then_inc(fin, 1)
            dve.wait_ge(fin_pe, 3)
            v.tensor_copy(ym[:], k.bank[0:E0, 2, 0:128]).then_inc(fin, 1)
            dve.sem_inc(added, 4)
            with dve.Fori(0, NC // 4) as i:
                for j in range(4):
                    dve.wait_ge(out, 4 * i + j + 1)
                    v.tensor_tensor(k.h[:, chunk(4 * i + j)], k.h[:, chunk(4 * i + j)], k.bank[:, 4 + j, 0:CH],
                                    ALU.add).then_inc(added, 1)

        @block.tensor
        def _(pe):
            t = nc.tensor
            pe.wait_ge(gate_in, 16)
            with pe.Fori(0, NC // 2) as i:
                for j in range(2):
                    norm.pe_spread(pe, 2 * i + j, j)
                for j in range(2):
                    pe.wait_ge(norm.u_ready, 2 * i + j + 1)
                    pe.wait_ge(copied, 2 * i + j)
                    for q in range(4):
                        last = t.matmul(k.bank[0:HALF, 4 + j, q * E0:(q + 1) * E0], ut[:, j, q * HALF:(q + 1) * HALF],
                                        gate[:], start=True, stop=True)
                    last.then_inc(logits, 1)
            pe.wait_ge(s, 10)
            for c in range(NC):
                if c >= 4:
                    pe.wait_ge(rt_ready, c - 3)
                for q in range(4):
                    last = t.transpose(k.bank[0:48, c % 4, q * HALF:(q + 1) * HALF], cat[:, 4 * c + q, :],
                                       k.ident[0:HALF, 0:HALF])
                last.then_inc(turned, 1)
            pe.wait_ge(mask_ready, 1)
            pe.wait_ge(k.w0_split, E0 * FF0 // 2048)

            def pe_mask(x, i):
                for q in range(2):
                    last = t.matmul(k.bank[:, 6 * (i % 2) + q, 0:CH], k.sel[:, bass.ds(x, 1), :].rearrange("p a b -> p (a b)"),
                                    mask[:, i * BLK + q * CH:i * BLK + (q + 1) * CH], start=True, stop=True)
                last.then_inc(spread, 1)

            pe_mask(0, 0)
            with pe.Fori(0, E0) as x:
                for i in range(NB):
                    pe_mask(x + (i + 1) // NB, (i + 1) % NB)
                    pe.wait_ge(masked, 2 * (x * NB + i) + 2)
                    for f in range(FC):
                        hi = w0_hi[:, bass.ds(x * FF0 + f * 128, 128)]
                        lo = w0_lo[:, bass.ds(x * FF0 + f * 128, 128)]
                        pe.wait_ge(summed, (x * NB + i) * FC + f + 1)
                        for m, (w, u) in enumerate(((hi, xm_hi), (hi, xm_lo), (lo, xm_hi))):
                            for q in range(2):
                                last = t.matmul(k.bank[:, 2 + 2 * (f % 2) + q, 0:CH], w, u[:, i % 2, q * CH:(q + 1) * CH],
                                                start=(m == 0), stop=(m == 2))
                        last.then_inc(up, 1)
            pe.wait_ge(masked, 2 * E0 * NB)
            pe.wait_ge(s, 7)
            t.matmul(k.bank[:, 0, 0:E0], k.ones[0:HALF, :], msum[:], start=True, stop=True).then_inc(fin_pe, 1)
            pe.wait_ge(fin, 1)
            pe.wait_ge(k.w2_in, 16)
            for x in range(E0):
                for f in range(FC):
                    last = t.matmul(k.bank[:, 1, x:x + 1], w2[:, x, f, :], hsum[:, x * FC + f:x * FC + f + 1],
                                    start=(f == 0), stop=(f == FC - 1))
            last.then_inc(fin_pe, 1)
            pe.wait_ge(fin, 4)
            t.transpose(k.bank[0:E0, 2, 0:128], ymt[:], k.ident[:]).then_inc(fin_pe, 1)
            pe.wait_ge(fin, 5)
            with pe.Fori(0, NC // 4) as i:
                for j in range(4):
                    pe.wait_ge(added, 4 * i + j + 1)
                    t.matmul(k.bank[:, 4 + j, 0:CH], ym[:], rt[0:E0, chunk(4 * i + j)], start=True, stop=True).then_inc(out, 1)


def sparse_attention(nc, k):
    a = k.a
    with ExitStack() as ctx:
        def sb(name, shape, dt=F32):
            return ctx.enter_context(nc.sbuf_tensor(f"at_{name}", shape, dt))

        def sem(name):
            return k.semaphore(f"at_{name}")

        NR = NH * NU
        GR = HG * NU
        q_all = k.weights[0:HALF, 1].bitcast(F32).rearrange("p a b -> p (a b)").rearrange("p (n d) -> p n d", n=NT)
        kt_all = k.hc
        v_all = sb("v_all", [HALF, NT, 128])
        wst = sb("wst", [128, 2, 1024])
        w_o = sb("w_o", [128, 128])
        v_mean = sb("v_mean", [128, B])
        hmu = sb("hmu", [128, NH])
        rank_t = sb("rank_t", [HALF, 2, 2 * 128])
        rank = sb("rank", [128, 2, L], BF16)
        expand = sb("expand", [128, 16, 2, GR], BF16)

        small_in = sem("small_in")
        made = sem("made")
        step = sem("choose_step")
        step_pe = sem("choose_product")
        w_in = [sem(f"w_in{p}") for p in range(2)]
        w_hi = sem("w_high")

        with ExitStack() as first:
            def sb1(name, shape, dt=F32):
                return first.enter_context(nc.sbuf_tensor(f"at_{name}", shape, dt))

            norm = Normed(nc, k, first, "at")
            ut = norm.ut
            w_qk = sb1("w_qk", [128, 3, 128])
            qt = sb1("qt", [128, 2, CH])
            kx = sb1("kx", [HALF, 2, 4, 128])
            idx = sb1("idx", [HALF, NS], I32)
            pos = sb1("pos", [HALF, 3, NS])
            line = sb1("line", [HALF, 2])
            pick = sb1("pick", [HALF, 2, NS + 1])
            ksm = sb1("ksm", [128, 2, NH, NS + 1])
            peak = sb1("peak", [HALF, 2, NH])
            m_all = sb1("m_all", [HALF, 2, 2 * 128])
            u_sum = sb1("u_sum", [128, B])
            cand = sb1("cand", [128, 2, L + 8])
            best = sb1("best", [128, 2, 8])
            chosen = sb1("chosen", [128, 2, L])
            count = sb1("count", [128, 2, L])
            qt_ready = sem("qt_ready")
            q_copied = sem("q_copied")
            kt_ready = sem("kt_ready")
            kt_copied = sem("kt_copied")
            tok_ready = sem("token_major_ready")
            kx_copied = sem("k_copied")
            ks_ready = sem("samples_ready")
            ks_masked = sem("samples_masked")
            sc_ready = sem("sampled_scores_ready")
            peaked = sem("peak_taken")
            u_summed = sem("u_summed")
            measured = sem("measure_taken")
            block = first.enter_context(nc.Block())

            def exists(c):
                return not isinstance(c, int) or 0 <= c < NC

            def chunks(eng, work):
                for c in range(2):
                    work(c, c)
                with eng.Fori(1, NC // 2 - 1) as i:
                    for j in range(2):
                        work(2 * i + j, j)
                for c in range(NC - 2, NC):
                    work(c, c % 2)

            @block.sync
            def _(sp):
                for q, name in enumerate(("wq", "wv", "wk")):
                    sp.dma_start(w_qk[:, q], a[name]).then_inc(small_in, 16)
                sp.dma_start(w_o[:], a["wo"]).then_inc(small_in, 16)
                sp.dma_start(idx[:], a["idx"].partition_broadcast(HALF)).then_inc(small_in, 16)

            @block.gpsimd
            def _(pool):
                g = nc.gpsimd
                g.iota(line[:], [[HALF, 2]], base=0, channel_multiplier=1,
                       allow_small_or_imprecise_dtypes=True).then_inc(made, 1)
                g.memset(expand[:], 0.0).then_inc(made, 1)
                with pool.Fori(0, NC // 2) as i:
                    for j in range(2):
                        norm.pool_diagonal(pool, 2 * i + j, j)
                pool.wait_ge(made, 2)
                g.affine_select(out=expand[:].rearrange("p b g (h u) -> p (b g h) u", h=HG),
                                in_=expand[:].rearrange("p b g (h u) -> p (b g h) u", h=HG),
                                compare_op=ALU.not_equal, fill=1.0, base=0,
                                pattern=[[-1, 128], [0, NU]], channel_multiplier=1).then_inc(made, 1)

            @block.scalar
            def _(act):
                def work(c, j):
                    act.wait_ge(qt_ready, c + 1)
                    if exists(c - 2):
                        act.wait_ge(sc_ready, 4 * (c - 1))
                    nc.scalar.activation(qt[:, j], k.bank[:, 2, 0:CH], ACT.Copy).then_inc(q_copied, 1)
                    act.wait_ge(kt_ready, c + 1)
                    nc.scalar.activation(kt_all[:, chunk(c)], k.bank[:, 3, 0:CH], ACT.Copy).then_inc(kt_copied, 1)
                    if exists(c - 2):
                        act.wait_ge(ks_ready, 2 * (c - 1))
                    for q in range(4):
                        act.wait_ge(tok_ready, 4 * c + q + 1)
                        for m, dst in enumerate((q_all[:, bass.ds(4 * c + q, 1), :].rearrange("p a b -> p (a b)"),
                                                 v_all[:, bass.ds(4 * c + q, 1), :].rearrange("p a b -> p (a b)"),
                                                 kx[:, j, q])):
                            last = nc.scalar.activation(dst, k.bank[0:HALF, 4 + q % 2, m * 128:(m + 1) * 128], ACT.Copy)
                        last.then_inc(kx_copied, 1)

                chunks(act, work)
                act.wait_ge(step_pe, 1)
                nc.scalar.activation(v_mean[:], k.bank[:, 2, 0:B], ACT.Copy, scale=1.0 / L)

            @block.vector
            def _(dve):
                v = nc.vector
                n = [0]

                def link(ins):
                    n[0] += 1
                    ins.then_inc(step, 1)
                    dve.wait_ge(step, n[0])

                norm.dve_start(dve)
                dve.wait_ge(small_in, 80)
                dve.wait_ge(made, 1)
                link(v.tensor_copy(pos[:, 0], idx[:]))
                link(v.tensor_scalar(pos[:, 1], pos[:, 0], 0.0, float(L), ALU.is_lt, ALU.mult))
                link(v.tensor_tensor(pos[:, 2], pos[:, 0], pos[:, 1], ALU.add))
                link(v.tensor_scalar(pos[:, 0], pos[:, 2], 0.0, float(L - 1), ALU.max, ALU.min))
                for q in range(2):
                    link(v.tensor_scalar(pick[:, q, 0:NS], pos[:, 0], line[:, q:q + 1], None, ALU.is_equal))
                link(v.tensor_reduce(pos[:, 1, 0:2], pick[:, :, 0:NS], X, ALU.add))
                link(v.tensor_scalar(pick[:, :, NS:NS + 1], pos[:, 1, 0:2].unsqueeze(2), 1.0 / NS, None, ALU.mult))
                link(v.tensor_scalar(hmu[:], k.hm[:], DH ** -0.5, None, ALU.mult))
                link(v.memset(cand[:], SENT))

                def normed(c, j):
                    if exists(c - 2):
                        dve.wait_ge(tok_ready, 4 * (c - 1))
                        dve.wait_ge(u_summed, c - 1)
                    norm.dve_apply(dve, c, j)
                    dve.wait_ge(norm.u_ready, c + 1)
                    v.tensor_reduce(u_sum[:, bass.ts(c, 2)], ut[:, j].rearrange("p (b l) -> p b l", b=2), X,
                                    ALU.add).then_inc(u_summed, 1)

                def work(c, j):
                    if exists(c + 1):
                        normed(c + 1, 1 - j)
                    for b in range(2):
                        dve.wait_ge(ks_ready, 2 * c + b + 1)
                        if exists(c - 1):
                            dve.wait_ge(sc_ready, 4 * c)
                        v.tensor_tensor(ksm[:, b], k.bank[:, 6, b * 64:b * 64 + NS + 1].unsqueeze(1).broadcast_to([128, NH, NS + 1]),
                                        k.hm[:].unsqueeze(2).broadcast_to([128, NH, NS + 1]), ALU.mult).then_inc(ks_masked, 1)
                    for q in range(4):
                        m = 4 * c + q
                        sc = k.bank[0:HALF, 7, 0:NH * (NS + 1)].rearrange("p (h s) -> p h s", h=NH)
                        dve.wait_ge(sc_ready, m + 1)
                        v.tensor_reduce(peak[:, q % 2], sc[:, :, 0:NS], X, ALU.max).then_inc(peaked, 1)
                        dve.wait_ge(peaked, m + 1)
                        v.tensor_tensor(m_all[:, q % 2, bass.ds((2 * c + q // 2) * NH, NH)], peak[:, q % 2],
                                        sc[:, :, NS:NS + 1].rearrange("p a b -> p (a b)"), ALU.subtract).then_inc(measured, 1)

                normed(0, 0)
                chunks(dve, work)
                dve.wait_ge(step_pe, 1)
                for gq in range(4):
                    last = v.tensor_copy(cand[:, gq // 2, (gq % 2) * HALF:(gq % 2) * HALF + HALF],
                                         k.bank[:, 0, gq * HALF:(gq + 1) * HALF])
                link(last)
                for r in range(NU // 8):
                    for g in range(2):
                        last = v.max(best[:, g], cand[:, g])
                    link(last)
                    for g in range(2):
                        last = v.match_replace(cand[:, g], best[:, g], cand[:, g], MARK)
                    link(last)
                for g in range(2):
                    last = v.max(best[:, g], cand[:, g])
                link(last)
                link(v.memset(best[:, :, NU % 8:8], SENT))
                for g in range(2):
                    last = v.match_replace(cand[:, g], best[:, g], cand[:, g], MARK)
                link(last)
                link(v.tensor_scalar(chosen[:], cand[:, :, 0:L], CUT, None, ALU.is_le))
                for g in range(2):
                    last = v.tensor_tensor_scan(count[:, g], k.ones[:, 0:1].broadcast_to([128, L]), chosen[:, g], 0.0, ALU.mult, ALU.add)
                link(last)
                link(v.tensor_tensor(count[:], count[:], chosen[:], ALU.mult))
                v.tensor_copy(rank[:], count[:]).then_inc(step, 1)
                dve.wait_ge(step_pe, 2)
                for gq in range(4):
                    g, half = gq // 2, gq % 2
                    v.tensor_copy(rank_t[:, half, g * 128:(g + 1) * 128], k.bank[0:HALF, 1, gq * 128:(gq + 1) * 128])
                k.at_steps = n[0]

            @block.tensor
            def _(pe):
                t = nc.tensor
                pe.wait_ge(small_in, 80)
                pe.wait_ge(step, 10)

                def query(c, j):
                    pe.wait_ge(norm.u_ready, c + 1)
                    if exists(c - 1):
                        pe.wait_ge(q_copied, c)
                    t.matmul(k.bank[:, 2, 0:CH], w_qk[:, 0], ut[:, j], start=True, stop=True).then_inc(qt_ready, 1)

                def key(c, j):
                    if exists(c - 1):
                        pe.wait_ge(kt_copied, c)
                    t.matmul(k.bank[:, 3, 0:CH], w_qk[:, 2], ut[:, j], start=True, stop=True).then_inc(kt_ready, 1)

                def token_major(c, j, q):
                    if q >= 2 or exists(c - 1):
                        pe.wait_ge(kx_copied, 4 * c + q - 1)
                    t.matmul(k.bank[0:HALF, 4 + q % 2, 0:384], ut[:, j, q * HALF:(q + 1) * HALF],
                             w_qk[:].rearrange("p a b -> p (a b)"), start=True, stop=True).then_inc(tok_ready, 1)

                def samples(c, j, b):
                    pe.wait_ge(kx_copied, 4 * c + 2 * b + 2)
                    if b or exists(c - 1):
                        pe.wait_ge(ks_masked, 2 * c + b)
                    for half in range(2):
                        last = t.matmul(k.bank[:, 6, b * 64:b * 64 + NS + 1], kx[:, j, 2 * b + half], pick[:, half],
                                        start=(half == 0), stop=(half == 1))
                    last.then_inc(ks_ready, 1)

                def sampled_scores(c, j, q):
                    pe.wait_ge(ks_masked, 2 * c + q // 2 + 1)
                    pe.wait_ge(q_copied, c + 1)
                    if q or exists(c - 1):
                        pe.wait_ge(measured, 4 * c + q)
                    t.matmul(k.bank[0:HALF, 7, 0:NH * (NS + 1)], qt[:, j, q * HALF:(q + 1) * HALF],
                             ksm[:, q // 2].rearrange("p a b -> p (a b)"), start=True, stop=True).then_inc(sc_ready, 1)

                def work(c, j):
                    ahead = exists(c + 1)
                    samples(c, j, 0)
                    if ahead:
                        query(c + 1, 1 - j)
                    samples(c, j, 1)
                    if ahead:
                        key(c + 1, 1 - j)
                    for q in range(4):
                        if ahead:
                            token_major(c + 1, 1 - j, q)
                        sampled_scores(c, j, q)
                    if exists(c + 2):
                        norm.pe_spread(pe, c + 2, j)

                for j in range(2):
                    norm.pe_spread(pe, j, j)
                query(0, 0)
                key(0, 0)
                for q in range(4):
                    token_major(0, 0, q)
                chunks(pe, work)
                pe.wait_ge(u_summed, NC)
                pe.wait_ge(q_copied, NC)
                t.matmul(k.bank[:, 2, 0:B], w_qk[:, 1], u_sum[:], start=True, stop=True)
                pe.wait_ge(measured, NT)
                for gq in range(4):
                    last = t.transpose(k.bank[:, 0, gq * HALF:(gq + 1) * HALF],
                                       m_all[:, gq % 2, (gq // 2) * 128:(gq // 2 + 1) * 128], k.ident[0:HALF, 0:HALF])
                last.then_inc(step_pe, 1)
                pe.wait_ge(step, 10 + 1 + 2 * (NU // 8) + 6)
                for gq in range(4):
                    g, half = gq // 2, gq % 2
                    last = t.transpose(k.bank[0:HALF, 1, gq * 128:(gq + 1) * 128], count[:, g, half * HALF:(half + 1) * HALF],
                                       k.ident[:])
                last.then_inc(step_pe, 1)

        attend(nc, k, q_all, kt_all, v_all, v_mean, wst, w_o, hmu, rank, rank_t, expand, w_in, w_hi)


def attend(nc, k, q_all, kt_all, v_all, v_mean, wst, w_o, hmu, rank, rank_t, expand, w_in, w_hi):
    with ExitStack() as ctx:
        def sb(name, shape, dt=F32):
            return ctx.enter_context(nc.sbuf_tensor(f"att_{name}", shape, dt))

        def sem(name):
            return k.semaphore(f"att_{name}")

        NR, GR = NH * NU, HG * NU
        U = 4
        uline = sb("uline", [HALF, NU])
        urow = sb("urow", [128, 5])
        hmt = sb("hmt", [GR, 2, NH, DH])
        oht = sb("oht", [GR, U, 2, L])
        oh = sb("oh", [HALF, 2, 2, NR])
        qs = sb("qs", [HALF, 2, 2, 128])
        qm = sb("qm", [128, 2, NR])
        nmax = sb("nmax", [GR, 2, 2])
        prob = sb("prob", [GR, 2, 2, L])
        tot = sb("tot", [GR, 2, 2, 2])
        pt = sb("pt", [HALF, 2, 4, GR])
        pv = sb("pv", [GR, 2, 2, 128])
        ot = sb("ot", [128, 2, L])
        made = sem("made")
        prep = sem("prep")
        rows = sem("rank_rows")
        onehot = sem("onehot")
        staged = sem("q_staged")
        gathered = sem("q_gathered")
        qmask = sem("q_masked")
        scored = sem("scored")
        maxed = sem("maxed")
        expd = sem("exped")
        recip = sem("recip")
        normed = sem("normed")
        turned = sem("prob_turned")
        pt_ready = sem("pt_ready")
        pv_ready = sem("pv_ready")
        pv_masked = sem("pv_masked")
        scat = sem("scattered")
        ot_ready = sem("ot_ready")
        proj = sem("projected")
        added = sem("added")
        block = ctx.enter_context(nc.Block())

        def batches(eng, step):
            for x in range(U):
                step(x, x)
            with eng.Fori(1, B // U) as i:
                for x in range(U):
                    step(U * i + x, x)

        def exists(b):
            return not isinstance(b, int) or 0 <= b < B

        @block.sync
        def _(sp):
            load_group(sp, k, 0, wst, w_in, k.group_split, 0)

        @block.gpsimd
        def _(pool):
            g = nc.gpsimd
            g.iota(uline[:], [[1, NU]], base=1, channel_multiplier=0, allow_small_or_imprecise_dtypes=True).then_inc(made, 1)
            g.iota(urow[:, 0:1], [[0, 1]], base=0, channel_multiplier=1, allow_small_or_imprecise_dtypes=True).then_inc(made, 1)
            g.memset(hmt[:], 1.0).then_inc(made, 1)
            pool.wait_ge(made, 3)
            for q in range(2):
                g.affine_select(out=hmt[:, q], in_=hmt[:, q], compare_op=ALU.is_ge, fill=0.0, base=NU * HG * q,
                                pattern=[[-NU, NH], [0, DH]], channel_multiplier=1).then_inc(made, 1)
            pool.wait_ge(made, 5)
            for q in range(2):
                g.affine_select(out=hmt[:, q], in_=hmt[:, q], compare_op=ALU.is_ge, fill=0.0, base=NU - 1 - NU * HG * q,
                                pattern=[[NU, NH], [0, DH]], channel_multiplier=-1).then_inc(made, 1)
            split_group(nc, pool, k, 0, wst, w_in, w_hi, 0, 0)

        @block.scalar
        def _(act):
            s = nc.scalar

            def exponentials(b, x):
                if not exists(b):
                    return
                act.wait_ge(maxed, b + 1)
                if exists(b - 2):
                    act.wait_ge(turned, b - 1)
                for g in range(2):
                    s.activation(prob[:, x % 2, g], k.bank[0:GR, 2, g * L:(g + 1) * L], ACT.Exp, bias=nmax[:, x % 2, g:g + 1],
                                 accum_out=tot[:, x % 2, 0, g:g + 1]).then_inc(expd, 1)

            def turned_copy(b, x):
                if not exists(b):
                    return
                act.wait_ge(turned, b + 1)
                if exists(b - 2):
                    act.wait_ge(pv_ready, b - 1)
                s.activation(pt[:, x % 2].rearrange("p a b -> p (a b)"), k.bank[0:HALF, 3, 0:4 * GR], ACT.Copy).then_inc(pt_ready, 1)

            def output_copy(b, x):
                if not exists(b):
                    return
                act.wait_ge(scat, b + 1)
                if exists(b - 2):
                    act.wait_ge(proj, b - 1)
                s.activation(ot[:, x % 2], k.bank[:, 5, 0:L], ACT.Identity, bias=v_mean[:, bass.ds(b, 1)]).then_inc(ot_ready, 1)

            def step(b, x):
                if exists(b):
                    if exists(b - 2):
                        act.wait_ge(gathered, b - 1)
                    s.activation(qs[:, x % 2], q_all[:, bass.ts(b, 2), :], ACT.Copy).then_inc(staged, 1)
                exponentials(b - 1, x - 1)
                turned_copy(b - 1, x - 1)
                output_copy(b - 2, x - 2)

            batches(act, step)
            exponentials(B - 1, B - 1)
            turned_copy(B - 1, B - 1)
            output_copy(B - 2, B - 2)
            output_copy(B - 1, B - 1)

        @block.vector
        def _(dve):
            v = nc.vector
            dve.wait_ge(made, 7)
            for m, edge in enumerate((NU, 2 * NU, 3 * NU)):
                v.tensor_scalar(urow[:, m + 1:m + 2], urow[:, 0:1], float(edge), -float(NU), ALU.is_ge, ALU.mult).then_inc(prep, 1)
            dve.wait_ge(prep, 3)
            v.tensor_reduce(urow[:, 4:5], urow[:, 0:4], X, ALU.add).then_inc(prep, 1)
            dve.wait_ge(prep, 4)
            v.tensor_scalar(urow[:, 0:1], urow[:, 4:5], 1.0, None, ALU.add).then_inc(prep, 1)
            dve.wait_ge(prep, 5)

            def one_hots(b, x):
                if not exists(b):
                    return
                dve.wait_ge(rows, b + 1)
                if exists(b - U):
                    dve.wait_ge(scat, b - U + 1)
                v.tensor_scalar(oht[:, x % U], k.bank[0:GR, 0, 0:2 * L].rearrange("p (g l) -> p g l", g=2), urow[0:GR, 0:1], None,
                                ALU.is_equal).then_inc(onehot, 1)
                if exists(b - 2):
                    dve.wait_ge(gathered, b - 1)
                for half in range(2):
                    v.tensor_tensor(oh[:, x % 2, half].rearrange("p (h u) -> p h u", h=NH),
                                    rank_t[:, half, bass.ts(b, NH)].unsqueeze(2).broadcast_to([HALF, NH, NU]),
                                    uline[:].unsqueeze(1).broadcast_to([HALF, NH, NU]), ALU.is_equal).then_inc(onehot, 1)

            def head_mask(b, x):
                if not exists(b):
                    return
                dve.wait_ge(gathered, b + 1)
                if exists(b - 2):
                    dve.wait_ge(scored, b - 1)
                v.tensor_tensor(qm[:, x % 2].rearrange("p (h u) -> p h u", h=NH), k.bank[:, 1, 0:NR].rearrange("p (h u) -> p h u", h=NH),
                                hmu[:].unsqueeze(2).broadcast_to([128, NH, NU]), ALU.mult).then_inc(qmask, 1)

            def maxima(b, x):
                if not exists(b):
                    return
                dve.wait_ge(scored, b + 1)
                if exists(b - 2):
                    dve.wait_ge(expd, 2 * b - 2)
                v.tensor_reduce(nmax[:, x % 2], k.bank[0:GR, 2, 0:2 * L].rearrange("p (g l) -> p g l", g=2), X, ALU.max,
                                negate=True).then_inc(maxed, 1)

            def normalise(b, x):
                if not exists(b):
                    return
                dve.wait_ge(expd, 2 * b + 2)
                v.reciprocal(tot[:, x % 2, 1], tot[:, x % 2, 0]).then_inc(recip, 1)
                dve.wait_ge(recip, b + 1)
                for g in range(2):
                    v.tensor_scalar(prob[:, x % 2, g], prob[:, x % 2, g], tot[:, x % 2, 1, g:g + 1], -1.0 / L, ALU.mult,
                                    ALU.add).then_inc(normed, 1)

            def value_mask(b, x):
                if not exists(b):
                    return
                dve.wait_ge(pv_ready, b + 1)
                if exists(b - 2):
                    dve.wait_ge(scat, b - 1)
                v.tensor_tensor(pv[:, x % 2], k.bank[0:GR, 4, 0:256].rearrange("p (g d) -> p g d", g=2),
                                hmt[:].rearrange("p g h d -> p g (h d)"), ALU.mult).then_inc(pv_masked, 1)

            def residual(b, x):
                if not exists(b):
                    return
                dve.wait_ge(proj, b + 1)
                v.tensor_tensor(k.h[:, bass.ts(b, L)], k.h[:, bass.ts(b, L)], k.bank[:, 7, 0:L], ALU.add).then_inc(added, 1)

            def step(b, x):
                one_hots(b, x)
                maxima(b - 1, x - 1)
                value_mask(b - 2, x - 2)
                normalise(b - 1, x - 1)
                head_mask(b, x)
                residual(b - 3, x - 3)

            batches(dve, step)
            for b in range(B, B + 3):
                step(b, b)

        @block.tensor
        def _(pe):
            t = nc.tensor
            pe.wait_ge(made, 7)

            def rank_rows(b, x, gb, at):
                if exists(b - 1):
                    pe.wait_ge(onehot, 3 * b)
                for g in range(2):
                    last = t.matmul(k.bank[0:GR, 0, g * L:(g + 1) * L], expand[:, bass.ds(at, 1), g].rearrange("p a b -> p (a b)"),
                                    rank[:, gb], start=True, stop=True)
                last.then_inc(rows, 1)

            def gather(b, x):
                pe.wait_ge(onehot, 3 * b + 3)
                pe.wait_ge(staged, b + 1)
                if exists(b - 1):
                    pe.wait_ge(qmask, b)
                for half in range(2):
                    last = t.matmul(k.bank[:, 1, 0:NR], qs[:, x % 2, half], oh[:, x % 2, half], start=(half == 0), stop=(half == 1))
                last.then_inc(gathered, 1)

            def score(b, x):
                if not exists(b):
                    return
                pe.wait_ge(qmask, b + 1)
                if exists(b - 1):
                    pe.wait_ge(expd, 2 * b)
                for g in range(2):
                    last = t.matmul(k.bank[0:GR, 2, g * L:(g + 1) * L], qm[:, x % 2, g * GR:(g + 1) * GR],
                                    kt_all[:, bass.ts(b, L)], start=True, stop=True)
                last.then_inc(scored, 1)

            def turn(b, x):
                if not exists(b):
                    return
                pe.wait_ge(normed, 2 * b + 2)
                if exists(b - 1):
                    pe.wait_ge(pt_ready, b)
                for half in range(2):
                    for g in range(2):
                        q = half * 2 + g
                        last = t.transpose(k.bank[0:HALF, 3, q * GR:(q + 1) * GR], prob[:, x % 2, g, half * HALF:(half + 1) * HALF],
                                           k.ident[0:GR, 0:GR])
                last.then_inc(turned, 1)

            def values(b, x):
                if not exists(b):
                    return
                pe.wait_ge(pt_ready, b + 1)
                if exists(b - 1):
                    pe.wait_ge(pv_masked, b)
                for g in range(2):
                    for half in range(2):
                        last = t.matmul(k.bank[0:GR, 4, g * 128:(g + 1) * 128], pt[:, x % 2, half * 2 + g],
                                        v_all[:, bass.ds(2 * b + half, 1), :].rearrange("p a b -> p (a b)"),
                                        start=(half == 0), stop=(half == 1))
                last.then_inc(pv_ready, 1)

            def scatter(b, x):
                if not exists(b):
                    return
                pe.wait_ge(pv_masked, b + 1)
                if exists(b - 1):
                    pe.wait_ge(ot_ready, b)
                for g in range(2):
                    last = t.matmul(k.bank[:, 5, 0:L], pv[:, x % 2, g], oht[:, x % U, g], start=(g == 0), stop=(g == 1))
                last.then_inc(scat, 1)

            def project(b, x):
                if not exists(b):
                    return
                pe.wait_ge(ot_ready, b + 1)
                if exists(b - 1):
                    pe.wait_ge(added, b)
                t.matmul(k.bank[:, 7, 0:L], w_o[:], ot[:, x % 2], start=True, stop=True).then_inc(proj, 1)

            def step(b, x, gb, at):
                rank_rows(b, x, gb, at)
                score(b - 1, x - 1)
                values(b - 2, x - 2)
                gather(b, x)
                project(b - 3, x - 3)
                turn(b - 1, x - 1)
                scatter(b - 2, x - 2)

            half_b = B // 2
            for x in range(U):
                step(x, x, 0, x)
            with pe.Fori(1, half_b // U) as i:
                for x in range(U):
                    step(U * i + x, x, 0, U * i + x)
            with pe.Fori(0, half_b // U) as i:
                for x in range(U):
                    step(U * i + (half_b + x), x, 1, U * i + x)
            for b in range(B, B + 3):
                score(b - 1, b - 1)
                values(b - 2, b - 2)
                project(b - 3, b - 3)
                turn(b - 1, b - 1)
                scatter(b - 2, b - 2)


PIECES = 4
PIECE = GE * HC * 128 // PIECES


def load_group(sp, k, g, wst, w_in, split, before):
    for m in range(2 * PIECES):
        src = k.a["e_w1"] if m < PIECES else k.a["e_w2"]
        if m + before >= 2:
            sp.wait_ge(split, before + m - 1)
        sp.dma_start(wst[:, m % 2, :], src[:, bass.ds(g * GE * HC * 128 + (m % PIECES) * PIECE, PIECE)]).then_inc(w_in[m % 2], 16)


def split_group(nc, pool, k, slot, wst, w_in, w_hi, before, high_before):
    for m in range(2 * PIECES):
        cols = slice((m % PIECES) * PIECE, (m % PIECES + 1) * PIECE)
        hi = k.weights[:, slot, 2 * (m // PIECES), cols]
        lo = k.weights[:, slot, 2 * (m // PIECES) + 1, cols]
        pool.wait_ge(w_in[m % 2], 8 * before + 16 * (m // 2 + 1))
        nc.gpsimd.tensor_copy(hi, wst[:, m % 2, :]).then_inc(w_hi, 1)
        pool.wait_ge(w_hi, high_before + m + 1)
        nc.gpsimd.tensor_tensor(lo, wst[:, m % 2, :], hi, ALU.subtract).then_inc(k.group_split, 1)


def second_mixture(nc, k):
    a = k.a
    with ExitStack() as ctx:
        def sb(name, shape, dt=F32):
            return ctx.enter_context(nc.sbuf_tensor(f"m1_{name}", shape, dt))

        def sem(name):
            return k.semaphore(f"m1_{name}")

        drop = E1 - TOP1
        TU = 8
        norm = Normed(nc, k, ctx, "m1")
        ut = norm.ut
        router = sb("router", [128, E1])
        rb = sb("rb", [HALF, E1])
        b1 = sb("b1", [128, E1, HC])
        b2 = sb("b2", [E1, 128])
        u_hi = sb("u_hi", [128, T], BF16)
        u_lo = sb("u_lo", [128, T], BF16)
        lg = sb("lg", [HALF, NT, E1])
        ex = k.hc[0:HALF, 0:NT * E1].rearrange("p (n e) -> p n e", n=NT)
        red = sb("red", [HALF, 5, NT])
        row = sb("row", [HALF, TU, E1 + 8])
        best = sb("best", [HALF, TU, 8])
        fin = sb("fin", [HALF, TU, E1 + 8])
        cat = sb("cat", [HALF, 2, 4, 2, E1])
        ct = sb("ct", [E1, 2, CH])
        comb = sb("comb", [128, T], F16)
        wst = sb("wst", [128, 2, PIECE])
        g = k.hc[:, 0:2 * BLK].rearrange("p (c n) -> p c n", c=2)
        hs = k.hc[:, 2 * BLK:4 * BLK].rearrange("p (c n) -> p c n", c=2)
        halves = k.hc[:, 4 * BLK:8 * BLK].bitcast(BF16).rearrange("p (m x c n) -> p m x c n", m=2, x=2, c=2)
        h_hi, h_lo = halves[:, 0], halves[:, 1]

        small_in = sem("small_in")
        u_high = sem("u_high")
        u_low = sem("u_low")
        logits = sem("logits")
        copied = sem("logits_copied")
        s = sem("routing_step")
        expd = sem("exp_ready")
        topk = sem("top_step")
        passed = sem("top_step_passed")
        kept = sem("kept")
        cat_ready = sem("cat_ready")
        turned = sem("comb_turned")
        c_high = sem("comb_high")
        c_low = sem("comb_low")
        bias = sem("bias_ready")
        bias_added = sem("bias_added")
        up = sem("up_ready")
        spread = sem("comb_spread")
        g_ready = sem("gelu_ready")
        scaled = sem("scaled")
        hi_ready = sem("hidden_high")
        low = sem("hidden_low")
        used = sem("hidden_used")
        y_ready = sem("y_ready")
        y_added = sem("y_added")
        w_in = [sem(f"w_in{p}") for p in range(2)]
        w_hi = sem("w_high")
        block = ctx.enter_context(nc.Block())

        def number(grp, tb, e):
            return (grp * NB + tb) * GE + e

        def two(ap):
            return ap.rearrange("p (a b) -> p a b", a=2)

        @block.sync
        def _(sp):
            for dst, src in ((router[:], a["router"]), (rb[:], a["router_b"].partition_broadcast(HALF)), (b1[:], a["e_b1"]),
                             (b2[:], a["e_b2"])):
                sp.dma_start(dst, src).then_inc(small_in, 16)
            for grp in range(1, NG):
                load_group(sp, k, grp, wst, w_in, k.group_split, 2 * PIECES * grp)

        @block.gpsimd
        def _(pool):
            with pool.Fori(0, NC // 2) as i:
                for j in range(2):
                    norm.pool_diagonal(pool, 2 * i + j, j)
            for grp in range(1, NG):
                if grp >= 2:
                    pool.wait_ge(y_ready, (grp - 1) * NB)
                split_group(nc, pool, k, grp % 2, wst, w_in, w_hi, 2 * PIECES * (grp - 1), 2 * PIECES * (grp - 1))

        @block.scalar
        def _(act):
            sc = nc.scalar
            with act.Fori(0, NC // 2) as i:
                for j in range(2):
                    act.wait_ge(norm.u_ready, 2 * i + j + 1)
                    sc.activation(u_hi[:, chunk(2 * i + j)], ut[:, j, :], ACT.Copy).then_inc(u_high, 1)
            act.wait_ge(s, 2)
            sc.activation(ex, lg[:], ACT.Exp).then_inc(expd, 1)
            act.wait_ge(s, 6)
            sc.activation(ex, ex, ACT.Exp).then_inc(expd, 1)
            with act.Fori(0, NC // 2) as i:
                for j in range(2):
                    c = 2 * i + j
                    act.wait_ge(turned, c + 1)
                    act.wait_ge(bias, 2 * i)
                    sc.activation(ct[:, j], k.bank[0:E1, j, 0:CH], ACT.Copy).then_inc(c_high, 1)
                    sc.activation(comb[:, chunk(c)], k.bank[:, j, 0:CH], ACT.Copy, scale=SCL).then_inc(c_high, 1)
            act.sem_inc(used, 2)
            act.wait_ge(c_low, NC)
            for grp in range(NG):
                with act.Fori(0, NB) as tb:
                    with act.Fori(0, GE // 2) as ee:
                        for x in range(2):
                            e = 2 * ee + x
                            it = number(grp, tb, e)
                            for c in range(HC):
                                act.wait_ge(up, 2 * it + c + 1)
                                act.wait_ge(scaled, 2 * it + c + 1)
                                sc.activation(two(g[:, c]), k.bank[:, 2 * c:2 * c + 2, 0:CH], ACT.Gelu,
                                              bias=b1[:, bass.ds(grp * GE + e, 1), c]).then_inc(g_ready, 1)
                            for c in range(HC):
                                act.wait_ge(scaled, 2 * it + c + 3)
                                act.wait_ge(used, it + 1)
                                sc.activation(h_hi[:, x, c], hs[:, c], ACT.Copy).then_inc(hi_ready, 1)

        @block.vector
        def _(dve):
            v = nc.vector
            norm.dve_start(dve)
            dve.wait_ge(small_in, 64)
            with dve.Fori(0, NC // 2) as i:
                dve.wait_ge(u_low, 2 * i)
                for j in range(2):
                    norm.dve_apply(dve, 2 * i + j, j)
                for j in range(2):
                    dve.wait_ge(u_high, 2 * i + j + 1)
                    v.tensor_tensor(u_lo[:, chunk(2 * i + j)], ut[:, j, :], u_hi[:, chunk(2 * i + j)],
                                    ALU.subtract).then_inc(u_low, 1)
                    dve.wait_ge(logits, 2 * i + j + 1)
                    v.tensor_tensor(lg[:, bass.ts(2 * i + j, 4), :],
                                    k.bank[0:HALF, 4 + j, 0:4 * E1].rearrange("p (n e) -> p n e", n=4),
                                    rb[:].unsqueeze(1).broadcast_to([HALF, 4, E1]), ALU.add).then_inc(copied, 1)
            dve.wait_ge(copied, NC)

            def wide(ap):
                return ap.unsqueeze(2).broadcast_to([HALF, NT, E1])

            v.tensor_reduce(red[:, 0], lg[:], X, ALU.max).then_inc(s, 1)
            dve.wait_ge(s, 1)
            v.tensor_tensor(lg[:], lg[:], wide(red[:, 0]), ALU.subtract).then_inc(s, 1)
            dve.wait_ge(expd, 1)
            v.tensor_reduce(red[:, 1], ex, X, ALU.add).then_inc(s, 1)
            dve.wait_ge(s, 3)
            v.reciprocal(red[:, 2], red[:, 1]).then_inc(s, 1)
            dve.wait_ge(s, 4)
            v.tensor_tensor(lg[:], ex, wide(red[:, 2]), ALU.mult).then_inc(s, 1)
            dve.wait_ge(s, 5)
            v.tensor_tensor(ex, lg[:], wide(red[:, 2]), ALU.subtract).then_inc(s, 1)
            v.memset(row[:], SENT).then_inc(s, 1)
            dve.wait_ge(s, 7)
            dve.wait_ge(expd, 2)
            n_top = [0]

            def link(last, per, i):
                n_top[0] += 1
                last.then_inc(topk, 1)
                dve.wait_ge(topk, i * per + n_top[0])
                dve.sem_inc(passed, 1)

            per = 2 + 2 * (drop // 8) + 2
            with dve.Fori(0, NT // TU) as i:
                dve.wait_ge(kept, TU * i)
                for j in range(TU):
                    last = v.tensor_scalar(row[:, j, 0:E1], lg[:, bass.ds(TU * i + j, 1), :].rearrange("p a b -> p (a b)"), -1.0, None, ALU.mult)
                link(last, per, i)
                for _r in range(drop // 8):
                    for j in range(TU):
                        last = v.max(best[:, j], row[:, j])
                    link(last, per, i)
                    for j in range(TU):
                        last = v.match_replace(row[:, j], best[:, j], row[:, j], MARK)
                    link(last, per, i)
                for j in range(TU):
                    last = v.max(best[:, j], row[:, j])
                link(last, per, i)
                link(v.memset(best[:, :, drop % 8:8], SENT), per, i)
                for j in range(TU):
                    last = v.match_replace(fin[:, j], best[:, j], row[:, j], MARK)
                link(last, per, i)
                for j in range(TU):
                    here = ex[:, bass.ds(TU * i + j, 1), :].rearrange("p a b -> p (a b)")
                    v.scalar_tensor_tensor(here, fin[:, j, 0:E1], CUT, here, ALU.is_gt, ALU.mult).then_inc(kept, 1)
            assert n_top[0] == per
            dve.wait_ge(kept, NT)
            v.tensor_reduce(red[:, 3], ex, X, ALU.add).then_inc(s, 1)
            dve.wait_ge(s, 8)
            v.reciprocal(red[:, 4], red[:, 3]).then_inc(s, 1)
            dve.wait_ge(s, 9)
            with dve.Fori(0, NC // 2) as i:
                for j in range(2):
                    c = 2 * i + j
                    dve.wait_ge(turned, 2 * i)
                    v.tensor_tensor(cat[:, j], ex[:, bass.ts(c, 4), :].unsqueeze(2).broadcast_to([HALF, 4, 2, E1]),
                                    red[:, 4, bass.ts(c, 4)].unsqueeze(2).unsqueeze(3).broadcast_to([HALF, 4, 2, E1]),
                                    ALU.mult).then_inc(cat_ready, 1)
                for j in range(2):
                    c = 2 * i + j
                    dve.wait_ge(c_high, 2 * c + 2)
                    lo = comb[E1:128, chunk(c)]
                    v.scalar_tensor_tensor(lo, k.bank[E1:128, j, 0:CH], SCL, lo, ALU.mult, ALU.subtract).then_inc(c_low, 1)
                    dve.wait_ge(bias, c + 1)
                    v.tensor_tensor(k.h[:, chunk(c)], k.h[:, chunk(c)], k.bank[:, 2 + j, 0:CH], ALU.add).then_inc(bias_added, 1)
            dve.sem_inc(scaled, 2)
            dve.sem_inc(low, 2)

            def expert(grp, tb, e, x):
                it = number(grp, tb, e)
                for c in range(HC):
                    dve.wait_ge(g_ready, 2 * it + c + 1)
                    dve.wait_ge(spread, it + 1)
                    dve.wait_ge(low, 2 * it + c + 1)
                    v.tensor_tensor(two(hs[:, c]), two(g[:, c]), k.bank[:, 4:6, 0:CH], ALU.mult).then_inc(scaled, 1)
                for c in range(HC):
                    dve.wait_ge(hi_ready, 2 * it + c + 1)
                    v.tensor_tensor(h_lo[:, x, c], hs[:, c], h_hi[:, x, c], ALU.subtract).then_inc(low, 1)

            def add(nth, tb):
                dve.wait_ge(y_ready, nth + 1)
                v.tensor_tensor(two(k.h[:, bass.ds(tb * BLK, BLK)]), two(k.h[:, bass.ds(tb * BLK, BLK)]), k.bank[:, 6:8, 0:CH],
                                ALU.add).then_inc(y_added, 1)

            def rest(grp, tb):
                expert(grp, tb, 1, 1)
                with dve.Fori(1, GE // 2) as ee:
                    for x in range(2):
                        expert(grp, tb, 2 * ee + x, x)

            for grp in range(NG):
                expert(grp, 0, 0, 0)
                if grp:
                    add(grp * NB - 1, NB - 1)
                rest(grp, 0)
                with dve.Fori(1, NB) as tb:
                    expert(grp, tb, 0, 0)
                    add(grp * NB + tb - 1, tb - 1)
                    rest(grp, tb)
            add(NG * NB - 1, NB - 1)

        @block.tensor
        def _(pe):
            t = nc.tensor
            pe.wait_ge(small_in, 64)
            with pe.Fori(0, NC // 2) as i:
                for j in range(2):
                    norm.pe_spread(pe, 2 * i + j, j)
                for j in range(2):
                    pe.wait_ge(norm.u_ready, 2 * i + j + 1)
                    pe.wait_ge(copied, 2 * i)
                    for q in range(4):
                        last = t.matmul(k.bank[0:HALF, 4 + j, q * E1:(q + 1) * E1], ut[:, j, q * HALF:(q + 1) * HALF],
                                        router[:], start=True, stop=True)
                    last.then_inc(logits, 1)
            with pe.Fori(0, NC // 2) as i:
                for j in range(2):
                    c = 2 * i + j
                    pe.wait_ge(cat_ready, c + 1)
                    pe.wait_ge(c_low, 2 * i)
                    for q in range(4):
                        last = t.transpose(k.bank[:, j, q * HALF:(q + 1) * HALF], cat[:, j, q].rearrange("p a b -> p (a b)"),
                                           k.ident[0:HALF, 0:HALF])
                    last.then_inc(turned, 1)
                for j in range(2):
                    c = 2 * i + j
                    pe.wait_ge(c_high, 2 * c + 1)
                    pe.wait_ge(bias_added, 2 * i)
                    t.matmul(k.bank[:, 2 + j, 0:CH], b2[:], ct[:, j], start=True, stop=True).then_inc(bias, 1)
            pe.wait_ge(bias_added, NC)
            pe.wait_ge(c_low, NC)

            def front(grp, tb, e, first=False):
                it = number(grp, tb, e)
                for c in range(HC):
                    if not first:
                        pe.wait_ge(g_ready, 2 * it + c - 1)
                    at = bass.ds((e * HC + c) * 128, 128)
                    w = [k.weights[:, grp % 2, m, at] for m in range(2)]
                    for m, (ww, uu) in enumerate(((w[0], u_hi), (w[0], u_lo), (w[1], u_hi))):
                        for q in range(2):
                            last = t.matmul(k.bank[:, 2 * c + q, 0:CH], ww, uu[:, bass.ds(tb * BLK + q * CH, CH)],
                                            start=(m == 0), stop=(m == 2))
                    last.then_inc(up, 1)
                if not first:
                    pe.wait_ge(scaled, 2 * it + 2)
                for q in range(2):
                    last = t.matmul(k.bank[:, 4 + q, 0:CH], k.sel[:, bass.ds(grp * GE + e, 1), :].rearrange("p a b -> p (a b)"),
                                    comb[:, bass.ds(tb * BLK + q * CH, CH)], start=True, stop=True)
                last.then_inc(spread, 1)

            def back(grp, tb, e, x, start=False, stop=False):
                it = number(grp, tb, e)
                for c in range(HC):
                    at = bass.ds((e * HC + c) * 128, 128)
                    w = [k.weights[:, grp % 2, 2 + m, at] for m in range(2)]
                    pe.wait_ge(hi_ready, 2 * it + c + 1)
                    for m, (ww, hh) in enumerate(((w[0], h_hi), (w[1], h_hi), (w[0], h_lo))):
                        if m == 2:
                            pe.wait_ge(low, 2 * it + c + 3)
                        for q in range(2):
                            last = t.matmul(k.bank[:, 6 + q, 0:CH], ww, hh[:, x, c, q * CH:(q + 1) * CH],
                                            start=(start and c == 0 and m == 0), stop=(stop and c == HC - 1 and m == 2))
                    if c == 0:
                        continue
                    last.then_inc(used, 1)
                    if stop:
                        pe.wait_ge(used, it + 3)
                        pe.sem_inc(y_ready, 1)

            def block_of_tokens(grp, tb, after, first=False):
                front(grp, tb, 1)
                if not first:
                    pe.wait_ge(y_added, grp * NB + tb)
                back(grp, tb, 0, 0, start=True)
                with pe.Fori(0, GE // 2 - 1) as ee:
                    for x in (1, 2):
                        front(grp, tb, 2 * ee + x + 1)
                        back(grp, tb, 2 * ee + x, x % 2)
                if after:
                    front(*after, 0)
                back(grp, tb, GE - 1, 1, stop=True)

            pe.wait_ge(k.group_split, 2 * PIECES)
            for grp in range(NG):
                if grp == 0:
                    front(0, 0, 0, first=True)
                    block_of_tokens(grp, 0, (grp, 1), first=True)
                with pe.Fori(0 if grp else 1, NB - 1) as tb:
                    block_of_tokens(grp, tb, (grp, tb + 1))
                if grp + 1 < NG:
                    pe.wait_ge(k.group_split, 2 * PIECES * (grp + 2))
                    block_of_tokens(grp, NB - 1, (grp + 1, 0))
                else:
                    block_of_tokens(grp, NB - 1, None)


def store(nc, k, out):
    with ExitStack() as ctx:
        stored = k.semaphore("result_stored")
        block = ctx.enter_context(nc.Block())

        @block.sync
        def _(sp):
            for p in range(4):
                cols = slice(p * T // 4, (p + 1) * T // 4)
                sp.dma_start(out[:, cols], k.h[:, cols]).then_inc(stored, 16)
            sp.wait_ge(stored, 64)


def audio_tower(nc, a, out):
    k = Kernel()
    k.a = a
    with ExitStack() as ctx:
        def sb(name, shape, dt=F32):
            return ctx.enter_context(nc.sbuf_tensor(name, shape, dt))

        k.semaphore = lambda name: ctx.enter_context(nc.semaphore(name))
        k.bank = ctx.enter_context(nc.psum_tensor("bank", [128, 8, 512], F32))
        k.h = sb("h", [128, T])
        k.hc = sb("hc", [128, T])
        k.rstd = sb("rstd", [128, NT])
        k.ident = sb("ident", [128, 128])
        k.mean_w = sb("mean_w", [128, 128])
        k.ones = sb("ones", [128, 128])
        k.eps = sb("eps", [128, 1])
        k.hm = sb("hm", [128, NH])
        k.sel = sb("sel", [128, E1, 128], F16)
        k.weights = sb("weights", [128, 2, 4, GE * HC * 128], BF16)
        k.w0_split = k.semaphore("w0_split")
        k.w2_in = k.semaphore("w0_down_in")
        k.group_split = k.semaphore("expert_group_split")
        stages = [
            lambda: constants_and_tokens(nc, k, a["x"], a["w_tok"], a["bias"]),
            lambda: (norm_statistics(nc, k, "n1"), recurrence(nc, k)),
            lambda: (norm_statistics(nc, k, "n2"), first_mixture(nc, k)),
            lambda: (norm_statistics(nc, k, "n3"), sparse_attention(nc, k)),
            lambda: (norm_statistics(nc, k, "n4"), second_mixture(nc, k)),
        ]
        for stage in stages:
            stage()
        store(nc, k, out)


def kernel(**i):
    import numpy as np
    import concourse.bacc as bacc
    from concourse.bass_utils import run_bass_kernel_spmd

    def two(v):
        return v.reshape(2, 128).T

    lay = {
        "x": i["x"][:, :3 * L].reshape(B * L, 2, KT).transpose(2, 1, 0),
        "w_tok": i["L0_tok_weight"].T.reshape(2, KT, D).transpose(1, 0, 2),
        "bias": i["L0_tok_bias"].reshape(D, 1),
        "theta": two(i["L0_attn_theta_log"]),
        "nu": two(i["L0_attn_nu_log"]),
        "gamma": two(i["L0_attn_gamma_log"]),
        "b_re": i["L0_attn_B_re"].T,
        "b_im": i["L0_attn_B_im"].T,
        "c_re": i["L0_attn_C_re"].T.reshape(2, 128, D).transpose(1, 0, 2),
        "c_im": i["L0_attn_C_im"].T.reshape(2, 128, D).transpose(1, 0, 2),
        "d": i["L0_attn_D"].T,
        "gate": i["L0_ffn_gate_weight"].T,
        "w1": i["L0_ffn_w1"].transpose(2, 0, 1).reshape(D, E0 * FF0),
        "w2": i["L0_ffn_w2"].reshape(E0, D, FC, 128).transpose(3, 0, 2, 1),
        "wq": i["L1_attn_Wq"], "wk": i["L1_attn_Wk"], "wv": i["L1_attn_Wv"], "wo": i["L1_attn_Wo"],
        "idx": i["L1_attn_idx_sample"].reshape(1, NS),
        "e_w1": i["L1_ffn_w1"][::-1].transpose(1, 0, 2).reshape(D, E1 * FF1),
        "e_b1": i["L1_ffn_b1"][::-1].reshape(E1, HC, 128).transpose(2, 0, 1),
        "e_w2": i["L1_ffn_w2"][::-1].reshape(E1, HC, 128, D).transpose(2, 0, 1, 3).reshape(128, E1 * HC * D),
        "e_b2": i["L1_ffn_b2"][::-1],
        "router": i["L1_ffn_router_w"][:, ::-1],
        "router_b": i["L1_ffn_router_b"][::-1].reshape(1, E1),
    }
    nc = bacc.Bacc("TRN2", target_bir_lowering=False, num_devices=1)
    arrays, args = {}, {}
    for name, v in lay.items():
        arrays[f"{name}_dram"] = v = np.ascontiguousarray(v)
        args[name] = nc.dram_tensor(f"{name}_dram", v.shape, mybir.dt.from_np(v.dtype), kind="ExternalInput").ap()
    out = nc.dram_tensor("out_dram", (D, T), F32, kind="ExternalOutput").ap()
    audio_tower(nc, args, out)
    r = run_bass_kernel_spmd(nc, [arrays], core_ids=[0])
    return r.results[0]["out_dram"].reshape(D, B, L).transpose(1, 2, 0)
```

```python
from contextlib import ExitStack

import concourse.bass as bass
from concourse import mybir

ALU = mybir.AluOpType
ACT = mybir.ActivationFunctionType
X = mybir.AxisListType.X
F32 = mybir.dt.float32
F16 = mybir.dt.float16
BF16 = mybir.dt.bfloat16
I32 = mybir.dt.int32

B, L, D = 32, 166, 128
T = B * L
HALF = L // 2
NT = 2 * B
CH = 2 * L
NC = T // CH
BLK = 2 * CH
NB = T // BLK
KT = 96
HID = 256
E0, FF0 = 16, 512
FC = FF0 // 128
E1, FF1, TOP1 = 64, 256, 42
HC = FF1 // 128
NH, DH = 8, 16
NS = 38
NU = 25
HG = 4
GE, NG = 16, 4
SENT = -2.0e38
MARK = -3.0e38
CUT = -2.5e38
WARM = 8
EPS = 1e-5
SCL = 256.0
ROUND = 12582912.0
LOG2E = 1.4426950408889634
LN2_HI, LN2_LO = 0.693359375, -2.12194440e-4
INV2PI = 0.15915494309189535
PI2_A, PI2_B = 6.28125, 0.0019350051879882812
PI2_C = 6.283185307179586 - 6.28125 - 0.0019350051879882812


def chunk(c):
    return bass.ts(c, CH)


class Kernel:
    pass


def load_table(nc, k, n, function):
    nc.scalar.activation(k.cells[:, n + 1:n + 2], k.cells[:, 0:1], function)


def warm_up(nc, k):
    for _ in range(WARM):
        nc.tensor.matmul(k.bank[:, 7, :], k.sel[:, 0, :], k.sel[:, 0:4, :].rearrange("p a b -> p (a b)"), start=True, stop=True)


TABLE_ANGLE = 60


class RecurrenceTables:

    def __init__(self, nc, k, ctx):
        def sb(name, shape, dt=F32):
            return ctx.enter_context(nc.sbuf_tensor(f"lru_{name}", shape, dt))

        self.nc, self.k = nc, k
        self.par = sb("par", [128, 3, 2])
        self.w_b = sb("w_b", [128, 2, HID])
        self.w_c = sb("w_c", [128, 3, 2, 128])
        self.w_cr = sb("w_cr", [128, 2, 2, 128])
        self.w_d = sb("w_d", [128, 128])
        self.ex = sb("ex", [128, 7, 4])
        self.bits = sb("bits", [128, 4], I32)
        self.mag = sb("mag", [128, 4])
        self.ph = sb("ph", [128, 5, 2])
        self.time = sb("time", [128, L])
        self.ang = sb("ang", [128, 4, 2, L])
        self.rot = sb("rot", [128, 4, 2, CH])
        self.decay = sb("decay", [128, 2, CH])
        self.par_in = k.semaphore("lru_par_in")
        self.w_in = k.semaphore("lru_w_in")
        self.time_made = k.semaphore("lru_time_made")
        self.step = k.semaphore("lru_table_step")
        self.sine = k.semaphore("lru_sine")
        self.done = k.semaphore("lru_tables_ready")

    def sync_parameters(self, sp):
        for q, name in enumerate(("theta", "nu", "gamma")):
            sp.dma_start(self.par[:, q, :], self.k.a[name]).then_inc(self.par_in, 16)

    def sync_weights(self, sp):
        for dst, name in ((self.w_cr[:, 0], "c_re"), (self.w_cr[:, 1], "c_im"), (self.w_b[:, 0, :], "b_re"),
                          (self.w_b[:, 1, :], "b_im"), (self.w_d[:], "d")):
            sp.dma_start(dst, self.k.a[name]).then_inc(self.w_in, 16)

    def pool_time(self):
        self.nc.gpsimd.iota(self.time[:], [[1, L]], base=1, channel_multiplier=0,
                            allow_small_or_imprecise_dtypes=True).then_inc(self.time_made, 1)

    def act_sines(self, act):
        act.wait_ge(self.step, TABLE_ANGLE)
        self.nc.scalar.activation(self.ang[:, 1], self.ang[:, 0], ACT.Sin).then_inc(self.sine, 1)
        self.nc.scalar.activation(self.ang[:, 2], self.ang[:, 0], ACT.Sin, scale=0.5).then_inc(self.sine, 1)

    def dve_tables(self, dve):
        par, w_c, w_cr, ex, bits, mag, ph = self.par, self.w_c, self.w_cr, self.ex, self.bits, self.mag, self.ph
        time, ang, rot, decay = self.time, self.ang, self.rot, self.decay
        n = [0]
        v = self.nc.vector

        def step(ins):
            n[0] += 1
            ins.then_inc(self.step, 1)
            dve.wait_ge(self.step, n[0])

        def exponential(out, x, cols):
            w = [ex[:, m, 0:cols] for m in range(7)]
            step(v.tensor_scalar(w[6], x, -87.0, 87.0, ALU.max, ALU.min))
            step(v.tensor_scalar(w[0], w[6], LOG2E, ROUND, ALU.mult, ALU.add))
            step(v.tensor_scalar(w[1], w[0], ROUND, None, ALU.subtract))
            step(v.scalar_tensor_tensor(w[2], w[1], -LN2_HI, w[6], ALU.mult, ALU.add))
            step(v.scalar_tensor_tensor(w[3], w[1], -LN2_LO, w[2], ALU.mult, ALU.add))
            step(v.tensor_scalar(w[4], w[3], 1.0 / 5040, None, ALU.mult))
            src, dst = w[4], w[5]
            for c in (1.0 / 720, 1.0 / 120, 1.0 / 24, 1.0 / 6, 0.5, 1.0):
                step(v.scalar_tensor_tensor(dst, src, c, w[3], ALU.add, ALU.mult))
                src, dst = dst, src
            step(v.tensor_scalar(w[0], w[1], 127.0, 8388608.0, ALU.add, ALU.mult))
            step(v.tensor_copy(bits[:, 0:cols], w[0]))
            step(v.scalar_tensor_tensor(out, src, 1.0, bits[:, 0:cols].bitcast(F32), ALU.add, ALU.mult))

        def wrapped(x, work, turns):
            step(v.tensor_scalar(work, turns, INV2PI, ROUND, ALU.mult, ALU.add))
            step(v.tensor_scalar(work, work, ROUND, None, ALU.subtract))
            for part in (PI2_A, PI2_B, PI2_C):
                step(v.scalar_tensor_tensor(x, work, -part, x, ALU.mult, ALU.add))

        dve.wait_ge(self.par_in, 48)
        both = par[:, 0:2, :].rearrange("p a b -> p (a b)")
        exponential(mag[:], both, 4)
        step(v.tensor_scalar(ph[:, 0], mag[:, 2:4], -1.0, None, ALU.mult))
        exponential(mag[:, 2:4], ph[:, 0], 2)
        step(v.tensor_copy(ph[:, 1], mag[:, 0:2]))
        wrapped(ph[:, 1], ph[:, 2], ph[:, 1])
        step(v.tensor_scalar(ph[:, 2], ph[:, 1], ROUND / 1024, None, ALU.add))
        step(v.tensor_scalar(ph[:, 3], ph[:, 2], ROUND / 1024, None, ALU.subtract))
        step(v.tensor_tensor(ph[:, 4], ph[:, 1], ph[:, 3], ALU.subtract))
        dve.wait_ge(self.time_made, 1)
        for p in range(2):
            step(v.tensor_scalar(ang[:, 0, p], time[:], ph[:, 3, p:p + 1], None, ALU.mult))
            step(v.tensor_scalar(ang[:, 1, p], time[:], ph[:, 4, p:p + 1], None, ALU.mult))
            step(v.tensor_tensor(ang[:, 2, p], ang[:, 0, p], ang[:, 1, p], ALU.add))
            wrapped(ang[:, 0, p], ang[:, 3, p], ang[:, 2, p])
            step(v.tensor_tensor(ang[:, 0, p], ang[:, 0, p], ang[:, 1, p], ALU.add))
            step(v.tensor_scalar(ang[:, 0, p], ang[:, 0, p], 3.1415925, -3.1415925, ALU.min, ALU.max))
        assert n[0] == TABLE_ANGLE, n[0]
        dve.wait_ge(self.w_in, 80)
        for p in range(2):
            v.tensor_scalar(w_c[:, 1, p], w_cr[:, 1, p], -1.0, None, ALU.mult)
            v.tensor_scalar(w_c[:, 2, p], w_cr[:, 0, p], -1.0, None, ALU.mult)
            step(v.tensor_copy(w_c[:, 0, p], w_cr[:, 0, p]))
        dve.wait_ge(self.sine, 2)
        step(v.tensor_tensor(ang[:, 3], ang[:, 2], ang[:, 2], ALU.mult))
        step(v.tensor_scalar(ang[:, 2], ang[:, 3], -2.0, 1.0, ALU.mult, ALU.add))
        for p in range(2):
            for q in range(2):
                cols = slice(q * L, (q + 1) * L)
                v.tensor_copy(rot[:, 0, p, cols], ang[:, 2, p])
                v.tensor_copy(rot[:, 1, p, cols], ang[:, 1, p])
                v.tensor_scalar(rot[:, 2, p, cols], ang[:, 2, p], par[:, 2, p:p + 1], None, ALU.mult)
                v.tensor_scalar(rot[:, 3, p, cols], ang[:, 1, p], par[:, 2, p:p + 1], None, ALU.mult)
                step(v.tensor_scalar(decay[:, p, cols], time[:], 0.0, mag[:, 2 + p:3 + p], ALU.mult, ALU.add))
                step(v.memset(decay[:, p, q * L:q * L + 1], 0.0))
        dve.sem_inc(self.done, 1)


def constants_and_tokens(nc, k, x, w_tok, bias, tables):
    with ExitStack() as ctx:
        xs = ctx.enter_context(nc.sbuf_tensor("xs", [KT, 2, T], F32))
        wt = ctx.enter_context(nc.sbuf_tensor("wt", [KT, 2, D], F32))
        bs = ctx.enter_context(nc.sbuf_tensor("bs", [128, 1], F32))
        parts = 4
        per = NC // parts
        w_in = k.semaphore("tok_w_in")
        x_in = [k.semaphore(f"tok_x_in{p}") for p in range(parts)]
        prod = k.semaphore("tok_product_ready")
        h_ready = k.semaphore("tok_bank_read")
        blank = k.semaphore("const_blank")
        made = k.semaphore("const_made")
        block = ctx.enter_context(nc.Block())

        @block.sync
        def _(sp):
            tables.sync_parameters(sp)
            sp.dma_start(wt[:], w_tok).then_inc(w_in, 16)
            sp.dma_start(bs[:], bias).then_inc(w_in, 16)
            for p in range(parts):
                cols = slice(p * per * CH, (p + 1) * per * CH)
                sp.dma_start(xs[:, :, cols], x[:, :, cols]).then_inc(x_in[p], 16)
            tables.sync_weights(sp)

        @block.gpsimd
        def _(pool):
            g = nc.gpsimd
            tables.pool_time()
            g.memset(k.ident[:], 0.0).then_inc(blank, 1)
            g.memset(k.sel[:], 0.0).then_inc(blank, 1)
            g.memset(k.hm[:], 1.0).then_inc(blank, 1)
            g.memset(k.mean_w[:], 1.0 / D).then_inc(made, 1)
            g.memset(k.ones[:], 1.0).then_inc(made, 1)
            g.memset(k.rstd[:], 0.0).then_inc(made, 1)
            g.memset(k.cells[:], 0.0).then_inc(made, 1)
            pool.wait_ge(blank, 3)
            g.affine_select(out=k.ident[:], in_=k.ident[:], compare_op=ALU.not_equal, fill=1.0, base=0,
                            pattern=[[-1, 128]], channel_multiplier=1).then_inc(made, 1)
            g.affine_select(out=k.sel[:], in_=k.sel[:], compare_op=ALU.not_equal, fill=1.0 / SCL, base=0,
                            pattern=[[-1, E1], [0, 128]], channel_multiplier=1).then_inc(blank, 1)
            g.affine_select(out=k.hm[:], in_=k.hm[:], compare_op=ALU.is_ge, fill=0.0, base=0,
                            pattern=[[-DH, NH]], channel_multiplier=1).then_inc(blank, 1)
            pool.wait_ge(blank, 5)
            g.affine_select(out=k.sel[:], in_=k.sel[:], compare_op=ALU.not_equal, fill=1.0 / SCL, base=-E1,
                            pattern=[[-1, E1], [0, 128]], channel_multiplier=1).then_inc(made, 1)
            g.affine_select(out=k.hm[:], in_=k.hm[:], compare_op=ALU.is_ge, fill=0.0, base=DH - 1,
                            pattern=[[DH, NH]], channel_multiplier=-1).then_inc(made, 1)

        @block.tensor
        def _(pe):
            pe.wait_ge(w_in, 32)
            for p in range(parts):
                pe.wait_ge(x_in[p], 16)
                for cc in range(per):
                    c = p * per + cc
                    if c >= 4:
                        pe.wait_ge(h_ready, c - 3)
                    for q in range(2):
                        last = nc.tensor.matmul(k.bank[:, c % 4, 0:CH], wt[:, q, :], xs[:, q, c * CH:(c + 1) * CH],
                                                start=(q == 0), stop=(q == 1))
                    last.then_inc(prod, 1)

        @block.vector
        def _(dve):
            tables.dve_tables(dve)

        @block.scalar
        def _(act):
            act.wait_ge(w_in, 32)
            for c in range(NC):
                act.wait_ge(prod, c + 1)
                nc.scalar.activation(k.h[:, c * CH:(c + 1) * CH], k.bank[:, c % 4, 0:CH], ACT.Identity,
                                     bias=bs[:]).then_inc(h_ready, 1)
                if c == NC // 2:
                    tables.act_sines(act)


DEEP, AHEAD = 4, 3


def norm_statistics(nc, k, name, table):
    with ExitStack() as ctx:
        sq = ctx.enter_context(nc.sbuf_tensor(f"{name}_sq", [128, DEEP, CH], F32))
        st = ctx.enter_context(nc.sbuf_tensor(f"{name}_st", [HALF, 4, NT], F32))
        mean = k.semaphore(f"{name}_mean")
        centred = k.semaphore(f"{name}_centred")
        squared = k.semaphore(f"{name}_squared")
        var = k.semaphore(f"{name}_variance")
        root = k.semaphore(f"{name}_root")
        step = k.semaphore(f"{name}_step")
        block = ctx.enter_context(nc.Block())
        v = k.bank[0:HALF, DEEP, 0:NT]

        def chunks(eng, work):
            with eng.Fori(0, NC // DEEP - 1) as i:
                for j in range(DEEP):
                    work(DEEP * i + j, j)
            for c in range(NC - DEEP, NC):
                work(c, c % DEEP)

        @block.tensor
        def _(pe):
            pe.sem_inc(var, DEEP)

            def means(c, j):
                pe.wait_ge(centred, c + 1)
                nc.tensor.matmul(k.bank[:, j, 0:CH], k.mean_w[:], k.h[:, chunk(c)], start=True, stop=True).then_inc(mean, 1)

            def work(c, j):
                if not isinstance(c, int) or c + AHEAD < NC:
                    means(c + AHEAD, (j + AHEAD) % DEEP)
                pe.wait_ge(squared, c + 1)
                for q in range(4):
                    last = nc.tensor.matmul(k.bank[0:HALF, DEEP, bass.ds(c * 4 + q, 1)],
                                            sq[:, j, q * HALF:(q + 1) * HALF], k.mean_w[:, 0:1], start=True, stop=True)
                last.then_inc(var, 1)

            for c in range(AHEAD):
                means(c, c)
            chunks(pe, work)

        @block.vector
        def _(dve):
            dve.sem_inc(centred, DEEP)
            with dve.Fori(0, NC // DEEP) as i:
                for j in range(DEEP):
                    dve.wait_ge(mean, DEEP * i + j + 1)
                    nc.vector.tensor_tensor(k.hc[:, chunk(DEEP * i + j)], k.h[:, chunk(DEEP * i + j)], k.bank[:, j, 0:CH],
                                            ALU.subtract).then_inc(centred, 1)
            dve.wait_ge(var, NC + DEEP)
            nc.vector.tensor_scalar(st[:, 0], v, EPS, None, ALU.add).then_inc(step, 1)
            dve.wait_ge(root, 1)
            nc.vector.reciprocal(st[:, 2], st[:, 1]).then_inc(step, 1)
            dve.wait_ge(step, 2)
            nc.vector.tensor_tensor(st[:, 3], st[:, 2], st[:, 2], ALU.mult).then_inc(step, 1)
            dve.wait_ge(step, 3)
            nc.vector.tensor_tensor(st[:, 1], st[:, 3], st[:, 0], ALU.mult).then_inc(step, 1)
            dve.wait_ge(step, 4)
            nc.vector.tensor_scalar(st[:, 3], st[:, 1], -0.5, 1.5, ALU.mult, ALU.add).then_inc(step, 1)
            dve.wait_ge(step, 5)
            nc.vector.tensor_tensor(k.rstd[0:HALF, 0:NT], st[:, 2], st[:, 3], ALU.mult).then_inc(step, 1)

        @block.scalar
        def _(act):
            load_table(nc, k, table, ACT.Sqrt)
            with act.Fori(0, NC // DEEP) as i:
                for j in range(DEEP):
                    act.wait_ge(centred, DEEP * i + j + DEEP + 1)
                    act.wait_ge(var, DEEP * i + j + 1)
                    nc.scalar.activation(sq[:, j, :], k.hc[:, chunk(DEEP * i + j)], ACT.Square).then_inc(squared, 1)
            act.wait_ge(step, 1)
            nc.scalar.activation(st[:, 1], st[:, 0], ACT.Sqrt).then_inc(root, 1)


def recurrence(nc, k, tables):
    a = k.a
    with ExitStack() as ctx:
        def sb(name, shape, dt=F32):
            return ctx.enter_context(nc.sbuf_tensor(f"lru_{name}", shape, dt))

        def sem(name):
            return k.semaphore(f"lru_{name}")

        w_b, w_c, w_d, rot, decay = tables.w_b, tables.w_c, tables.w_d, tables.rot, tables.decay
        diag = sb("diag", [128, 2, 4, HALF])
        ut = sb("ut", [128, 2, CH])
        va = sb("va", [128, 2, CH])
        vb = sb("vb", [128, 2, CH])
        gs = sb("gs", [128, 2, CH])
        xc = sb("xc", [128, 2, 2, CH])
        xsn = sb("xs", [128, 2, 2, CH])
        ysb = sb("ysb", [128, 2, CH])
        piece = E0 * FF0 // NC
        wst = sb("wst", [128, 2, piece])

        diag_ready = sem("diag_ready")
        spread = sem("rstd_spread")
        u_ready = sem("u_ready")
        bu = sem("bu_ready")
        turned = sem("bu_turned")
        joined = sem("turned_joined")
        scanned = sem("scanned")
        back = sem("turned_back")
        y_half = sem("y_half")
        y_ready = sem("y_ready")
        y_copied = sem("y_copied")
        y_added = sem("y_added")
        w_in = [sem(f"w0_in{p}") for p in range(2)]
        w_hi = sem("w0_high")
        block = ctx.enter_context(nc.Block())

        def exists(c):
            return not isinstance(c, int) or 0 <= c < NC

        def chunks(eng, work):
            for c in range(2):
                work(c, c)
            with eng.Fori(1, NC // 2 - 1) as i:
                for j in range(2):
                    work(2 * i + j, j)
            for c in range(NC - 2, NC):
                work(c, c % 2)

        w0 = k.weights[:, 0].rearrange("p a b -> p (a b)")
        w0_hi, w0_lo = w0[:, 0:E0 * FF0], w0[:, E0 * FF0:]
        k.w0_down = k.weights[:, 1].bitcast(F32).rearrange("p a b -> p (a b)")

        @block.sync
        def _(sp):
            for p in range(NC):
                if p >= 2:
                    sp.wait_ge(k.w0_split, p - 1)
                sp.dma_start(wst[:, p % 2, :], a["w1"][:, p * piece:(p + 1) * piece]).then_inc(w_in[p % 2], 16)
            sp.dma_start(k.w0_down, a["w2"].rearrange("p e f d -> p (e f d)")).then_inc(k.w2_in, 16)

        @block.gpsimd
        def _(pool):
            g = nc.gpsimd
            def diagonal(c, j):
                pool.wait_ge(spread, c + 1)
                g.tensor_tensor(diag[:, j], k.ident[:, 0:HALF].unsqueeze(1).broadcast_to([128, 4, HALF]),
                                k.rstd[:, bass.ts(c, 4)].unsqueeze(2).broadcast_to([128, 4, HALF]),
                                ALU.mult).then_inc(diag_ready, 1)

            def work(c, j):
                if exists(c + 2):
                    diagonal(c + 2, j)
                cols = bass.ts(c, piece)
                pool.wait_ge(w_in[j], 8 * c + (16 - 8 * j))
                g.tensor_copy(w0_hi[:, cols], wst[:, j, :]).then_inc(w_hi, 1)
                pool.wait_ge(w_hi, c + 1)
                g.tensor_tensor(w0_lo[:, cols], wst[:, j, :], w0_hi[:, cols], ALU.subtract).then_inc(k.w0_split, 1)
                pool.wait_ge(y_copied, c + 3)
                g.tensor_tensor(k.h[:, chunk(c)], k.h[:, chunk(c)], ysb[:, j, :], ALU.add).then_inc(y_added, 1)

            for j in range(2):
                diagonal(j, j)
            chunks(pool, work)

        @block.scalar
        def _(act):
            act.sem_inc(y_copied, 2)
            act.sem_inc(y_added, 2)
            with act.Fori(0, NC // 2) as i:
                for j in range(2):
                    act.wait_ge(y_ready, 2 * i + j + 1)
                    act.wait_ge(y_added, 2 * i + j + 1)
                    nc.scalar.activation(ysb[:, j, :], k.bank[:, 6 + j, 0:CH], ACT.Copy).then_inc(y_copied, 1)

        @block.vector
        def _(dve):
            v = nc.vector
            dve.sem_inc(spread, 2)
            dve.wait_ge(tables.done, 1)

            def tab(m, p):
                return rot[:, m, p].unsqueeze(1).broadcast_to([128, 2, CH])

            def normed(c, j):
                if exists(c - 2):
                    dve.wait_ge(y_ready, c - 1)
                dve.wait_ge(spread, c + 3)
                v.tensor_tensor(ut[:, j, :], k.hc[:, chunk(c)], k.bank[:, j, 0:CH], ALU.mult).then_inc(u_ready, 1)

            def state(c, p):
                m = 2 * c + p
                pair = k.bank[:, 2 + 2 * p:4 + 2 * p, 0:CH]
                dve.wait_ge(bu, m + 1)
                if p or exists(c - 1):
                    dve.wait_ge(scanned, 2 * m)
                v.tensor_tensor(va[:], pair, tab(2, p), ALU.mult).then_inc(turned, 1)
                v.tensor_tensor(vb[:], pair, tab(3, p), ALU.mult).then_inc(turned, 1)
                dve.wait_ge(turned, 2 * m + 2)
                v.tensor_tensor(va[:, 0], va[:, 0], vb[:, 1], ALU.add).then_inc(joined, 1)
                v.tensor_tensor(va[:, 1], va[:, 1], vb[:, 0], ALU.subtract).then_inc(joined, 1)
                dve.wait_ge(joined, 2 * m + 2)
                if p or exists(c - 1):
                    dve.wait_ge(back, 2 * m)
                for q in range(2):
                    v.tensor_tensor_scan(gs[:, q], decay[:, p], va[:, q], 0.0, ALU.mult, ALU.add).then_inc(scanned, 1)
                dve.wait_ge(scanned, 2 * m + 2)
                if exists(c - 1):
                    dve.wait_ge(y_half if p == 0 else y_ready, c)
                v.tensor_tensor(xc[:, p], gs[:], tab(0, p), ALU.mult).then_inc(back, 1)
                v.tensor_tensor(xsn[:, p], gs[:], tab(1, p), ALU.mult).then_inc(back, 1)

            def work(c, j):
                state(c, 0)
                if exists(c + 1):
                    normed(c + 1, 1 - j)
                state(c, 1)

            normed(0, 0)
            chunks(dve, work)

        @block.tensor
        def _(pe):
            pe.wait_ge(tables.w_in, 80)
            pe.wait_ge(tables.done, 1)

            def spread_rstd(c, j):
                pe.wait_ge(diag_ready, c + 1)
                nc.tensor.matmul(k.bank[:, j, 0:CH], k.ones[:], diag[:, j].rearrange("p a b -> p (a b)"),
                                 start=True, stop=True).then_inc(spread, 1)

            def inputs(c, j, p):
                pe.wait_ge(u_ready, c + 1)
                if exists(c - 1):
                    pe.wait_ge(turned, 4 * c + 2 * p - 2)
                for q in range(2):
                    last = nc.tensor.matmul(k.bank[:, 2 + 2 * p + q, 0:CH], w_b[:, q, p * 128:(p + 1) * 128],
                                            ut[:, j, :], start=True, stop=True)
                last.then_inc(bu, 1)

            def outputs(c, j, p):
                if p == 0:
                    pe.wait_ge(y_copied, c + 1)
                pe.wait_ge(back, 4 * c + 2 * p + 2)
                parts = [] if p else [(w_d[:], ut[:, j, :])]
                parts += [(w_c[:, 0, p], xc[:, p, 0]), (w_c[:, 2, p], xsn[:, p, 1]),
                          (w_c[:, 1, p], xsn[:, p, 0]), (w_c[:, 1, p], xc[:, p, 1])]
                for q, (w, x) in enumerate(parts):
                    last = nc.tensor.matmul(k.bank[:, 6 + j, 0:CH], w, x, start=(p == 0 and q == 0),
                                            stop=(p == 1 and q == len(parts) - 1))
                last.then_inc(y_ready if p else y_half, 1)

            def work(c, j):
                outputs(c, j, 0)
                if exists(c + 1):
                    for p in range(2):
                        inputs(c + 1, 1 - j, p)
                if exists(c + 2):
                    spread_rstd(c + 2, j)
                outputs(c, j, 1)

            for j in range(2):
                spread_rstd(j, j)
            for p in range(2):
                inputs(0, 0, p)
            chunks(pe, work)


class Normed:

    def __init__(self, nc, k, ctx, name):
        self.nc, self.k = nc, k
        self.diag = ctx.enter_context(nc.sbuf_tensor(f"{name}_diag", [128, 2, 4, HALF], F32))
        self.ut = ctx.enter_context(nc.sbuf_tensor(f"{name}_ut", [128, 2, CH], F32))
        self.diag_ready = k.semaphore(f"{name}_diag_ready")
        self.spread = k.semaphore(f"{name}_rstd_spread")
        self.u_ready = k.semaphore(f"{name}_u_ready")

    def pool_diagonal(self, pool, c, j):
        k = self.k
        pool.wait_ge(self.spread, c + 1)
        self.nc.gpsimd.tensor_tensor(
            self.diag[:, j], k.ident[:, 0:HALF].unsqueeze(1).broadcast_to([128, 4, HALF]),
            k.rstd[:, bass.ts(c, 4)].unsqueeze(2).broadcast_to([128, 4, HALF]), ALU.mult).then_inc(self.diag_ready, 1)

    def pe_spread(self, pe, c, j):
        pe.wait_ge(self.diag_ready, c + 1)
        self.nc.tensor.matmul(self.k.bank[:, j, 0:CH], self.k.ones[:],
                              self.diag[:, j].rearrange("p a b -> p (a b)"), start=True, stop=True).then_inc(self.spread, 1)

    def dve_start(self, dve):
        dve.sem_inc(self.spread, 2)

    def dve_apply(self, dve, c, j):
        dve.wait_ge(self.spread, c + 3)
        self.nc.vector.tensor_tensor(self.ut[:, j, :], self.k.hc[:, chunk(c)], self.k.bank[:, j, 0:CH],
                                     ALU.mult).then_inc(self.u_ready, 1)


def first_mixture(nc, k):
    a = k.a
    with ExitStack() as ctx:
        def sb(name, shape, dt=F32):
            return ctx.enter_context(nc.sbuf_tensor(f"m0_{name}", shape, dt))

        def sem(name):
            return k.semaphore(f"m0_{name}")

        norm = Normed(nc, k, ctx, "m0")
        ut = norm.ut
        gate = sb("gate", [128, E0])
        u_hi = sb("u_hi", [128, T], BF16)
        u_lo = sb("u_lo", [128, T], BF16)
        rows = sb("rows", [HALF, NT, E0 + 8])
        top = sb("top", [HALF, NT, 8])
        left = sb("left", [HALF, NT, E0 + 8])
        gap = sb("gap", [HALF, NT, E0])
        tot = sb("tot", [HALF, 2, NT])
        cat = sb("cat", [HALF, NT, 48])
        rt = k.hc[0:48, :]
        mask = sb("mask", [128, T], F16)
        xm_hi = sb("xm_hi", [128, 2, BLK], BF16)
        xm_lo = sb("xm_lo", [128, 2, BLK], BF16)
        junk = sb("junk", [128, 2, BLK], BF16)
        part = sb("part", [128, E0 * FC * NB])
        hsum = sb("hsum", [128, FC, E0 * E0])
        msum = sb("msum", [HALF, E0])
        cnt = sb("cnt", [E0, 2])
        ym = sb("ym", [128, 128])

        gate_in = sem("gate_in")
        u_high = sem("u_high")
        u_low = sem("u_low")
        logits = sem("logits")
        copied = sem("logits_copied")
        s = sem("routing_step")
        expd = sem("exp_ready")
        blank = sem("mask_blank")
        turned = sem("rows_turned")
        rt_ready = sem("rt_ready")
        mask_ready = sem("mask_ready")
        spread = sem("mask_spread")
        masked = sem("u_masked")
        up = sem("up_ready")
        summed = sem("silu_summed")
        fin = sem("mean_step")
        fin_pe = sem("mean_product")
        out = sem("out_ready")
        added = sem("out_added")
        block = ctx.enter_context(nc.Block())
        w0 = k.weights[:, 0].rearrange("p a b -> p (a b)")
        w0_hi, w0_lo = w0[:, 0:E0 * FF0], w0[:, E0 * FF0:]
        w2 = k.w0_down.rearrange("p (e f d) -> p e f d", e=E0, f=FC)
        PAIRS = 3

        def bank_pair(i, f):
            return 2 * ((i * FC + f) % PAIRS)

        def last_use(m):
            before = [n for n in range(NB * FC) if n % PAIRS == m % PAIRS]
            return m - PAIRS if m >= PAIRS else before[-1] - NB * FC

        @block.sync
        def _(sp):
            sp.dma_start(gate[:], a["gate"]).then_inc(gate_in, 16)

        @block.gpsimd
        def _(pool):
            with pool.Fori(0, NC // 2) as i:
                for j in range(2):
                    norm.pool_diagonal(pool, 2 * i + j, j)
            nc.gpsimd.memset(cat[:], 0.0).then_inc(blank, 1)
            nc.gpsimd.memset(mask[:], 0.0).then_inc(blank, 1)
            nc.gpsimd.memset(ym[:], 0.0).then_inc(blank, 1)
            nc.gpsimd.memset(hsum[:], 0.0).then_inc(blank, 1)

        @block.scalar
        def _(act):
            with act.Fori(0, NC // 2) as i:
                for j in range(2):
                    act.wait_ge(norm.u_ready, 2 * i + j + 1)
                    nc.scalar.activation(u_hi[:, chunk(2 * i + j)], ut[:, j, :], ACT.Copy).then_inc(u_high, 1)
            act.wait_ge(s, 2)
            nc.scalar.activation(gap[:], gap[:], ACT.Exp).then_inc(expd, 1)
            act.wait_ge(blank, 2)
            with act.Fori(0, NC // 4) as i:
                for j in range(4):
                    act.wait_ge(turned, 4 * i + j + 1)
                    nc.scalar.activation(rt[:, chunk(4 * i + j)], k.bank[0:48, j, 0:CH], ACT.Copy).then_inc(rt_ready, 1)
            act.sem_inc(summed, PAIRS)
            load_table(nc, k, 1, ACT.Silu)
            with act.Fori(0, E0) as x:
                for i in range(NB):
                    for f in range(FC):
                        act.wait_ge(up, (x * NB + i) * FC + f + 1)
                        act.wait_ge(summed, x * (NB * FC) + (i * FC + f - 1 + PAIRS))
                        pair = bank_pair(i, f)
                        nc.scalar.activation(junk[:, f % 2].rearrange("p (a b) -> p a b", a=2),
                                             k.bank[:, pair:pair + 2, 0:CH], ACT.Silu,
                                             accum_out=part[:, bass.ds(x * (NB * FC) + (f * NB + i), 1)]).then_inc(summed, 1)

        @block.vector
        def _(dve):
            v = nc.vector
            norm.dve_start(dve)
            v.memset(rows[:], SENT).then_inc(copied, 1)
            dve.wait_ge(copied, 1)
            with dve.Fori(0, NC // 2) as i:
                dve.wait_ge(u_low, 2 * i)
                for j in range(2):
                    norm.dve_apply(dve, 2 * i + j, j)
                for j in range(2):
                    dve.wait_ge(u_high, 2 * i + j + 1)
                    v.tensor_tensor(u_lo[:, chunk(2 * i + j)], ut[:, j, :], u_hi[:, chunk(2 * i + j)],
                                    ALU.subtract).then_inc(u_low, 1)
                    dve.wait_ge(logits, 2 * i + j + 1)
                    v.tensor_copy(rows[:, bass.ts(2 * i + j, 4), 0:E0],
                                  k.bank[0:HALF, 4 + j, 0:4 * E0].rearrange("p (n e) -> p n e", n=4)).then_inc(copied, 1)
            dve.wait_ge(copied, NC + 1)
            for n in range(NT):
                last = v.max(top[:, n, :], rows[:, n, :])
            last.then_inc(s, 1)
            dve.wait_ge(s, 1)
            v.tensor_tensor(gap[:], rows[:, :, 0:E0], top[:, :, 0:1].broadcast_to([HALF, NT, E0]), ALU.subtract).then_inc(s, 1)
            dve.wait_ge(s, 2)
            v.memset(top[:, :, 2:8], SENT).then_inc(s, 1)
            dve.wait_ge(s, 3)
            for n in range(NT):
                last = v.match_replace(left[:, n, :], top[:, n, :], rows[:, n, :], MARK)
            last.then_inc(s, 1)
            dve.wait_ge(s, 4)
            dve.wait_ge(blank, 2)
            v.tensor_scalar(cat[:, :, 32:48], left[:, :, 0:E0], CUT, SCL, ALU.is_le, ALU.mult).then_inc(s, 1)
            dve.wait_ge(s, 5)
            dve.wait_ge(expd, 1)
            v.scalar_tensor_tensor(gap[:], cat[:, :, 32:48], 1.0 / SCL, gap[:], ALU.mult, ALU.mult).then_inc(s, 1)
            v.tensor_reduce(msum[:], cat[:, :, 32:48].rearrange("p n e -> p e n"), X, ALU.add).then_inc(s, 1)
            dve.wait_ge(s, 6)
            v.tensor_reduce(tot[:, 0], gap[:], X, ALU.add).then_inc(s, 1)
            dve.wait_ge(s, 8)
            v.reciprocal(tot[:, 1], tot[:, 0]).then_inc(s, 1)
            dve.wait_ge(s, 9)
            v.tensor_tensor(cat[:, :, 0:E0], gap[:], tot[:, 1].unsqueeze(2).broadcast_to([HALF, NT, E0]),
                            ALU.mult).then_inc(s, 1)
            for c in range(NC):
                dve.wait_ge(rt_ready, c + 1)
                v.tensor_copy(mask[0:E0, c * CH:(c + 1) * CH], rt[32:48, c * CH:(c + 1) * CH]).then_inc(mask_ready, 1)
            dve.wait_ge(u_low, NC)
            with dve.Fori(0, E0) as x:
                for i in range(NB):
                    dve.wait_ge(spread, x * NB + i + 1)
                    m = k.bank[:, 6:8, 0:CH]
                    for dst, src in ((xm_hi, u_hi), (xm_lo, u_lo)):
                        v.tensor_tensor(dst[:, i % 2].rearrange("p (a b) -> p a b", a=2),
                                        src[:, i * BLK:(i + 1) * BLK].rearrange("p (a b) -> p a b", a=2), m,
                                        ALU.mult).then_inc(masked, 1)
            dve.wait_ge(summed, E0 * NB * FC + PAIRS)
            dve.wait_ge(blank, 4)
            v.tensor_reduce(hsum[:, :, 0:E0 * E0:E0 + 1], part[:].rearrange("p (x f i) -> p f x i", f=FC, i=NB), X,
                            ALU.add).then_inc(fin, 1)
            dve.wait_ge(fin_pe, 1)
            v.tensor_scalar(cnt[:, 0:1], k.bank[0:E0, 6, 0:1], 1.0 / SCL, 1.0, ALU.mult, ALU.max).then_inc(fin, 1)
            dve.wait_ge(fin, 2)
            v.reciprocal(cnt[:, 1:2], cnt[:, 0:1]).then_inc(fin, 1)
            dve.wait_ge(fin, 3)
            dve.wait_ge(fin_pe, 2)
            v.tensor_scalar(ym[0:E0], k.bank[0:E0, 7, 0:128], cnt[:, 1:2], None, ALU.mult).then_inc(fin, 1)
            dve.sem_inc(added, 4)
            with dve.Fori(0, NC // 4) as i:
                for j in range(4):
                    dve.wait_ge(out, 4 * i + j + 1)
                    v.tensor_tensor(k.h[:, chunk(4 * i + j)], k.h[:, chunk(4 * i + j)], k.bank[:, 4 + j, 0:CH],
                                    ALU.add).then_inc(added, 1)

        @block.tensor
        def _(pe):
            t = nc.tensor
            warm_up(nc, k)
            pe.wait_ge(gate_in, 16)
            with pe.Fori(0, NC // 2) as i:
                for j in range(2):
                    norm.pe_spread(pe, 2 * i + j, j)
                for j in range(2):
                    pe.wait_ge(norm.u_ready, 2 * i + j + 1)
                    pe.wait_ge(copied, 2 * i + j)
                    for q in range(4):
                        last = t.matmul(k.bank[0:HALF, 4 + j, q * E0:(q + 1) * E0], ut[:, j, q * HALF:(q + 1) * HALF],
                                        gate[:], start=True, stop=True)
                    last.then_inc(logits, 1)
            pe.wait_ge(s, 10)
            for c in range(NC):
                if c >= 4:
                    pe.wait_ge(rt_ready, c - 3)
                for q in range(4):
                    last = t.transpose(k.bank[0:48, c % 4, q * HALF:(q + 1) * HALF], cat[:, 4 * c + q, :],
                                       k.ident[0:HALF, 0:HALF])
                last.then_inc(turned, 1)
            pe.wait_ge(mask_ready, NC)
            pe.wait_ge(k.w0_split, NC)

            def pe_mask(x, i):
                for q in range(2):
                    last = t.matmul(k.bank[:, 6 + q, 0:CH], k.sel[:, bass.ds(x, 1), :].rearrange("p a b -> p (a b)"),
                                    mask[:, i * BLK + q * CH:i * BLK + (q + 1) * CH], start=True, stop=True)
                last.then_inc(spread, 1)

            pe_mask(0, 0)
            with pe.Fori(0, E0) as x:
                for i in range(NB):
                    pe.wait_ge(masked, 2 * (x * NB + i) + 2)
                    pe_mask(x + (i + 1) // NB, (i + 1) % NB)
                    for f in range(FC):
                        hi = w0_hi[:, bass.ds(x * FF0 + f * 128, 128)]
                        lo = w0_lo[:, bass.ds(x * FF0 + f * 128, 128)]
                        pe.wait_ge(summed, x * (NB * FC) + (last_use(i * FC + f) + 1 + PAIRS))
                        for m, (w, u) in enumerate(((hi, xm_hi), (hi, xm_lo), (lo, xm_hi))):
                            for q in range(2):
                                last = t.matmul(k.bank[:, bank_pair(i, f) + q, 0:CH], w, u[:, i % 2, q * CH:(q + 1) * CH],
                                                start=(m == 0), stop=(m == 2))
                        last.then_inc(up, 1)
            pe.wait_ge(masked, 2 * E0 * NB)
            pe.wait_ge(s, 7)
            t.matmul(k.bank[0:E0, 6, 0:1], msum[:], k.ones[0:HALF, 0:1], start=True, stop=True).then_inc(fin_pe, 1)
            pe.wait_ge(fin, 1)
            pe.wait_ge(k.w2_in, 16)
            for x in range(E0):
                for f in range(FC):
                    last = t.matmul(k.bank[0:E0, 7, 0:128], hsum[:, f, x * E0:(x + 1) * E0], w2[:, x, f, :],
                                    start=(x == 0 and f == 0), stop=(x == E0 - 1 and f == FC - 1))
            last.then_inc(fin_pe, 1)
            pe.wait_ge(fin, 4)
            with pe.Fori(0, NC // 4) as i:
                for j in range(4):
                    pe.wait_ge(added, 4 * i + j + 1)
                    t.matmul(k.bank[:, 4 + j, 0:CH], ym[:], k.hc[:, chunk(4 * i + j)], start=True, stop=True).then_inc(out, 1)


def sparse_attention(nc, k):
    a = k.a
    with ExitStack() as ctx:
        def sb(name, shape, dt=F32):
            return ctx.enter_context(nc.sbuf_tensor(f"at_{name}", shape, dt))

        def sem(name):
            return k.semaphore(f"at_{name}")

        GR = HG * NU
        q_all = k.weights[0:HALF, 1].bitcast(F32).rearrange("p a b -> p (a b)").rearrange("p (n d) -> p n d", n=NT)
        kt_all = k.hc
        v_all = sb("v_all", [HALF, NT, 128])
        wst = sb("wst", [128, 2, 1024])
        w_o = sb("w_o", [128, 128])
        v_mean = sb("v_mean", [128, B])
        hmu = sb("hmu", [128, NH])
        rank_t = sb("rank_t", [HALF, 2, 2 * 128])
        rank = sb("rank", [128, 2, L], BF16)
        expand = sb("expand", [128, 16, 2, GR], BF16)

        small_in = sem("small_in")
        made = sem("made")
        step = sem("choose_step")
        step_pe = sem("choose_product")
        w_in = [sem(f"w_in{p}") for p in range(2)]
        w_hi = sem("w_high")

        with ExitStack() as first:
            def sb1(name, shape, dt=F32):
                return first.enter_context(nc.sbuf_tensor(f"at_{name}", shape, dt))

            norm = Normed(nc, k, first, "at")
            ut = norm.ut
            w_qk = sb1("w_qk", [128, 3, 128])
            qt = sb1("qt", [128, 2, CH])
            kx = sb1("kx", [HALF, 2, 4, 128])
            idx = sb1("idx", [HALF, NS], I32)
            pos = sb1("pos", [HALF, 3, NS])
            line = sb1("line", [HALF, 2])
            pick = sb1("pick", [HALF, 2, NS + 1])
            ksm = sb1("ksm", [128, 2, NH, NS + 1])
            peak = sb1("peak", [HALF, 2, NH])
            m_all = sb1("m_all", [HALF, 2, 2 * 128])
            u_sum = sb1("u_sum", [128, B])
            cand = sb1("cand", [128, 2, L + 8])
            best = sb1("best", [128, 2, 8])
            chosen = sb1("chosen", [128, 2, L])
            count = sb1("count", [128, 2, L])
            qt_ready = sem("qt_ready")
            q_copied = sem("q_copied")
            kt_ready = sem("kt_ready")
            kt_copied = sem("kt_copied")
            tok_ready = sem("token_major_ready")
            kx_copied = sem("k_copied")
            ks_ready = sem("samples_ready")
            ks_masked = sem("samples_masked")
            sc_ready = sem("sampled_scores_ready")
            peaked = sem("peak_taken")
            u_summed = sem("u_summed")
            measured = sem("measure_taken")
            block = first.enter_context(nc.Block())

            def exists(c):
                return not isinstance(c, int) or 0 <= c < NC

            def chunks(eng, work):
                for c in range(2):
                    work(c, c)
                with eng.Fori(1, NC // 2 - 1) as i:
                    for j in range(2):
                        work(2 * i + j, j)
                for c in range(NC - 2, NC):
                    work(c, c % 2)

            def score_bank(j, q):
                return k.bank[0:HALF, 7 if q % 2 else 1 - j, 0:NH * (NS + 1)]

            @block.sync
            def _(sp):
                for q, name in enumerate(("wq", "wv", "wk")):
                    sp.dma_start(w_qk[:, q], a[name]).then_inc(small_in, 16)
                sp.dma_start(w_o[:], a["wo"]).then_inc(small_in, 16)
                sp.dma_start(idx[:], a["idx"].partition_broadcast(HALF)).then_inc(small_in, 16)

            @block.gpsimd
            def _(pool):
                g = nc.gpsimd
                g.iota(line[:], [[HALF, 2]], base=0, channel_multiplier=1,
                       allow_small_or_imprecise_dtypes=True).then_inc(made, 1)
                with pool.Fori(0, NC // 2) as i:
                    for j in range(2):
                        norm.pool_diagonal(pool, 2 * i + j, j)
                g.memset(expand[:], 0.0).then_inc(made, 1)
                pool.wait_ge(made, 2)
                g.affine_select(out=expand[:].rearrange("p b g (h u) -> p (b g h) u", h=HG),
                                in_=expand[:].rearrange("p b g (h u) -> p (b g h) u", h=HG),
                                compare_op=ALU.not_equal, fill=1.0, base=0,
                                pattern=[[-1, 128], [0, NU]], channel_multiplier=1).then_inc(made, 1)

            @block.scalar
            def _(act):
                def work(c, j):
                    act.wait_ge(qt_ready, c + 1)
                    if exists(c - 2):
                        act.wait_ge(sc_ready, 4 * (c - 1))
                    nc.scalar.activation(qt[:, j], k.bank[:, 2, 0:CH], ACT.Copy).then_inc(q_copied, 1)
                    act.wait_ge(kt_ready, c + 1)
                    nc.scalar.activation(kt_all[:, chunk(c)], k.bank[:, 3, 0:CH], ACT.Copy).then_inc(kt_copied, 1)
                    if exists(c - 2):
                        act.wait_ge(ks_ready, 2 * (c - 1))
                    for q in range(4):
                        act.wait_ge(tok_ready, 4 * c + q + 1)
                        for m, dst in enumerate((q_all[:, bass.ds(4 * c + q, 1), :].rearrange("p a b -> p (a b)"),
                                                 v_all[:, bass.ds(4 * c + q, 1), :].rearrange("p a b -> p (a b)"),
                                                 kx[:, j, q])):
                            last = nc.scalar.activation(dst, k.bank[0:HALF, 4 + q % 2, m * 128:(m + 1) * 128], ACT.Copy)
                        last.then_inc(kx_copied, 1)

                chunks(act, work)
                act.wait_ge(step_pe, 1)
                nc.scalar.activation(v_mean[:], k.bank[:, 2, 0:B], ACT.Copy, scale=1.0 / L)

            @block.vector
            def _(dve):
                v = nc.vector
                n = [0]

                def link(ins):
                    n[0] += 1
                    ins.then_inc(step, 1)
                    dve.wait_ge(step, n[0])

                norm.dve_start(dve)
                def normed(c, j):
                    if exists(c - 2):
                        dve.wait_ge(tok_ready, 4 * (c - 1))
                        dve.wait_ge(u_summed, c - 1)
                    norm.dve_apply(dve, c, j)
                    dve.wait_ge(norm.u_ready, c + 1)
                    v.tensor_reduce(u_sum[:, bass.ts(c, 2)], ut[:, j].rearrange("p (b l) -> p b l", b=2), X,
                                    ALU.add).then_inc(u_summed, 1)

                def work(c, j):
                    for b in range(2):
                        dve.wait_ge(ks_ready, 2 * c + 2)
                        if exists(c - 1):
                            dve.wait_ge(sc_ready, 4 * c)
                        v.tensor_tensor(ksm[:, b], k.bank[:, 6, b * 64:b * 64 + NS + 1].unsqueeze(1).broadcast_to([128, NH, NS + 1]),
                                        k.hm[:].unsqueeze(2).broadcast_to([128, NH, NS + 1]), ALU.mult).then_inc(ks_masked, 1)
                    for q in range(4):
                        m = 4 * c + q
                        if q == 3 and exists(c + 2):
                            normed(c + 2, j)
                        sc = score_bank(j, q).rearrange("p (h s) -> p h s", h=NH)
                        dve.wait_ge(sc_ready, m + 1)
                        v.tensor_reduce(peak[:, q % 2], sc[:, :, 0:NS], X, ALU.max).then_inc(peaked, 1)
                        dve.wait_ge(peaked, m + 1)
                        v.tensor_tensor(m_all[:, q % 2, bass.ds((2 * c + q // 2) * NH, NH)], peak[:, q % 2],
                                        sc[:, :, NS:NS + 1].rearrange("p a b -> p (a b)"), ALU.subtract).then_inc(measured, 1)

                normed(0, 0)
                normed(1, 1)
                dve.wait_ge(small_in, 80)
                dve.wait_ge(made, 1)
                link(v.tensor_copy(pos[:, 0], idx[:]))
                link(v.tensor_scalar(pos[:, 1], pos[:, 0], 0.0, float(L), ALU.is_lt, ALU.mult))
                link(v.tensor_tensor(pos[:, 2], pos[:, 0], pos[:, 1], ALU.add))
                link(v.tensor_scalar(pos[:, 0], pos[:, 2], 0.0, float(L - 1), ALU.max, ALU.min))
                for q in range(2):
                    link(v.tensor_scalar(pick[:, q, 0:NS], pos[:, 0], line[:, q:q + 1], None, ALU.is_equal))
                link(v.tensor_reduce(pos[:, 1, 0:2], pick[:, :, 0:NS], X, ALU.add))
                link(v.tensor_scalar(pick[:, :, NS:NS + 1], pos[:, 1, 0:2].unsqueeze(2), 1.0 / NS, None, ALU.mult))
                link(v.tensor_scalar(hmu[:], k.hm[:], DH ** -0.5, None, ALU.mult))
                link(v.memset(cand[:], SENT))
                chunks(dve, work)
                dve.wait_ge(step_pe, 1)
                for gq in range(4):
                    last = v.tensor_copy(cand[:, gq // 2, (gq % 2) * HALF:(gq % 2) * HALF + HALF],
                                         k.bank[:, 0, gq * HALF:(gq + 1) * HALF])
                link(last)
                for r in range(NU // 8):
                    for g in range(2):
                        last = v.max(best[:, g], cand[:, g])
                    link(last)
                    for g in range(2):
                        last = v.match_replace(cand[:, g], best[:, g], cand[:, g], MARK)
                    link(last)
                for g in range(2):
                    last = v.max(best[:, g], cand[:, g])
                link(last)
                link(v.memset(best[:, :, NU % 8:8], SENT))
                for g in range(2):
                    last = v.match_replace(cand[:, g], best[:, g], cand[:, g], MARK)
                link(last)
                link(v.tensor_scalar(chosen[:], cand[:, :, 0:L], CUT, None, ALU.is_le))
                for g in range(2):
                    last = v.tensor_tensor_scan(count[:, g], k.ones[:, 0:1].broadcast_to([128, L]), chosen[:, g], 0.0, ALU.mult, ALU.add)
                link(last)
                link(v.tensor_tensor(count[:], count[:], chosen[:], ALU.mult))
                v.tensor_copy(rank[:], count[:]).then_inc(step, 1)
                dve.wait_ge(step_pe, 2)
                for gq in range(4):
                    g, half = gq // 2, gq % 2
                    v.tensor_copy(rank_t[:, half, g * 128:(g + 1) * 128], k.bank[0:HALF, 1, gq * 128:(gq + 1) * 128])

            @block.tensor
            def _(pe):
                t = nc.tensor

                def query(c, j):
                    pe.wait_ge(norm.u_ready, c + 1)
                    if exists(c - 1):
                        pe.wait_ge(q_copied, c)
                    t.matmul(k.bank[:, 2, 0:CH], w_qk[:, 0], ut[:, j], start=True, stop=True).then_inc(qt_ready, 1)

                def key(c, j):
                    if exists(c - 1):
                        pe.wait_ge(kt_copied, c)
                    t.matmul(k.bank[:, 3, 0:CH], w_qk[:, 2], ut[:, j], start=True, stop=True).then_inc(kt_ready, 1)

                def token_major(c, j, q):
                    if q >= 2 or exists(c - 1):
                        pe.wait_ge(kx_copied, 4 * c + q - 1)
                    t.matmul(k.bank[0:HALF, 4 + q % 2, 0:384], ut[:, j, q * HALF:(q + 1) * HALF],
                             w_qk[:].rearrange("p a b -> p (a b)"), start=True, stop=True).then_inc(tok_ready, 1)

                def samples(c, j, b):
                    pe.wait_ge(kx_copied, 4 * c + 2 * b + 2)
                    if exists(c - 1):
                        pe.wait_ge(ks_masked, 2 * c)
                    for half in range(2):
                        last = t.matmul(k.bank[:, 6, b * 64:b * 64 + NS + 1], kx[:, j, 2 * b + half], pick[:, half],
                                        start=(half == 0), stop=(half == 1))
                    last.then_inc(ks_ready, 1)

                def sampled_scores(c, j, q):
                    pe.wait_ge(ks_masked, 2 * c + q // 2 + 1)
                    pe.wait_ge(q_copied, c + 1)
                    if q >= 2 or q and exists(c - 1):
                        pe.wait_ge(measured, 4 * c + q - 1)
                    t.matmul(score_bank(j, q), qt[:, j, q * HALF:(q + 1) * HALF],
                             ksm[:, q // 2].rearrange("p a b -> p (a b)"), start=True, stop=True).then_inc(sc_ready, 1)

                def work(c, j):
                    ahead = exists(c + 1)
                    samples(c, j, 0)
                    samples(c, j, 1)
                    if ahead:
                        query(c + 1, 1 - j)
                        key(c + 1, 1 - j)
                    if exists(c + 2):
                        if exists(c - 1):
                            pe.wait_ge(measured, 4 * c - 1)
                        norm.pe_spread(pe, c + 2, j)
                    for q in range(4):
                        if ahead:
                            token_major(c + 1, 1 - j, q)
                        sampled_scores(c, j, q)

                for j in range(2):
                    norm.pe_spread(pe, j, j)
                pe.wait_ge(small_in, 80)
                query(0, 0)
                key(0, 0)
                for q in range(4):
                    token_major(0, 0, q)
                pe.wait_ge(step, 10)
                chunks(pe, work)
                pe.wait_ge(u_summed, NC)
                pe.wait_ge(q_copied, NC)
                t.matmul(k.bank[:, 2, 0:B], w_qk[:, 1], u_sum[:], start=True, stop=True)
                pe.wait_ge(measured, NT)
                for gq in range(4):
                    last = t.transpose(k.bank[:, 0, gq * HALF:(gq + 1) * HALF],
                                       m_all[:, gq % 2, (gq // 2) * 128:(gq // 2 + 1) * 128], k.ident[0:HALF, 0:HALF])
                last.then_inc(step_pe, 1)
                pe.wait_ge(step, 10 + 1 + 2 * (NU // 8) + 6)
                for gq in range(4):
                    g, half = gq // 2, gq % 2
                    last = t.transpose(k.bank[0:HALF, 1, gq * 128:(gq + 1) * 128], count[:, g, half * HALF:(half + 1) * HALF],
                                       k.ident[:])
                last.then_inc(step_pe, 1)

        attend(nc, k, q_all, kt_all, v_all, v_mean, wst, w_o, hmu, rank, rank_t, expand, w_in, w_hi)


def attend(nc, k, q_all, kt_all, v_all, v_mean, wst, w_o, hmu, rank, rank_t, expand, w_in, w_hi):
    with ExitStack() as ctx:
        def sb(name, shape, dt=F32):
            return ctx.enter_context(nc.sbuf_tensor(f"att_{name}", shape, dt))

        def sem(name):
            return k.semaphore(f"att_{name}")

        NR, GR = NH * NU, HG * NU
        U = 4
        uline = sb("uline", [HALF, NU])
        urow = sb("urow", [128, 5])
        hmt = sb("hmt", [GR, 2, NH, DH])
        oht = sb("oht", [GR, U, 2, L])
        oh = sb("oh", [HALF, 2, 2, NR])
        qs = sb("qs", [HALF, 2, 2, 128])
        qm = sb("qm", [128, 2, NR])
        nmax = sb("nmax", [GR, 2, 2])
        prob = sb("prob", [GR, 2, 2, L])
        tot = sb("tot", [GR, 2, 2, 2])
        pt = sb("pt", [HALF, 2, 4, GR])
        pv = sb("pv", [GR, 2, 2, 128])
        ot = sb("ot", [128, 2, L])
        made = sem("made")
        prep = sem("prep")
        rows = sem("rank_rows")
        onehot = sem("onehot")
        staged = sem("q_staged")
        gathered = sem("q_gathered")
        qmask = sem("q_masked")
        scored = sem("scored")
        maxed = sem("maxed")
        expd = sem("exped")
        recip = sem("recip")
        normed = sem("normed")
        turned = sem("prob_turned")
        pt_ready = sem("pt_ready")
        pv_ready = sem("pv_ready")
        pv_masked = sem("pv_masked")
        scat = sem("scattered")
        ot_ready = sem("ot_ready")
        proj = sem("projected")
        added = sem("added")
        block = ctx.enter_context(nc.Block())

        def batches(eng, step):
            for x in range(U):
                step(x, x)
            with eng.Fori(1, B // U) as i:
                for x in range(U):
                    step(U * i + x, x)

        def exists(b):
            return not isinstance(b, int) or 0 <= b < B

        @block.sync
        def _(sp):
            load_group(sp, k, 0, wst, w_in, k.group_split, 0)

        @block.gpsimd
        def _(pool):
            g = nc.gpsimd
            g.iota(uline[:], [[1, NU]], base=1, channel_multiplier=0, allow_small_or_imprecise_dtypes=True).then_inc(made, 1)
            g.iota(urow[:, 0:1], [[0, 1]], base=0, channel_multiplier=1, allow_small_or_imprecise_dtypes=True).then_inc(made, 1)
            g.memset(hmt[:], 1.0).then_inc(made, 1)
            pool.wait_ge(made, 3)
            for q in range(2):
                g.affine_select(out=hmt[:, q], in_=hmt[:, q], compare_op=ALU.is_ge, fill=0.0, base=NU * HG * q,
                                pattern=[[-NU, NH], [0, DH]], channel_multiplier=1).then_inc(made, 1)
            pool.wait_ge(made, 5)
            for q in range(2):
                g.affine_select(out=hmt[:, q], in_=hmt[:, q], compare_op=ALU.is_ge, fill=0.0, base=NU - 1 - NU * HG * q,
                                pattern=[[NU, NH], [0, DH]], channel_multiplier=-1).then_inc(made, 1)
            split_group(nc, pool, k, 0, wst, w_in, w_hi, 0, 0)

        @block.scalar
        def _(act):
            s = nc.scalar

            def exponentials(b, x):
                if not exists(b):
                    return
                act.wait_ge(maxed, b + 1)
                if exists(b - 2):
                    act.wait_ge(turned, b - 1)
                for g in range(2):
                    s.activation(prob[:, x % 2, g], k.bank[0:GR, 2, g * L:(g + 1) * L], ACT.Exp, bias=nmax[:, x % 2, g:g + 1],
                                 accum_out=tot[:, x % 2, 0, g:g + 1]).then_inc(expd, 1)

            def turned_copy(b, x):
                if not exists(b):
                    return
                act.wait_ge(turned, b + 1)
                if exists(b - 2):
                    act.wait_ge(pv_ready, b - 1)
                s.activation(pt[:, x % 2].rearrange("p a b -> p (a b)"), k.bank[0:HALF, 3, 0:4 * GR], ACT.Copy).then_inc(pt_ready, 1)

            def output_copy(b, x):
                if not exists(b):
                    return
                act.wait_ge(scat, b + 1)
                if exists(b - 2):
                    act.wait_ge(proj, b - 1)
                s.activation(ot[:, x % 2], k.bank[:, 5, 0:L], ACT.Identity, bias=v_mean[:, bass.ds(b, 1)]).then_inc(ot_ready, 1)

            def step(b, x):
                if exists(b):
                    if exists(b - 2):
                        act.wait_ge(gathered, b - 1)
                    s.activation(qs[:, x % 2], q_all[:, bass.ts(b, 2), :], ACT.Copy).then_inc(staged, 1)
                exponentials(b - 1, x - 1)
                turned_copy(b - 1, x - 1)
                output_copy(b - 2, x - 2)

            batches(act, step)
            exponentials(B - 1, B - 1)
            turned_copy(B - 1, B - 1)
            output_copy(B - 2, B - 2)
            output_copy(B - 1, B - 1)

        @block.vector
        def _(dve):
            v = nc.vector
            dve.wait_ge(made, 7)
            for m, edge in enumerate((NU, 2 * NU, 3 * NU)):
                v.tensor_scalar(urow[:, m + 1:m + 2], urow[:, 0:1], float(edge), -float(NU), ALU.is_ge, ALU.mult).then_inc(prep, 1)
            dve.wait_ge(prep, 3)
            v.tensor_reduce(urow[:, 4:5], urow[:, 0:4], X, ALU.add).then_inc(prep, 1)
            dve.wait_ge(prep, 4)
            v.tensor_scalar(urow[:, 0:1], urow[:, 4:5], 1.0, None, ALU.add).then_inc(prep, 1)
            dve.wait_ge(prep, 5)

            def one_hots(b, x):
                if not exists(b):
                    return
                dve.wait_ge(rows, b + 1)
                if exists(b - U):
                    dve.wait_ge(scat, b - U + 1)
                v.tensor_scalar(oht[:, x % U], k.bank[0:GR, 0, 0:2 * L].rearrange("p (g l) -> p g l", g=2), urow[0:GR, 0:1], None,
                                ALU.is_equal).then_inc(onehot, 1)
                if exists(b - 2):
                    dve.wait_ge(gathered, b - 1)
                for half in range(2):
                    v.tensor_tensor(oh[:, x % 2, half].rearrange("p (h u) -> p h u", h=NH),
                                    rank_t[:, half, bass.ts(b, NH)].unsqueeze(2).broadcast_to([HALF, NH, NU]),
                                    uline[:].unsqueeze(1).broadcast_to([HALF, NH, NU]), ALU.is_equal).then_inc(onehot, 1)

            def head_mask(b, x):
                if not exists(b):
                    return
                dve.wait_ge(gathered, b + 1)
                if exists(b - 2):
                    dve.wait_ge(scored, b - 1)
                v.tensor_tensor(qm[:, x % 2].rearrange("p (h u) -> p h u", h=NH), k.bank[:, 1, 0:NR].rearrange("p (h u) -> p h u", h=NH),
                                hmu[:].unsqueeze(2).broadcast_to([128, NH, NU]), ALU.mult).then_inc(qmask, 1)

            def maxima(b, x):
                if not exists(b):
                    return
                dve.wait_ge(scored, b + 1)
                if exists(b - 2):
                    dve.wait_ge(expd, 2 * b - 2)
                v.tensor_reduce(nmax[:, x % 2], k.bank[0:GR, 2, 0:2 * L].rearrange("p (g l) -> p g l", g=2), X, ALU.max,
                                negate=True).then_inc(maxed, 1)

            def normalise(b, x):
                if not exists(b):
                    return
                dve.wait_ge(expd, 2 * b + 2)
                v.reciprocal(tot[:, x % 2, 1], tot[:, x % 2, 0]).then_inc(recip, 1)
                dve.wait_ge(recip, b + 1)
                for g in range(2):
                    v.tensor_scalar(prob[:, x % 2, g], prob[:, x % 2, g], tot[:, x % 2, 1, g:g + 1], -1.0 / L, ALU.mult,
                                    ALU.add).then_inc(normed, 1)

            def value_mask(b, x):
                if not exists(b):
                    return
                dve.wait_ge(pv_ready, b + 1)
                if exists(b - 2):
                    dve.wait_ge(scat, b - 1)
                v.tensor_tensor(pv[:, x % 2], k.bank[0:GR, 4, 0:256].rearrange("p (g d) -> p g d", g=2),
                                hmt[:].rearrange("p g h d -> p g (h d)"), ALU.mult).then_inc(pv_masked, 1)

            def residual(b, x):
                if not exists(b):
                    return
                dve.wait_ge(proj, b + 1)
                v.tensor_tensor(k.h[:, bass.ts(b, L)], k.h[:, bass.ts(b, L)], k.bank[:, 7, 0:L], ALU.add).then_inc(added, 1)

            def step(b, x):
                one_hots(b, x)
                maxima(b - 1, x - 1)
                value_mask(b - 2, x - 2)
                normalise(b - 1, x - 1)
                head_mask(b, x)
                residual(b - 3, x - 3)

            batches(dve, step)
            for b in range(B, B + 3):
                step(b, b)

        @block.tensor
        def _(pe):
            t = nc.tensor
            pe.wait_ge(made, 7)

            def rank_rows(b, gb, at):
                if exists(b - 1):
                    pe.wait_ge(onehot, 3 * b)
                for g in range(2):
                    last = t.matmul(k.bank[0:GR, 0, g * L:(g + 1) * L], expand[:, bass.ds(at, 1), g].rearrange("p a b -> p (a b)"),
                                    rank[:, gb], start=True, stop=True)
                last.then_inc(rows, 1)

            def gather(b, x):
                pe.wait_ge(onehot, 3 * b + 3)
                pe.wait_ge(staged, b + 1)
                if exists(b - 1):
                    pe.wait_ge(qmask, b)
                for half in range(2):
                    last = t.matmul(k.bank[:, 1, 0:NR], qs[:, x % 2, half], oh[:, x % 2, half], start=(half == 0), stop=(half == 1))
                last.then_inc(gathered, 1)

            def score(b, x):
                if not exists(b):
                    return
                pe.wait_ge(qmask, b + 1)
                if exists(b - 1):
                    pe.wait_ge(expd, 2 * b)
                for g in range(2):
                    last = t.matmul(k.bank[0:GR, 2, g * L:(g + 1) * L], qm[:, x % 2, g * GR:(g + 1) * GR],
                                    kt_all[:, bass.ts(b, L)], start=True, stop=True)
                last.then_inc(scored, 1)

            def turn(b, x):
                if not exists(b):
                    return
                pe.wait_ge(normed, 2 * b + 2)
                if exists(b - 1):
                    pe.wait_ge(pt_ready, b)
                for half in range(2):
                    for g in range(2):
                        q = half * 2 + g
                        last = t.transpose(k.bank[0:HALF, 3, q * GR:(q + 1) * GR], prob[:, x % 2, g, half * HALF:(half + 1) * HALF],
                                           k.ident[0:GR, 0:GR])
                last.then_inc(turned, 1)

            def values(b, x):
                if not exists(b):
                    return
                pe.wait_ge(pt_ready, b + 1)
                if exists(b - 1):
                    pe.wait_ge(pv_masked, b)
                for g in range(2):
                    for half in range(2):
                        last = t.matmul(k.bank[0:GR, 4, g * 128:(g + 1) * 128], pt[:, x % 2, half * 2 + g],
                                        v_all[:, bass.ds(2 * b + half, 1), :].rearrange("p a b -> p (a b)"),
                                        start=(half == 0), stop=(half == 1))
                last.then_inc(pv_ready, 1)

            def scatter(b, x):
                if not exists(b):
                    return
                pe.wait_ge(pv_masked, b + 1)
                if exists(b - 1):
                    pe.wait_ge(ot_ready, b)
                for g in range(2):
                    last = t.matmul(k.bank[:, 5, 0:L], pv[:, x % 2, g], oht[:, x % U, g], start=(g == 0), stop=(g == 1))
                last.then_inc(scat, 1)

            def project(b, x):
                if not exists(b):
                    return
                pe.wait_ge(ot_ready, b + 1)
                if exists(b - 1):
                    pe.wait_ge(added, b)
                t.matmul(k.bank[:, 7, 0:L], w_o[:], ot[:, x % 2], start=True, stop=True).then_inc(proj, 1)

            def step(b, x, following):
                score(b - 1, x - 1)
                values(b - 2, x - 2)
                gather(b, x)
                project(b - 3, x - 3)
                if following:
                    rank_rows(b + 1, *following)
                turn(b - 1, x - 1)
                scatter(b - 2, x - 2)

            half_b = B // 2
            passes = half_b // U

            def one_pass(i, half, last=False):
                for x in range(U):
                    following = (half, U * i + (x + 1 - half * half_b))
                    if last and x == U - 1:
                        following = (1, 0) if half == 0 else None
                    step(U * i + x, x, following)

            rank_rows(0, 0, 0)
            one_pass(0, 0)
            with pe.Fori(1, passes - 1) as i:
                one_pass(i, 0)
            one_pass(passes - 1, 0, last=True)
            with pe.Fori(passes, 2 * passes - 1) as i:
                one_pass(i, 1)
            one_pass(2 * passes - 1, 1, last=True)
            for b in range(B, B + 3):
                score(b - 1, b - 1)
                values(b - 2, b - 2)
                project(b - 3, b - 3)
                turn(b - 1, b - 1)
                scatter(b - 2, b - 2)


PIECES = 4
PIECE = GE * HC * 128 // PIECES


def load_group(sp, k, g, wst, w_in, split, before):
    for m in range(2 * PIECES):
        src = k.a["e_w1"] if m < PIECES else k.a["e_w2"]
        if m + before >= 2:
            sp.wait_ge(split, before + m - 1)
        sp.dma_start(wst[:, m % 2, :], src[:, bass.ds(g * GE * HC * 128 + (m % PIECES) * PIECE, PIECE)]).then_inc(w_in[m % 2], 16)


def split_group(nc, pool, k, slot, wst, w_in, w_hi, before, high_before):
    for m in range(2 * PIECES):
        cols = slice((m % PIECES) * PIECE, (m % PIECES + 1) * PIECE)
        hi = k.weights[:, slot, 2 * (m // PIECES), cols]
        lo = k.weights[:, slot, 2 * (m // PIECES) + 1, cols]
        pool.wait_ge(w_in[m % 2], 8 * before + 16 * (m // 2 + 1))
        nc.gpsimd.tensor_copy(hi, wst[:, m % 2, :]).then_inc(w_hi, 1)
        pool.wait_ge(w_hi, high_before + m + 1)
        nc.gpsimd.tensor_tensor(lo, wst[:, m % 2, :], hi, ALU.subtract).then_inc(k.group_split, 1)


ROUTE = [0, 8, 16, 24, 32, 40, 49, 50, 51, 52, 54, 55, 55, 55, 55, 55, 55]
CAT_AT, TURN_AT = 10, 15


def second_mixture(nc, k):
    a = k.a
    with ExitStack() as ctx:
        def sb(name, shape, dt=F32):
            return ctx.enter_context(nc.sbuf_tensor(f"m1_{name}", shape, dt))

        def sem(name):
            return k.semaphore(f"m1_{name}")

        drop = E1 - TOP1
        TU = BLK // HALF
        norm = Normed(nc, k, ctx, "m1")
        ut = norm.ut
        router = sb("router", [128, E1])
        rb = sb("rb", [HALF, E1])
        b1 = sb("b1", [128, E1, HC])
        b2 = sb("b2", [128, 128])
        u_hi = sb("u_hi", [128, T], BF16)
        u_lo = sb("u_lo", [128, T], BF16)
        lg = sb("lg", [HALF, NT, E1])
        row = sb("row", [HALF, TU, E1 + 8])
        ex = sb("ex", [HALF, NT, E1])
        red = sb("red", [HALF, 3, NT])
        best = sb("best", [HALF, TU, 8])
        share = sb("share", [HALF, 3, TU])
        cat = norm.diag[0:HALF].rearrange("p a b c -> p (a b c)")[:, 0:TU * E1].rearrange("p (n e) -> p n e", n=TU)
        comb32 = ut[:].rearrange("p a b -> p (a b)")
        cat16 = sb("cat16", [HALF, TU, 2, E1], F16)
        ident16 = sb("ident16", [HALF, HALF], F16)
        comb = sb("comb", [128, T], F16)
        wst = sb("wst", [128, 2, PIECE])
        g = k.hc[:, 0:2 * BLK].rearrange("p (c n) -> p c n", c=2)
        hs = k.hc[:, 2 * BLK:4 * BLK].rearrange("p (c n) -> p c n", c=2)
        halves = k.hc[:, 4 * BLK:8 * BLK].bitcast(BF16).rearrange("p (m x c n) -> p m x c n", m=2, x=2, c=2)
        h_hi, h_lo = halves[:, 0], halves[:, 1]

        small_in = sem("small_in")
        filled = sem("filled")
        u_high = sem("u_high")
        u_low = sem("u_low")
        logits = sem("logits")
        copied = sem("logits_copied")
        prepared = sem("prepared")
        row_ready = sem("row_ready")
        exp_passed = sem("exp_passed")
        s = sem("routing_step")
        expd = sem("exp_ready")
        topk = sem("top_step")
        passed = sem("top_step_passed")
        cat_ready = sem("cat_ready")
        cat_high = sem("cat_high")
        cat_low = sem("cat_low")
        turned = sem("comb_turned")
        comb_ready = sem("comb_ready")
        up = sem("up_ready")
        spread = sem("comb_spread")
        g_ready = sem("gelu_ready")
        scaled = sem("scaled")
        hi_ready = sem("hidden_high")
        low = sem("hidden_low")
        used = sem("hidden_used")
        y_added = sem("y_added")
        w_in = [sem(f"w_in{p}") for p in range(2)]
        w_hi = sem("w_high")
        block = ctx.enter_context(nc.Block())

        def number(grp, tb, e):
            return (grp * NB + tb) * GE + e

        def two(ap):
            return ap.rearrange("p (a b) -> p a b", a=2)

        @block.sync
        def _(sp):
            for dst, src in ((router[:], a["router"]), (rb[:], a["router_b"].partition_broadcast(HALF)), (b1[:], a["e_b1"]),
                             (b2[0:E1], a["e_b2"]), (b2[E1:128], a["e_b2"])):
                sp.dma_start(dst, src).then_inc(small_in, 16)
            for grp in range(1, NG):
                load_group(sp, k, grp, wst, w_in, k.group_split, 2 * PIECES * grp)

        @block.gpsimd
        def _(pool):
            nc.gpsimd.memset(row[:, :, E1:E1 + 8], SENT).then_inc(filled, 1)
            with pool.Fori(0, NC // 2) as i:
                for j in range(2):
                    norm.pool_diagonal(pool, 2 * i + j, j)
            for grp in range(1, NG):
                if grp >= 2:
                    pool.wait_ge(used, (grp - 1) * NB * GE + 2)
                split_group(nc, pool, k, grp % 2, wst, w_in, w_hi, 2 * PIECES * (grp - 1), 2 * PIECES * (grp - 1))

        @block.scalar
        def _(act):
            sc = nc.scalar
            sc.activation(ident16[:], k.ident[0:HALF, 0:HALF], ACT.Copy).then_inc(prepared, 1)
            act.wait_ge(small_in, 80)
            sc.activation(b2[:], b2[:], ACT.Copy, scale=1.0 / SCL).then_inc(prepared, 1)

            def u_highs(i, j):
                act.wait_ge(norm.u_ready, 2 * i + j + 1)
                sc.activation(u_hi[:, chunk(2 * i + j)], ut[:, j, :], ACT.Copy).then_inc(u_high, 1)

            def exponentials(i):
                tiles = bass.ts(i, TU)
                act.wait_ge(s, 6 * i + 2)
                sc.activation(ex[:, tiles, :], lg[:, tiles, :], ACT.Exp).then_inc(expd, 1)
                act.wait_ge(s, 6 * i + 6)
                act.sem_inc(exp_passed, 1)
                sc.activation(ex[:, tiles, :], ex[:, tiles, :], ACT.Exp).then_inc(expd, 1)

            load_table(nc, k, 2, ACT.Exp)
            for j in range(2):
                u_highs(0, j)
            with act.Fori(1, NB) as i:
                for j in range(2):
                    u_highs(i, j)
                exponentials(i - 1)
            exponentials(NB - 1)

            def row_copies(b):
                sc.activation(row[:, :, 0:E1], lg[:, bass.ds(b * TU, TU), :], ACT.Copy).then_inc(row_ready, 1)

            def cat_highs(b):
                act.wait_ge(cat_ready, b + 1)
                sc.activation(cat16[:, :, 0], cat, ACT.Copy).then_inc(cat_high, 1)

            def comb_copies(b):
                act.wait_ge(turned, b + 1)
                sc.activation(two(comb[:, bass.ds(b * BLK, BLK)]), k.bank[:, 4:6, 0:CH], ACT.Copy).then_inc(comb_ready, 1)
                sc.activation(two(comb32), k.bank[:, 4:6, 0:CH], ACT.Copy).then_inc(comb_ready, 1)

            row_copies(0)
            cat_highs(0)
            comb_copies(0)
            act.sem_inc(used, 2)
            load_table(nc, k, 0, ACT.Gelu)

            def expert(grp, tb, e, x, after_gelu=None, before_gelu=None):
                it = number(grp, tb, e)
                if before_gelu:
                    before_gelu()
                for c in range(HC):
                    act.wait_ge(up, 2 * it + c + 1)
                    act.wait_ge(scaled, 2 * it + c + 1)
                    sc.activation(two(g[:, c]), k.bank[:, 2 * c:2 * c + 2, 0:CH], ACT.Gelu,
                                  bias=b1[:, bass.ds(grp * GE + e, 1), c]).then_inc(g_ready, 1)
                if after_gelu:
                    after_gelu()
                for c in range(HC):
                    act.wait_ge(scaled, 2 * it + c + 3)
                    act.wait_ge(used, it + 1)
                    sc.activation(h_hi[:, x, c], hs[:, c], ACT.Copy).then_inc(hi_ready, 1)

            with act.Fori(0, NB - 1) as tb:
                for e in range(GE):
                    expert(0, tb, e, e % 2,
                           after_gelu={0: lambda: row_copies(tb + 1), CAT_AT: lambda: cat_highs(tb + 1)}.get(e),
                           before_gelu=(lambda: comb_copies(tb + 1)) if e == TURN_AT else None)
            with act.Fori(0, GE // 2) as ee:
                for x in range(2):
                    expert(0, NB - 1, 2 * ee + x, x)
            for grp in range(1, NG):
                with act.Fori(0, NB) as tb:
                    with act.Fori(0, GE // 2) as ee:
                        for x in range(2):
                            expert(grp, tb, 2 * ee + x, x)

        @block.vector
        def _(dve):
            v = nc.vector
            norm.dve_start(dve)

            def wide(n, tiles):
                return red[:, n, tiles].unsqueeze(2).broadcast_to([HALF, TU, E1])

            def softmaxes(i):
                tiles = bass.ts(i, TU)
                l, x = lg[:, tiles, :], ex[:, tiles, :]

                def greatest():
                    dve.wait_ge(copied, 2 * i + 2)
                    v.tensor_reduce(red[:, 0, tiles], l, X, ALU.max).then_inc(s, 1)

                def centre():
                    dve.wait_ge(s, 6 * i + 1)
                    v.tensor_tensor(l, l, wide(0, tiles), ALU.subtract).then_inc(s, 1)

                def total():
                    dve.wait_ge(expd, 2 * i + 1)
                    v.tensor_reduce(red[:, 1, tiles], x, X, ALU.add).then_inc(s, 1)

                def inverse():
                    dve.wait_ge(s, 6 * i + 3)
                    v.reciprocal(red[:, 2, tiles], red[:, 1, tiles]).then_inc(s, 1)

                def negated():
                    dve.wait_ge(s, 6 * i + 4)
                    v.scalar_tensor_tensor(l, x, -1.0, wide(2, tiles), ALU.mult, ALU.mult).then_inc(s, 1)

                def second():
                    dve.wait_ge(s, 6 * i + 5)
                    v.scalar_tensor_tensor(x, l, -1.0, wide(2, tiles), ALU.mult, ALU.subtract).then_inc(s, 1)

                return greatest, centre, total, inverse, negated, second

            def low_half(i, j):
                dve.wait_ge(u_high, 2 * i + j + 1)
                v.tensor_tensor(u_lo[:, chunk(2 * i + j)], ut[:, j, :], u_hi[:, chunk(2 * i + j)],
                                ALU.subtract).then_inc(u_low, 1)

            def logit(i, j):
                dve.wait_ge(logits, 2 * i + j + 1)
                v.tensor_tensor(lg[:, bass.ts(2 * i + j, 4), :],
                                k.bank[0:HALF, 4 + j, 0:4 * E1].rearrange("p (n e) -> p n e", n=4),
                                rb[:].unsqueeze(1).broadcast_to([HALF, 4, E1]), ALU.add).then_inc(copied, 1)

            for j in range(2):
                norm.dve_apply(dve, j, j)
            dve.wait_ge(small_in, 80)
            for j in range(2):
                low_half(0, j)
                logit(0, j)
            with dve.Fori(1, NB) as i:
                dve.wait_ge(u_low, 2 * i)
                greatest, centre, total, inverse, negated, second = softmaxes(i - 1)
                norm.dve_apply(dve, 2 * i, 0)
                greatest()
                norm.dve_apply(dve, 2 * i + 1, 1)
                centre()
                low_half(i, 0)
                logit(i, 0)
                total()
                low_half(i, 1)
                inverse()
                logit(i, 1)
                negated()
                second()
            for step in softmaxes(NB - 1):
                step()

            def routing(b):
                first, steps, n = bass.ds(b * TU, TU), [], [0]
                x = ex[:, first, :]

                def over_tiles(op):
                    for j in range(TU):
                        def one(j=j):
                            if j == 0:
                                if n[0]:
                                    follow(n[0])
                                else:
                                    dve.wait_ge(row_ready, b + 1)
                                    dve.sem_inc(passed, 1)
                            last = op(j)
                            if j == TU - 1:
                                last.then_inc(topk, 1)
                                n[0] += 1
                        steps.append(one)

                def follow(count):
                    dve.wait_ge(topk, b * per + count)
                    dve.sem_inc(passed, 1)

                def single(op):
                    def one():
                        follow(n[0])
                        op().then_inc(topk, 1)
                        n[0] += 1
                    steps.append(one)

                for _r in range(drop // 8):
                    over_tiles(lambda j: v.max(best[:, j], row[:, j]))
                    over_tiles(lambda j: v.match_replace(row[:, j], best[:, j], row[:, j], MARK))
                over_tiles(lambda j: v.max(best[:, j], row[:, j]))
                single(lambda: v.memset(best[:, :, drop % 8:8], SENT))
                over_tiles(lambda j: v.match_replace(row[:, j], best[:, j], row[:, j], MARK))
                single(lambda: v.scalar_tensor_tensor(x, row[:, :, 0:E1], CUT, x, ALU.is_gt, ALU.mult))
                single(lambda: v.tensor_reduce(share[:, 0], x, X, ALU.add))
                single(lambda: v.tensor_scalar(share[:, 1], share[:, 0], 1.0 / SCL, None, ALU.mult))
                single(lambda: v.reciprocal(share[:, 2], share[:, 1]))

                def scale():
                    follow(n[0])
                    if not isinstance(b, int):
                        dve.wait_ge(cat_low, b)
                    v.tensor_tensor(cat, x, share[:, 2].unsqueeze(2).broadcast_to([HALF, TU, E1]),
                                    ALU.mult).then_inc(cat_ready, 1)

                def rest():
                    dve.wait_ge(cat_high, b + 1)
                    v.tensor_tensor(cat16[:, :, 1], cat, cat16[:, :, 0], ALU.subtract).then_inc(cat_low, 1)

                steps += [scale, rest]
                return steps

            per = 2 * (drop // 8) + 7
            dve.wait_ge(filled, 1)
            dve.wait_ge(s, 6 * NB)
            dve.wait_ge(expd, 2 * NB)
            for step in routing(0):
                step()
            dve.sem_inc(scaled, 2)
            dve.sem_inc(low, 2)

            def expert(grp, tb, e, x, y_of=None):
                it = number(grp, tb, e)
                for c in range(HC):
                    dve.wait_ge(g_ready, 2 * it + c + 1)
                    dve.wait_ge(spread, it + 1)
                    dve.wait_ge(low, 2 * it + c + 1)
                    v.tensor_tensor(two(hs[:, c]), two(g[:, c]), k.bank[:, 4:6, 0:CH], ALU.mult).then_inc(scaled, 1)
                if y_of:
                    add(*y_of)
                for c in range(HC):
                    dve.wait_ge(hi_ready, 2 * it + c + 1)
                    v.tensor_tensor(h_lo[:, x, c], hs[:, c], h_hi[:, x, c], ALU.subtract).then_inc(low, 1)

            def add(nth, tb):
                dve.wait_ge(used, (nth + 1) * GE + 2)
                v.tensor_tensor(two(k.h[:, bass.ds(tb * BLK, BLK)]), two(k.h[:, bass.ds(tb * BLK, BLK)]), k.bank[:, 6:8, 0:CH],
                                ALU.add).then_inc(y_added, 1)

            def rest(grp, tb):
                expert(grp, tb, 1, 1)
                with dve.Fori(1, GE // 2) as ee:
                    for x in range(2):
                        expert(grp, tb, 2 * ee + x, x)

            def block_and_routing(tb):
                steps = routing(tb + 1)
                for e in range(GE):
                    expert(0, tb, e, e % 2, y_of=(tb - 1, tb - 1) if e == 0 and not isinstance(tb, int) else None)
                    for step in steps[ROUTE[e]:ROUTE[e + 1]]:
                        step()

            block_and_routing(0)
            with dve.Fori(1, NB - 1) as tb:
                block_and_routing(tb)
            expert(0, NB - 1, 0, 0, y_of=(NB - 2, NB - 2))
            rest(0, NB - 1)
            for grp in range(1, NG):
                expert(grp, 0, 0, 0, y_of=(grp * NB - 1, NB - 1))
                rest(grp, 0)
                with dve.Fori(1, NB) as tb:
                    expert(grp, tb, 0, 0, y_of=(grp * NB + tb - 1, tb - 1))
                    rest(grp, tb)
            add(NG * NB - 1, NB - 1)

        @block.tensor
        def _(pe):
            t = nc.tensor
            pe.wait_ge(small_in, 80)
            with pe.Fori(0, NC // 2) as i:
                for j in range(2):
                    norm.pe_spread(pe, 2 * i + j, j)
                for j in range(2):
                    pe.wait_ge(norm.u_ready, 2 * i + j + 1)
                    pe.wait_ge(copied, 2 * i)
                    for q in range(4):
                        last = t.matmul(k.bank[0:HALF, 4 + j, q * E1:(q + 1) * E1], ut[:, j, q * HALF:(q + 1) * HALF],
                                        router[:], start=True, stop=True)
                    last.then_inc(logits, 1)

            def turn(b):
                pe.wait_ge(cat_low, b + 1)
                for n in range(TU):
                    last = t.matmul(k.bank[:, 4 + n // 4, n % 4 * HALF:(n % 4 + 1) * HALF],
                                    cat16[:, n].rearrange("p a b -> p (a b)"), ident16[:], start=True, stop=True)
                last.then_inc(turned, 1)

            pe.wait_ge(copied, NC)
            pe.wait_ge(prepared, 2)
            turn(0)

            def front(grp, tb, e, first=False, turning=None):
                it = number(grp, tb, e)
                if turning is not None:
                    pe.wait_ge(scaled, 2 * it + 2)
                    turn(turning)
                for c in range(HC):
                    if not first:
                        pe.wait_ge(g_ready, 2 * it + c - 1)
                    at = bass.ds((e * HC + c) * 128, 128)
                    w = [k.weights[:, grp % 2, m, at] for m in range(2)]
                    for m, (ww, uu) in enumerate(((w[0], u_hi), (w[0], u_lo), (w[1], u_hi))):
                        for q in range(2):
                            last = t.matmul(k.bank[:, 2 * c + q, 0:CH], ww, uu[:, bass.ds(tb * BLK + q * CH, CH)],
                                            start=(m == 0), stop=(m == 2))
                    last.then_inc(up, 1)
                if turning is not None:
                    pe.wait_ge(comb_ready, 2 * turning + 2)
                elif first:
                    pe.wait_ge(comb_ready, 2)
                else:
                    pe.wait_ge(scaled, 2 * it + 2)
                for q in range(2):
                    last = t.matmul(k.bank[:, 4 + q, 0:CH], k.sel[:, bass.ds(grp * GE + e, 1), :].rearrange("p a b -> p (a b)"),
                                    comb[:, bass.ds(tb * BLK + q * CH, CH)], start=True, stop=True)
                last.then_inc(spread, 1)

            def back(grp, tb, e, x, start=False, stop=False):
                it = number(grp, tb, e)
                for c in range(HC):
                    at = bass.ds((e * HC + c) * 128, 128)
                    w = [k.weights[:, grp % 2, 2 + m, at] for m in range(2)]
                    pe.wait_ge(hi_ready, 2 * it + c + 1)
                    for m, (ww, hh) in enumerate(((w[0], h_hi), (w[1], h_hi), (w[0], h_lo))):
                        if m == 2:
                            pe.wait_ge(low, 2 * it + c + 3)
                        for q in range(2):
                            last = t.matmul(k.bank[:, 6 + q, 0:CH], ww, hh[:, x, c, q * CH:(q + 1) * CH],
                                            start=(start and c == 0 and m == 0), stop=(stop and c == HC - 1 and m == 2))
                    if c == 0:
                        continue
                    last.then_inc(used, 1)

            def bias(tb):
                for q in range(2):
                    t.matmul(k.bank[:, 6 + q, 0:CH], b2[:], comb32[:, q * CH:(q + 1) * CH], start=True, stop=False)

            def block_and_routing(tb, first=False):
                front(0, tb, 1)
                if not first:
                    pe.wait_ge(y_added, tb)
                bias(tb)
                back(0, tb, 0, 0)
                for e in range(1, GE - 1):
                    front(0, tb, e + 1, turning=tb + 1 if e + 1 == TURN_AT else None)
                    back(0, tb, e, e % 2)
                front(0, tb + 1, 0)
                back(0, tb, GE - 1, 1, stop=True)

            def block_of_tokens(grp, tb, after):
                front(grp, tb, 1)
                pe.wait_ge(y_added, grp * NB + tb)
                if grp == 0:
                    bias(tb)
                back(grp, tb, 0, 0, start=(grp > 0))
                with pe.Fori(0, GE // 2 - 1) as ee:
                    for x in (1, 2):
                        front(grp, tb, 2 * ee + x + 1)
                        back(grp, tb, 2 * ee + x, x % 2)
                if after:
                    front(*after, 0)
                back(grp, tb, GE - 1, 1, stop=True)

            pe.wait_ge(k.group_split, 2 * PIECES)
            front(0, 0, 0, first=True)
            block_and_routing(0, first=True)
            with pe.Fori(1, NB - 1) as tb:
                block_and_routing(tb)
            for grp in range(NG):
                if grp:
                    with pe.Fori(0, NB - 1) as tb:
                        block_of_tokens(grp, tb, (grp, tb + 1))
                if grp + 1 < NG:
                    pe.wait_ge(k.group_split, 2 * PIECES * (grp + 2))
                    block_of_tokens(grp, NB - 1, (grp + 1, 0))
                else:
                    block_of_tokens(grp, NB - 1, None)


def store(nc, k, out):
    with ExitStack() as ctx:
        stored = k.semaphore("result_stored")
        block = ctx.enter_context(nc.Block())

        @block.sync
        def _(sp):
            for p in range(4):
                cols = slice(p * T // 4, (p + 1) * T // 4)
                sp.dma_start(out[:, cols], k.h[:, cols]).then_inc(stored, 16)
            sp.wait_ge(stored, 64)


def audio_tower(nc, a, out):
    k = Kernel()
    k.a = a
    with ExitStack() as ctx:
        def sb(name, shape, dt=F32):
            return ctx.enter_context(nc.sbuf_tensor(name, shape, dt))

        k.semaphore = lambda name: ctx.enter_context(nc.semaphore(name))
        k.bank = ctx.enter_context(nc.psum_tensor("bank", [128, 8, 512], F32))
        k.h = sb("h", [128, T])
        k.hc = sb("hc", [128, T])
        k.rstd = sb("rstd", [128, NT])
        k.ident = sb("ident", [128, 128])
        k.mean_w = sb("mean_w", [128, 128])
        k.ones = sb("ones", [128, 128])
        k.cells = sb("cells", [1, 8])
        k.hm = sb("hm", [128, NH])
        k.sel = sb("sel", [128, E1, 128], F16)
        k.weights = sb("weights", [128, 2, 4, GE * HC * 128], BF16)
        k.w0_split = k.semaphore("w0_split")
        k.w2_in = k.semaphore("w0_down_in")
        k.group_split = k.semaphore("expert_group_split")
        with ExitStack() as inner:
            tables = RecurrenceTables(nc, k, inner)
            constants_and_tokens(nc, k, a["x"], a["w_tok"], a["bias"], tables)
            norm_statistics(nc, k, "n1", 3)
            recurrence(nc, k, tables)
        norm_statistics(nc, k, "n2", 4)
        first_mixture(nc, k)
        norm_statistics(nc, k, "n3", 5)
        sparse_attention(nc, k)
        norm_statistics(nc, k, "n4", 6)
        second_mixture(nc, k)
        store(nc, k, out)


def kernel(**i):
    import numpy as np
    import concourse.bacc as bacc
    from concourse.bass_utils import run_bass_kernel_spmd

    def two(v):
        return v.reshape(2, 128).T

    lay = {
        "x": i["x"][:, :3 * L].reshape(B * L, 2, KT).transpose(2, 1, 0),
        "w_tok": i["L0_tok_weight"].T.reshape(2, KT, D).transpose(1, 0, 2),
        "bias": i["L0_tok_bias"].reshape(D, 1),
        "theta": two(i["L0_attn_theta_log"]),
        "nu": two(i["L0_attn_nu_log"]),
        "gamma": two(i["L0_attn_gamma_log"]),
        "b_re": i["L0_attn_B_re"].T,
        "b_im": i["L0_attn_B_im"].T,
        "c_re": i["L0_attn_C_re"].T.reshape(2, 128, D).transpose(1, 0, 2),
        "c_im": i["L0_attn_C_im"].T.reshape(2, 128, D).transpose(1, 0, 2),
        "d": i["L0_attn_D"].T,
        "gate": i["L0_ffn_gate_weight"].T,
        "w1": i["L0_ffn_w1"].transpose(2, 0, 1).reshape(D, E0 * FF0),
        "w2": i["L0_ffn_w2"].reshape(E0, D, FC, 128).transpose(3, 0, 2, 1),
        "wq": i["L1_attn_Wq"], "wk": i["L1_attn_Wk"], "wv": i["L1_attn_Wv"], "wo": i["L1_attn_Wo"],
        "idx": i["L1_attn_idx_sample"].reshape(1, NS),
        "e_w1": i["L1_ffn_w1"][::-1].transpose(1, 0, 2).reshape(D, E1 * FF1),
        "e_b1": i["L1_ffn_b1"][::-1].reshape(E1, HC, 128).transpose(2, 0, 1),
        "e_w2": i["L1_ffn_w2"][::-1].reshape(E1, HC, 128, D).transpose(2, 0, 1, 3).reshape(128, E1 * HC * D),
        "e_b2": i["L1_ffn_b2"][::-1],
        "router": i["L1_ffn_router_w"][:, ::-1],
        "router_b": i["L1_ffn_router_b"][::-1].reshape(1, E1),
    }
    nc = bacc.Bacc("TRN2", target_bir_lowering=False, num_devices=1)
    arrays, args = {}, {}
    for name, v in lay.items():
        arrays[f"{name}_dram"] = v = np.ascontiguousarray(v)
        args[name] = nc.dram_tensor(f"{name}_dram", v.shape, mybir.dt.from_np(v.dtype), kind="ExternalInput").ap()
    out = nc.dram_tensor("out_dram", (D, T), F32, kind="ExternalOutput").ap()
    audio_tower(nc, args, out)
    r = run_bass_kernel_spmd(nc, [arrays], core_ids=[0])
    return r.results[0]["out_dram"].reshape(D, B, L).transpose(1, 2, 0)
```
